# Optimizing a Trainium2 kernel written in Bass

```python
import numpy as np
import jax
import jax.numpy as jnp

def _softmax(x, axis=-1):
    return jax.nn.softmax(x, axis=axis)

def _gelu(x):
    return jax.nn.gelu(x, approximate=True)

def _silu(x):
    return jax.nn.silu(x)

def _sigmoid(x):
    return jax.nn.sigmoid(x)

def _layernorm(x, axis=-1, eps=1e-05):
    m = jnp.mean(x, axis=axis, keepdims=True)
    v = jnp.var(x, axis=axis, keepdims=True)
    return (x - m) / jnp.sqrt(v + eps)

def _scatter_add(tgt, idx, src, axis=0):
    return tgt.at[idx].add(src)

def _segment_sum(src, seg, n):
    return jax.ops.segment_sum(src, seg, n)
kernel_name = 'mk_flamingo_gated_d2_seqx_r8_e03451'

def setup_inputs(seed: int=0):
    np.random.seed(seed)
    _w = jnp.asarray

    def _rec_inputs():
        import jax
        import jax.numpy as jnp
        _rk = jax.random.key(seed)
        x = -0.0002928 + 1 * jax.random.normal(jax.random.fold_in(_rk, 1), (32, 128, 128), jnp.float32)
        _lenS = 128 - jax.random.randint(jax.random.fold_in(_rk, 7), (32,), 0, max(1, 128 // 4) + 1, jnp.int32)
        _lenS2 = 77 - jax.random.randint(jax.random.fold_in(_rk, 8), (32,), 0, max(1, 77 // 4) + 1, jnp.int32)
        _ctx_1024P = jax.random.normal(jax.random.fold_in(_rk, 11), (32, 16, 128), jnp.float32)
        _ctx_1024c = jax.random.dirichlet(jax.random.fold_in(_rk, 511), 0.3 * jnp.ones((16,), jnp.float32), (32, 77))
        _ctx_1024t = jnp.einsum('bsk,bkd->bsd', _ctx_1024c, _ctx_1024P)
        _ctx_1024t = _ctx_1024t * jax.lax.rsqrt(jnp.mean(jnp.square(_ctx_1024t)) + 1e-12) * 0.953939
        ctx_1024 = -1.39393e-06 + 0.999914 * (_ctx_1024t + 0.3 * jax.random.normal(jax.random.fold_in(_rk, 611), (32, 77, 128), jnp.float32))
        _g = jax.random.normal(jax.random.fold_in(_rk, 9001), (2, 2), jnp.float32)
        _g = jnp.sign(_g) * jnp.maximum(jnp.abs(_g), 1.0) + (_g == 0) * 1.0
        g_xattn = _g[0]
        g_ffn = _g[1]
        return (x, ctx_1024, g_xattn, g_ffn)
    x, ctx_1024, g_xattn, g_ffn = _rec_inputs()

    def _L0_xattn_setup():
        import jax, jax.numpy as jnp
        import numpy as np
        NUM_HEADS = 16

        def _rope_tables(seq_len, head_dim, dtype):
            inv_freq = 1.0 / 10000.0 ** (jnp.arange(0, head_dim, 2, dtype=jnp.float32) / head_dim)
            freqs = jnp.arange(seq_len, dtype=jnp.float32)[:, None] * inv_freq[None, :]
            emb = jnp.concatenate([freqs, freqs], axis=-1)
            return (jnp.cos(emb).astype(dtype), jnp.sin(emb).astype(dtype))

        def _rotate_half(t):
            d = t.shape[-1] // 2
            return jnp.concatenate([-t[..., d:], t[..., :d]], axis=-1)

        def _apply_rope(t):
            cos, sin = _rope_tables(t.shape[2], t.shape[3], t.dtype)
            return t * cos[None, None] + _rotate_half(t) * sin[None, None]

        def _forward(x, context, Wq, Wkv, Wo, bo):
            B, Nq, C = x.shape
            Nkv = context.shape[1]
            H = NUM_HEADS
            hd = C // H
            scale = hd ** (-0.5)
            q = (x @ Wq).reshape(B, Nq, H, hd).transpose(0, 2, 1, 3)
            kv = (context @ Wkv).reshape(B, Nkv, 2, H, hd).transpose(2, 0, 3, 1, 4)
            k, v = (kv[0], kv[1])
            q = _apply_rope(q)
            k = _apply_rope(k)
            attn = jnp.einsum('bhqd,bhkd->bhqk', q, k) * scale
            attn = jax.nn.softmax(attn, axis=-1)
            out = jnp.einsum('bhqk,bhkd->bhqd', attn, v)
            out = out.transpose(0, 2, 1, 3).reshape(B, Nq, C)
            return out @ Wo + bo
        key = jax.random.key(seed)
        ks = jax.random.split(key, 6)
        B, N, C = (2, 256, 128)
        s = C ** (-0.5)
        return {'x': jax.random.normal(ks[0], (B, N, C), dtype=jnp.float32), 'context': jax.random.normal(ks[1], (B, N, C), dtype=jnp.float32), 'Wq': jax.random.normal(ks[2], (C, C), dtype=jnp.float32) * s, 'Wkv': jax.random.normal(ks[3], (C, 2 * C), dtype=jnp.float32) * s, 'Wo': jax.random.normal(ks[4], (C, C), dtype=jnp.float32) * s, 'bo': jnp.zeros((C,), dtype=jnp.float32)}
    _L0_xattn_all = _L0_xattn_setup()
    _L0_xattn_in = {k: v for k, v in _L0_xattn_all.items() if k in ('Wq', 'Wkv', 'Wo', 'bo')}
    del _L0_xattn_all

    def _L0_ffn_setup():
        import jax, jax.numpy as jnp
        import numpy as np
        B, S, D, H, M, E, K = (8, 256, 128, 256, 64, 8, 2)
        EH = H // 2

        def _layernorm(x, g, b, eps=1e-05):
            mu = jnp.mean(x, axis=-1, keepdims=True)
            var = jnp.var(x, axis=-1, keepdims=True)
            return (x - mu) * jax.lax.rsqrt(var + eps) * g + b
        key = jax.random.key(seed)
        ks = jax.random.split(key, 16)
        sc = lambda *shape: 1.0 / np.sqrt(shape[0])
        return {'inputs_embeds': jax.random.normal(ks[0], (B, S, D), jnp.float32), 'W_enc': jax.random.normal(ks[1], (D, H), jnp.float32) * sc(D), 'b_enc': jnp.zeros((H,), jnp.float32), 'W_s2c': jax.random.normal(ks[2], (H, M), jnp.float32) * sc(H), 'b_s2c': jnp.zeros((M,), jnp.float32), 'Wr': jax.random.normal(ks[3], (M, E), jnp.float32) * sc(M), 'br': jnp.zeros((E,), jnp.float32), 'W1': jax.random.normal(ks[4], (E, M, EH), jnp.float32) * sc(M), 'b1': jnp.zeros((E, EH), jnp.float32), 'W2': jax.random.normal(ks[5], (E, EH, M), jnp.float32) * sc(EH), 'b2': jnp.zeros((E, M), jnp.float32), 'W_c2s': jax.random.normal(ks[6], (M, H), jnp.float32) * sc(M), 'b_c2s': jnp.zeros((H,), jnp.float32), 'W_dec': jax.random.normal(ks[7], (H, D), jnp.float32) * sc(H), 'b_dec': jnp.zeros((D,), jnp.float32), 'ln_g': jnp.ones((D,), jnp.float32), 'ln_b': jnp.zeros((D,), jnp.float32)}
    _L0_ffn_all = _L0_ffn_setup()
    _L0_ffn_in = {k: v for k, v in _L0_ffn_all.items() if k in ('W_enc', 'b_enc', 'W_s2c', 'b_s2c', 'Wr', 'br', 'W1', 'b1', 'W2', 'b2', 'W_c2s', 'b_c2s', 'W_dec', 'b_dec', 'ln_g', 'ln_b')}
    del _L0_ffn_all

    def _L1_xattn_setup():
        import jax, jax.numpy as jnp
        import numpy as np
        import math
        B, SQ, SK, D = (4, 256, 256, 128)
        key = jax.random.key(seed)
        ks = jax.random.split(key, 9)
        s = 1.0 / math.sqrt(D)
        return {'q': jax.random.normal(ks[0], (B, SQ, D), jnp.float32), 'k': jax.random.normal(ks[1], (B, SK, D), jnp.float32), 'v': jax.random.normal(ks[2], (B, SK, D), jnp.float32), 'Wq': jax.random.normal(ks[3], (D, D), jnp.float32) * s, 'bq': jax.random.normal(ks[4], (D,), jnp.float32) * s, 'Wk': jax.random.normal(ks[5], (D, D), jnp.float32) * s, 'bk': jax.random.normal(ks[6], (D,), jnp.float32) * s, 'Wv': jax.random.normal(ks[7], (D, D), jnp.float32) * s, 'bv': jax.random.normal(ks[8], (D,), jnp.float32) * s}
    _L1_xattn_all = _L1_xattn_setup()
    _L1_xattn_in = {k: v for k, v in _L1_xattn_all.items() if k in ('Wq', 'bq', 'Wk', 'bk', 'Wv', 'bv')}
    del _L1_xattn_all

    def _L1_ffn_setup():
        import jax, jax.numpy as jnp
        import numpy as np
        E, K = (8, 4)
        B, S, D = (4, 128, 128)
        H = D * 2 * 4 // 3

        def _swiglu(u, w1, w2, w3):
            h = jnp.einsum('...d,hd->...h', u, w1)
            v = jnp.einsum('...d,hd->...h', u, w2)
            return jnp.einsum('...h,dh->...d', jax.nn.sigmoid(h) * h * v, w3)
        key = jax.random.key(seed)
        ks = jax.random.split(key, 9)
        std = 0.02
        return {'x': jax.random.normal(ks[0], (B, S, D), jnp.float32), 'Wg': jax.random.normal(ks[1], (E, D), jnp.float32) * std, 'routing_bias': jnp.zeros((E,), jnp.float32), 'W1': jax.random.normal(ks[2], (E, H, D), jnp.float32) * std, 'W2': jax.random.normal(ks[3], (E, H, D), jnp.float32) * std, 'W3': jax.random.normal(ks[4], (E, D, H), jnp.float32) * std, 'Ws1': jax.random.normal(ks[5], (H, D), jnp.float32) * std, 'Ws2': jax.random.normal(ks[6], (H, D), jnp.float32) * std, 'Ws3': jax.random.normal(ks[7], (D, H), jnp.float32) * std}
    _L1_ffn_all = _L1_ffn_setup()
    _L1_ffn_in = {k: v for k, v in _L1_ffn_all.items() if k in ('Wg', 'routing_bias', 'W1', 'W2', 'W3', 'Ws1', 'Ws2', 'Ws3')}
    del _L1_ffn_all
    return {'x': x, 'ctx_1024': ctx_1024, 'g_xattn': g_xattn, 'g_ffn': g_ffn, 'L0_xattn_Wq': _L0_xattn_in['Wq'], 'L0_xattn_Wkv': _L0_xattn_in['Wkv'], 'L0_xattn_Wo': _L0_xattn_in['Wo'], 'L0_xattn_bo': _L0_xattn_in['bo'], 'L0_ffn_W_enc': _L0_ffn_in['W_enc'], 'L0_ffn_b_enc': _L0_ffn_in['b_enc'], 'L0_ffn_W_s2c': _L0_ffn_in['W_s2c'], 'L0_ffn_b_s2c': _L0_ffn_in['b_s2c'], 'L0_ffn_Wr': _L0_ffn_in['Wr'], 'L0_ffn_br': _L0_ffn_in['br'], 'L0_ffn_W1': _L0_ffn_in['W1'], 'L0_ffn_b1': _L0_ffn_in['b1'], 'L0_ffn_W2': _L0_ffn_in['W2'], 'L0_ffn_b2': _L0_ffn_in['b2'], 'L0_ffn_W_c2s': _L0_ffn_in['W_c2s'], 'L0_ffn_b_c2s': _L0_ffn_in['b_c2s'], 'L0_ffn_W_dec': _L0_ffn_in['W_dec'], 'L0_ffn_b_dec': _L0_ffn_in['b_dec'], 'L0_ffn_ln_g': _L0_ffn_in['ln_g'], 'L0_ffn_ln_b': _L0_ffn_in['ln_b'], 'L1_xattn_Wq': _L1_xattn_in['Wq'], 'L1_xattn_bq': _L1_xattn_in['bq'], 'L1_xattn_Wk': _L1_xattn_in['Wk'], 'L1_xattn_bk': _L1_xattn_in['bk'], 'L1_xattn_Wv': _L1_xattn_in['Wv'], 'L1_xattn_bv': _L1_xattn_in['bv'], 'L1_ffn_Wg': _L1_ffn_in['Wg'], 'L1_ffn_routing_bias': _L1_ffn_in['routing_bias'], 'L1_ffn_W1': _L1_ffn_in['W1'], 'L1_ffn_W2': _L1_ffn_in['W2'], 'L1_ffn_W3': _L1_ffn_in['W3'], 'L1_ffn_Ws1': _L1_ffn_in['Ws1'], 'L1_ffn_Ws2': _L1_ffn_in['Ws2'], 'L1_ffn_Ws3': _L1_ffn_in['Ws3']}

def reference(x, ctx_1024, g_xattn, g_ffn, L0_xattn_Wq, L0_xattn_Wkv, L0_xattn_Wo, L0_xattn_bo, L0_ffn_W_enc, L0_ffn_b_enc, L0_ffn_W_s2c, L0_ffn_b_s2c, L0_ffn_Wr, L0_ffn_br, L0_ffn_W1, L0_ffn_b1, L0_ffn_W2, L0_ffn_b2, L0_ffn_W_c2s, L0_ffn_b_c2s, L0_ffn_W_dec, L0_ffn_b_dec, L0_ffn_ln_g, L0_ffn_ln_b, L1_xattn_Wq, L1_xattn_bq, L1_xattn_Wk, L1_xattn_bk, L1_xattn_Wv, L1_xattn_bv, L1_ffn_Wg, L1_ffn_routing_bias, L1_ffn_W1, L1_ffn_W2, L1_ffn_W3, L1_ffn_Ws1, L1_ffn_Ws2, L1_ffn_Ws3):
    import jax
    import jax.numpy as jnp

    def _L0_xattn_ref(x, context, Wq, Wkv, Wo, bo):
        import jax, jax.numpy as jnp
        import numpy as np
        NUM_HEADS = 16

        def _rope_tables(seq_len, head_dim, dtype):
            inv_freq = 1.0 / 10000.0 ** (jnp.arange(0, head_dim, 2, dtype=jnp.float32) / head_dim)
            freqs = jnp.arange(seq_len, dtype=jnp.float32)[:, None] * inv_freq[None, :]
            emb = jnp.concatenate([freqs, freqs], axis=-1)
            return (jnp.cos(emb).astype(dtype), jnp.sin(emb).astype(dtype))

        def _rotate_half(t):
            d = t.shape[-1] // 2
            return jnp.concatenate([-t[..., d:], t[..., :d]], axis=-1)

        def _apply_rope(t):
            cos, sin = _rope_tables(t.shape[2], t.shape[3], t.dtype)
            return t * cos[None, None] + _rotate_half(t) * sin[None, None]

        def _forward(x, context, Wq, Wkv, Wo, bo):
            B, Nq, C = x.shape
            Nkv = context.shape[1]
            H = NUM_HEADS
            hd = C // H
            scale = hd ** (-0.5)
            q = (x @ Wq).reshape(B, Nq, H, hd).transpose(0, 2, 1, 3)
            kv = (context @ Wkv).reshape(B, Nkv, 2, H, hd).transpose(2, 0, 3, 1, 4)
            k, v = (kv[0], kv[1])
            q = _apply_rope(q)
            k = _apply_rope(k)
            attn = jnp.einsum('bhqd,bhkd->bhqk', q, k) * scale
            attn = jax.nn.softmax(attn, axis=-1)
            out = jnp.einsum('bhqk,bhkd->bhqd', attn, v)
            out = out.transpose(0, 2, 1, 3).reshape(B, Nq, C)
            return out @ Wo + bo
        return _forward(x, context, Wq, Wkv, Wo, bo)

    def _L0_ffn_ref(inputs_embeds, W_enc, b_enc, W_s2c, b_s2c, Wr, br, W1, b1, W2, b2, W_c2s, b_c2s, W_dec, b_dec, ln_g, ln_b):
        import jax, jax.numpy as jnp
        import numpy as np
        B, S, D, H, M, E, K = (8, 256, 128, 256, 64, 8, 2)
        EH = H // 2

        def _layernorm(x, g, b, eps=1e-05):
            mu = jnp.mean(x, axis=-1, keepdims=True)
            var = jnp.var(x, axis=-1, keepdims=True)
            return (x - mu) * jax.lax.rsqrt(var + eps) * g + b
        b, s, d = inputs_embeds.shape
        spikes_enc = jax.nn.sigmoid(inputs_embeds @ W_enc + b_enc)
        flat = spikes_enc.reshape(b * s, -1)
        cont = flat @ W_s2c + b_s2c
        probs = jax.nn.softmax(cont @ Wr + br, axis=-1)
        topk_w, topk_idx = jax.lax.top_k(probs, K)
        topk_w = topk_w / jnp.sum(topk_w, axis=-1, keepdims=True)
        gate = jnp.sum(jax.nn.one_hot(topk_idx, E, dtype=cont.dtype) * topk_w[..., None], axis=1)
        h = jax.nn.relu(jnp.einsum('tm,emh->eth', cont, W1) + b1[:, None, :])
        y = jnp.einsum('eth,ehm->etm', h, W2) + b2[:, None, :]
        expert_out = jnp.einsum('etm,te->tm', y, gate)
        spikes_moe = jax.nn.sigmoid(expert_out @ W_c2s + b_c2s)
        spikes_moe = spikes_moe.reshape(b, s, -1)
        decoded = spikes_moe @ W_dec + b_dec
        return _layernorm(decoded, ln_g, ln_b)

    def _L1_xattn_ref(q, k, v, Wq, bq, Wk, bk, Wv, bv):
        import jax, jax.numpy as jnp
        import numpy as np
        import math
        B, SQ, SK, D = (4, 256, 256, 128)
        qp = jnp.einsum('bsd,ed->bse', q, Wq) + bq
        kp = jnp.einsum('bsd,ed->bse', k, Wk) + bk
        vp = jnp.einsum('bsd,ed->bse', v, Wv) + bv
        scale = 1.0 / jnp.sqrt(jnp.asarray(kp.shape[-1], qp.dtype))
        scores = jnp.einsum('bqd,bkd->bqk', qp, kp) * scale
        attn = jax.nn.softmax(scores, axis=-1)
        return jnp.einsum('bqk,bkd->bqd', attn, vp)

    def _L1_ffn_ref(x, Wg, routing_bias, W1, W2, W3, Ws1, Ws2, Ws3):
        import jax, jax.numpy as jnp
        import numpy as np
        E, K = (8, 4)
        B, S, D = (4, 128, 128)
        H = D * 2 * 4 // 3

        def _swiglu(u, w1, w2, w3):
            h = jnp.einsum('...d,hd->...h', u, w1)
            v = jnp.einsum('...d,hd->...h', u, w2)
            return jnp.einsum('...h,dh->...d', jax.nn.sigmoid(h) * h * v, w3)
        gate = jnp.einsum('bsd,ed->bse', x, Wg) + routing_bias
        _, top_idx = jax.lax.top_k(gate, K)
        mask = jax.nn.one_hot(top_idx, E, dtype=gate.dtype).sum(-2)
        masked_gate = jnp.where(mask > 0, gate, -jnp.inf)
        probs = jax.nn.softmax(masked_gate, axis=-1)
        weights = probs * mask
        out = _swiglu(x, Ws1, Ws2, Ws3)
        h1 = jnp.einsum('bsd,ehd->ebsh', x, W1)
        h2 = jnp.einsum('bsd,ehd->ebsh', x, W2)
        eo = jnp.einsum('ebsh,edh->ebsd', jax.nn.sigmoid(h1) * h1 * h2, W3)
        out = out + jnp.einsum('ebsd,bse->bsd', eo, weights)
        return out
    x = x + jnp.tanh(g_xattn[0]) * _L0_xattn_ref(_layernorm(x, axis=-1), ctx_1024, L0_xattn_Wq, L0_xattn_Wkv, L0_xattn_Wo, L0_xattn_bo)
    x = x + jnp.tanh(g_ffn[0]) * _L0_ffn_ref(_layernorm(x, axis=-1), L0_ffn_W_enc, L0_ffn_b_enc, L0_ffn_W_s2c, L0_ffn_b_s2c, L0_ffn_Wr, L0_ffn_br, L0_ffn_W1, L0_ffn_b1, L0_ffn_W2, L0_ffn_b2, L0_ffn_W_c2s, L0_ffn_b_c2s, L0_ffn_W_dec, L0_ffn_b_dec, L0_ffn_ln_g, L0_ffn_ln_b)
    x = x + jnp.tanh(g_xattn[1]) * _L1_xattn_ref(_layernorm(x, axis=-1), ctx_1024, ctx_1024, L1_xattn_Wq, L1_xattn_bq, L1_xattn_Wk, L1_xattn_bk, L1_xattn_Wv, L1_xattn_bv)
    x = x + jnp.tanh(g_ffn[1]) * _L1_ffn_ref(_layernorm(x, axis=-1), L1_ffn_Wg, L1_ffn_routing_bias, L1_ffn_W1, L1_ffn_W2, L1_ffn_W3, L1_ffn_Ws1, L1_ffn_Ws2, L1_ffn_Ws3)
    return x

_drawn_inputs = setup_inputs


def setup_inputs(seed=0):
    import zlib

    import numpy as np

    out = dict(_drawn_inputs(seed))
    spreads = {'g_ffn': (-1.0, 0.6),
     'L0_xattn_bo': (0.0, 0.1),
     'L0_ffn_b_enc': (0.0, 0.726),
     'L0_ffn_b_s2c': (0.0, 0.1),
     'L0_ffn_br': (0.0, 0.1),
     'L0_ffn_b1': (0.0, 0.668),
     'L0_ffn_b2': (0.0, 0.511),
     'L0_ffn_b_c2s': (0.0, 0.273),
     'L0_ffn_b_dec': (0.0, 0.1),
     'L0_ffn_ln_g': (1.0, 0.2),
     'L0_ffn_ln_b': (0.0, 0.1),
     'L1_ffn_routing_bias': (0.0, 0.8)}
    factors = {'L1_xattn_bq': 4.077,
     'L1_xattn_bk': 8.0,
     'L1_ffn_Wg': 8.0,
     'L1_ffn_W1': 8.0,
     'L1_ffn_W2': 8.0,
     'L1_ffn_W3': 8.0,
     'L1_ffn_Ws1': 8.0,
     'L1_ffn_Ws2': 8.0,
     'L1_ffn_Ws3': 8.0}
    for name, (base, spread) in spreads.items():
        noise = np.random.default_rng([zlib.crc32(name.encode()), seed]).standard_normal(out[name].shape)
        drawn = base * np.exp(spread * noise) if base else spread * noise
        out[name] = jnp.asarray(drawn.astype(out[name].dtype))
    for name, factor in factors.items():
        out[name] = (out[name] * factor).astype(out[name].dtype)
    return out
```

```python
from contextlib import ExitStack

import numpy as np

import concourse.bass as bass
from concourse import mybir

B, T, S, D = 32, 128, 77, 128
NB = 4
G = B // NB
GT = NB * T
GS = NB * S
HEADS = 16
HD = D // HEADS
QUADS = HEADS // NB
NQ = 4
UNITS = NB * QUADS
VP = 3 * (HD + 1)
E0, M0, EH0, H0 = 8, 64, 128, 256
E1, K1, H1 = 8, 4, D * 2 * 4 // 3
K0 = 2
CH = -(-(E1 + 1) * H1 // 128)
W1C = CH * 128
WPREP = W1C * 3 // G
EPS = 1e-5
RSQRT_MAGIC = 0x5F3759DF
NEWTON = 3

ALU = mybir.AluOpType
ACT = mybir.ActivationFunctionType
AX = mybir.AxisListType
F32 = mybir.dt.float32
F32R = mybir.dt.float32r
BF16 = mybir.dt.bfloat16
F16 = mybir.dt.float16
I32 = mybir.dt.int32

WA = {n: i * 128 for i, n in enumerate(("q", "qp", "k", "kp", "v", "o"))}
CC, _at = {}, 0
for _n, _w in (("ident", 128), ("cosq", T), ("sinq", T), ("cosk", S), ("sink", S), ("mask", NQ), ("qmask", QUADS), ("tri", 64)):
    CC[_n] = (_at, _at + _w)
    _at += _w
NC_COLS = _at
WS, _at = {}, 0
for _n, _w in (("enc", H0), ("w1", E0 * EH0), ("w2", E0 * 2 * M0), ("c2s", H0), ("b2", 2 * M0)):
    WS[_n] = (_at, _at + _w)
    _at += _w
NS_COLS = _at
WF, _at = {}, 0
for _n, _w in (("s2c", 2 * 2 * M0), ("wr", E0), ("dec", 2 * D), ("b_enc", 2), ("b_s2c", 1), ("b1", E0),
               ("b_c2s", 2), ("br", E0), ("b_dec", D), ("ln_g", D), ("ln_b", D)):
    WF[_n] = (_at, _at + _w)
    _at += _w
NF_COLS = _at
WL, _at = {}, 0
for _n, _w in (("q", D), ("k", D), ("v", D), ("bq", 1), ("bk", 1), ("bv", D), ("wg", E1), ("rb", E1)):
    WL[_n] = (_at, _at + _w)
    _at += _w
NL_COLS = _at


class Signal:

    def __init__(self, sem, per):
        self.sem, self.per = sem, per

    def upto(self, g, k=None, back=0):
        return g * self.per + ((self.per if k is None else k) - back * self.per)

    def comes(self, g, k=None, back=0):
        return not isinstance(g, int) or self.upto(g, k, back) > 0


def build(nc, x_d, ctxt_d, gates_d, wa_d, bo_d, const_d, ws_d, wf_d, wl_d, sel0_d, sel1_d, w123_d, out_d):
    ctx = ExitStack()
    with ctx:
        def sb(name, shape, dt=F32):
            return ctx.enter_context(nc.sbuf_tensor(name, shape, dt))

        def signal(name, per):
            return Signal(ctx.enter_context(nc.semaphore(name)), per)

        x = sb("x", [T, B, D])
        ctxt = sb("ctxt", [D, GS])
        const = sb("const", [128, NC_COLS])
        tg = sb("tg", [128, 4])
        g_raw = sb("g_raw", [128, 4])
        stats = sb("stats", [128, NB, 6])
        mv = sb("mv", [128, NB, 2])
        work = sb("work", [128, 3, NB])
        xn = sb("xn", [128, NB, D])
        xh = sb("xh", [D, GT], F32R)
        xl = sb("xl", [D, GT], F32R)

        def cc(name):
            a, b = CC[name]
            return const[:, a:b]

        ident = cc("ident")

        x_in = signal("x_in", 16)
        layer0_attention(nc, x, ctxt, const, cc, ident, tg, g_raw, stats, mv, work, xn, xh, xl,
                         x_d, ctxt_d, gates_d, wa_d, bo_d, const_d, x_in, signal)
        layer0_ffn(nc, x, cc, ident, tg, stats, mv, work, xn, xh, xl, ws_d, wf_d, sel0_d, signal)
        with ExitStack() as keep:
            def kept(name, shape):
                return keep.enter_context(nc.sbuf_tensor(name, shape, F32R))

            xh1 = kept("xh1", [D, B * T])
            xl1 = kept("xl1", [D, B * T])
            gt1 = kept("gt1", [128, B * T])
            wh = kept("wh", [128, 3 * W1C])
            wlo = kept("wlo", [128, 3 * W1C])
            layer1_attention(nc, x, ctxt, cc, ident, tg, stats, mv, work, xn, xh, xl, xh1, xl1, gt1, wh, wlo,
                             wl_d, w123_d, ctxt_d, signal)
            layer1_ffn(nc, x, ident, tg, xh1, xl1, gt1, wh, wlo, sel1_d, out_d, signal)


class Norm:

    def __init__(self, signal, name, tile, stats, mv, work, xn, ident, turns=True):
        self.tile, self.stats, self.mv, self.work, self.xn, self.ident = tile, stats, mv, work, xn, ident
        self.bn = signal(f"{name}_bn", NB + 1)
        self.moments = signal(f"{name}_moments", NB)
        self.newton = signal(f"{name}_newton", 3 + 3 * NEWTON)
        self.rows = signal(f"{name}_rows", NB)
        self.turned = signal(f"{name}_turned", 1)
        self.high = signal(f"{name}_high", 1)
        self.low = signal(f"{name}_low", 1)
        self.turns = turns

    def vector_stats(self, nc, dve, g):
        for t in range(NB):
            nc.vector.bn_stats(self.stats[:, t, :], self.tile(g, t)).then_inc(self.bn.sem, 1)
        dve.wait_ge(self.bn.sem, self.bn.upto(g, NB))
        dve.sem_inc(self.bn.sem, 1)
        for t in range(NB):
            nc.vector.bn_aggr(self.mv[:, t, :], self.stats[:, t, :]).then_inc(self.moments.sem, 1)

    def vector_guess(self, nc, dve, g):
        v, half, y = self.work[:, 0, :], self.work[:, 1, :], self.work[:, 2, :]
        dve.wait_ge(self.moments.sem, self.moments.upto(g))
        nc.vector.tensor_scalar(v, self.mv[:, :, 1], EPS, None, ALU.add).then_inc(self.newton.sem, 1)
        dve.wait_ge(self.newton.sem, self.newton.upto(g, 1))
        nc.vector.tensor_scalar(half.bitcast(I32), v.bitcast(I32), 1, None, ALU.logical_shift_right)\
            .then_inc(self.newton.sem, 1)
        dve.wait_ge(self.newton.sem, self.newton.upto(g, 2))
        nc.vector.tensor_scalar(y.bitcast(I32), half.bitcast(I32), -1, RSQRT_MAGIC, ALU.mult, ALU.add)\
            .then_inc(self.newton.sem, 1)

    def vector_newton(self, nc, dve, g, i):
        v, a, y = self.work[:, 0, :], self.work[:, 1, :], self.work[:, 2, :]
        dve.wait_ge(self.newton.sem, self.newton.upto(g, 3 + 3 * i))
        nc.vector.tensor_tensor(a, y, y, ALU.mult).then_inc(self.newton.sem, 1)
        dve.wait_ge(self.newton.sem, self.newton.upto(g, 4 + 3 * i))
        nc.vector.scalar_tensor_tensor(out=a, in0=a, scalar=-0.5, in1=v, op0=ALU.mult, op1=ALU.mult)\
            .then_inc(self.newton.sem, 1)
        dve.wait_ge(self.newton.sem, self.newton.upto(g, 5 + 3 * i))
        nc.vector.scalar_tensor_tensor(out=y, in0=a, scalar=1.5, in1=y, op0=ALU.add, op1=ALU.mult)\
            .then_inc(self.newton.sem, 1)

    def vector_scale(self, nc, dve, g):
        self.vector_guess(nc, dve, g)
        for i in range(NEWTON):
            self.vector_newton(nc, dve, g, i)

    def vector_rows(self, nc, dve, g):
        dve.wait_ge(self.newton.sem, self.newton.upto(g))
        if self.turns:
            if self.turned.comes(g, back=1):
                dve.wait_ge(self.turned.sem, self.turned.upto(g, back=1))
        for t in range(NB):
            nc.vector.tensor_scalar(self.xn[:, t, :], self.tile(g, t), self.mv[:, t, 0:1],
                                    self.work[:, 2, t:t + 1], ALU.subtract, ALU.mult).then_inc(self.rows.sem, 1)

    def tensor_turn(self, nc, pe, g, bank):
        for t in range(NB):
            pe.wait_ge(self.rows.sem, self.rows.upto(g, t + 1))
            last = nc.tensor.transpose(bank[:, t * D:(t + 1) * D], self.xn[:, t, :], self.ident)
        last.then_inc(self.turned.sem, 1)

    def scalar_high(self, nc, act, g, bank, high):
        act.wait_ge(self.turned.sem, self.turned.upto(g))
        nc.scalar.copy(high, bank[:, 0:GT]).then_inc(self.high.sem, 1)

    def vector_low(self, nc, dve, g, bank, high, low):
        dve.wait_ge(self.high.sem, self.high.upto(g))
        nc.vector.tensor_tensor(low, bank[:, 0:GT], high.bitcast(F32), ALU.subtract).then_inc(self.low.sem, 1)


def split_product(nc, out, w_high, w_low, m_high, m_low, start, stop, **kw):
    nc.tensor.matmul(out, w_low, m_high, start=start, stop=False, **kw)
    nc.tensor.matmul(out, w_high, m_low, start=False, stop=False, **kw)
    return nc.tensor.matmul(out, w_high, m_high, start=False, stop=stop, **kw)


def layer0_attention(nc, x, ctxt, const, cc, ident, tg, g_raw, stats, mv, work, xn, xh, xl,
                     x_d, ctxt_d, gates_d, wa_d, bo_d, const_d, x_in, signal_of):
    with ExitStack() as ctx:
        def sb(name, shape, dt=F32):
            return ctx.enter_context(nc.sbuf_tensor("a0_" + name, shape, dt))

        def pb(name):
            return ctx.enter_context(nc.psum_tensor("a0_" + name, [128, 512], F32))

        def signal(name, per):
            return signal_of("a0_" + name, per)

        wa = sb("wa", [D, 6 * 128])
        bo = sb("bo", [1, D])
        one_row = sb("one_row", [1, T])
        wqh = sb("wqh", [D, 2 * 128], F32R)
        wql = sb("wql", [D, 2 * 128], F32R)
        qc = sb("qc", [D, GT])
        qs = sb("qs", [D, GT])
        qf = sb("qf", [D, GT])
        kc = sb("kc", [D, GS])
        ks = sb("ks", [D, GS])
        kf = sb("kf", [D, GS])
        kb = sb("kb", [D, 2, NQ, NB, S])
        qz = sb("qz", [D, 2, QUADS, T])
        vr1 = sb("vr1", [S, GT])
        vx = sb("vx", [S, 2, NB, HEADS, VP], BF16)
        mx = sb("mx", [T, 2, NQ])
        ss = sb("ss", [T, 2, NQ, S])
        p32 = sb("p32", [S, 2, NQ * T])
        p1 = sb("p1", [S, 4, NQ * T], F16)
        p2 = sb("p2", [S, 4, NQ * T], F16)
        o9 = sb("o9", [T, HEADS, HD + 1])
        rec = sb("rec", [T, HEADS])
        on = sb("on", [T, HEADS, HD])
        ot = sb("ot", [D, T])

        bank_s = [pb("s0"), pb("s1")]
        bank_t = [pb("t0"), pb("t1")]
        bank_o = [pb("o0"), pb("o1")]
        bank_w = pb("w")
        bank_m = pb("m")

        norm = Norm(signal, "norm", lambda g, t: x[:, g * NB + t, :], stats, mv, work, xn, ident)
        const_in = signal("const_in", 16)
        ctx_in = signal("ctx_in", 16)
        zeroed = signal("zeroed", 1)
        g_tanh = signal("g_tanh", 1)
        wq_high = signal("wq_high", 1)
        wq_low = signal("wq_low", 1)
        q_made = signal("q_made", 2)
        qcs = signal("qcs", 2)
        k_made = signal("k_made", 2)
        kcs = signal("kcs", 2)
        kf_ready = signal("kf_ready", 1)
        kb_ready = signal("kb_ready", 1)
        v_made = signal("v_made", 1)
        v_part = signal("v_part", 2)
        v_rest = signal("v_rest", 1)
        v_third = signal("v_third", 1)
        qf_ready = signal("qf_ready", 1)
        qz_ready = signal("qz_ready", NB)
        s_full = signal("s_full", UNITS)
        s_max = signal("s_max", UNITS)
        ss_ready = signal("ss_ready", UNITS)
        t_full = signal("t_full", UNITS)
        p32_ready = signal("p32_ready", UNITS)
        p1_ready = signal("p1_ready", UNITS)
        p2_ready = signal("p2_ready", UNITS)
        pv_done = signal("pv_done", UNITS)
        o_sum = signal("o_sum", NB)
        o_rec = signal("o_rec", NB)
        on_ready = signal("on_ready", NB)
        on_turned = signal("on_turned", NB)
        ot_ready = signal("ot_ready", NB)
        w_done = signal("w_done", NB)
        x_done = signal("x_done", NB)

        def vx_parts(par):
            return vx[:, bass.ds(par, 1), :, :, :].rearrange("s o b h (n c) -> s (o b) h n c", n=3)

        def lag(u, by):
            return (0, u - by) if u >= by else (1, u - by + UNITS)

        def batch_before(g, u, by):
            b = u // QUADS - by
            return (g, b) if b >= 0 else (g - 1, b + NB)

        with nc.Block() as block:

            @block.sync
            def _(sp):
                sp.dma_start(const[:, :], const_d).then_inc(const_in.sem, 16)
                sp.dma_start(x[:, 0:NB, :], x_d[0:NB].rearrange("b t d -> t b d")).then_inc(x_in.sem, 16)
                sp.dma_start(wa[:, :], wa_d).then_inc(const_in.sem, 16)
                sp.dma_start(bo[:, :], bo_d).then_inc(const_in.sem, 16)
                sp.dma_start(g_raw[:, :], gates_d).then_inc(const_in.sem, 16)
                sp.dma_start(ctxt[:, :], ctxt_d[:, 0:GS]).then_inc(ctx_in.sem, 16)
                for g in range(1, G):
                    sp.dma_start(x[:, g * NB:(g + 1) * NB, :],
                                 x_d[g * NB:(g + 1) * NB].rearrange("b t d -> t b d")).then_inc(x_in.sem, 16)
                with sp.Fori(1, G) as g:
                    if k_made.comes(g, back=1):
                        sp.wait_ge(k_made.sem, k_made.upto(g, back=1))
                    if v_made.comes(g, back=1):
                        sp.wait_ge(v_made.sem, v_made.upto(g, back=1))
                    sp.dma_start(ctxt[:, :], ctxt_d[:, bass.ds(g * GS, GS)]).then_inc(ctx_in.sem, 16)

            @block.gpsimd
            def _(pool):
                nc.gpsimd.memset(vx[:, :, :, :, :], 0.0).then_inc(zeroed.sem, 1)
                nc.gpsimd.memset(one_row[:, :], 1.0).then_inc(zeroed.sem, 1)
                pool.wait_ge(zeroed.sem, 2)
                for par in range(2):
                    nc.gpsimd.memset(vx[:, par, :, :, HD:HD + 1], 1.0).then_inc(zeroed.sem, 1)
                pool.wait_ge(zeroed.sem, 4)

                def keys(g):
                    pool.wait_ge(kcs.sem, kcs.upto(g))
                    if kb_ready.comes(g, back=1):
                        pool.wait_ge(kb_ready.sem, kb_ready.upto(g, back=1))
                    nc.gpsimd.tensor_tensor(kf[:, :], kc[:, :], ks[:, :], ALU.add).then_inc(kf_ready.sem, 1)

                def third(g):
                    pool.wait_ge(v_part.sem, v_part.upto(g))
                    v = vx_parts(g % 2)
                    nc.gpsimd.tensor_tensor(v[:, :, :, 2, 0:HD], vr1.rearrange("s (b h c) -> s b h c", b=NB, h=HEADS),
                                            v[:, :, :, 1, 0:HD], ALU.subtract).then_inc(v_third.sem, 1)

                def queries(g):
                    pool.wait_ge(qcs.sem, qcs.upto(g))
                    if qz_ready.comes(g, back=1):
                        pool.wait_ge(qz_ready.sem, qz_ready.upto(g, back=1))
                    nc.gpsimd.tensor_tensor(qf[:, :], qc[:, :], qs[:, :], ALU.add).then_inc(qf_ready.sem, 1)

                def second_part(g, u):
                    back, v = lag(u, 4)
                    pool.wait_ge(p1_ready.sem, p1_ready.upto(g, u + 1))
                    if pv_done.comes(g, v + 1, back=back):
                        pool.wait_ge(pv_done.sem, pv_done.upto(g, v + 1, back=back))
                    nc.gpsimd.tensor_tensor(p2[:, u % 4, :], p32[:, u % 2, :], p1[:, u % 4, :],
                                            ALU.subtract).then_inc(p2_ready.sem, 1)

                def group(g, more):
                    for u in range(UNITS):
                        second_part(g, u)
                        if more:
                            if u == 4:
                                keys(g + 1)
                            if u == 8:
                                third(g + 1)
                            if u == 14:
                                queries(g + 1)

                keys(0)
                third(0)
                queries(0)
                group(0, True)
                with pool.Fori(1, G - 1) as g:
                    group(g, True)
                group(G - 1, False)

            @block.scalar
            def _(act):
                act.wait_ge(const_in.sem, 64)
                nc.scalar.activation(tg[:, :], g_raw[:, :], ACT.Tanh).then_inc(g_tanh.sem, 1)
                nc.scalar.copy(wqh[:, :], wa[:, WA["q"]:WA["q"] + 256]).then_inc(wq_high.sem, 1)
                act.wait_ge(zeroed.sem, 4)

                def high(g):
                    if q_made.comes(g, back=1):
                        act.wait_ge(q_made.sem, q_made.upto(g, back=1))
                    norm.scalar_high(nc, act, g, bank_m, xh[:, :])

                def keys(g):
                    act.wait_ge(kf_ready.sem, kf_ready.upto(g))
                    if s_full.comes(g, back=2):
                        act.wait_ge(s_full.sem, s_full.upto(g, back=2))
                    for j in range(NQ):
                        last = nc.scalar.activation(kb[:, bass.ds(g % 2, 1), j, :, :],
                                                    kf.rearrange("d (o b s) -> d o b s", o=1, b=NB), ACT.Copy,
                                                    scale=cc("mask")[:, j:j + 1])
                    last.then_inc(kb_ready.sem, 1)

                def values(g):
                    act.wait_ge(v_made.sem, v_made.upto(g))
                    if pv_done.comes(g, back=2):
                        act.wait_ge(pv_done.sem, pv_done.upto(g, back=2))
                    v = vx_parts(g % 2)
                    nc.scalar.copy(v[:, :, :, 0, 0:HD],
                                   bank_m[0:S, :].rearrange("s (b h c) -> s b h c", b=NB, h=HEADS)).then_inc(v_part.sem, 1)

                def values2(g):
                    act.wait_ge(v_rest.sem, v_rest.upto(g))
                    v = vx_parts(g % 2)
                    nc.scalar.copy(v[:, :, :, 1, 0:HD],
                                   vr1.rearrange("s (b h c) -> s b h c", b=NB, h=HEADS)).then_inc(v_part.sem, 1)

                def exps(g, u):
                    act.wait_ge(t_full.sem, t_full.upto(g, u + 1))
                    back, v = lag(u, 2)
                    if p2_ready.comes(g, v + 1, back=back):
                        act.wait_ge(p2_ready.sem, p2_ready.upto(g, v + 1, back=back))
                    nc.scalar.activation(p32[:, u % 2, :], bank_t[u % 2][0:S, :], ACT.Exp).then_inc(p32_ready.sem, 1)
                    back, v = lag(u, 4)
                    if pv_done.comes(g, v + 1, back=back):
                        act.wait_ge(pv_done.sem, pv_done.upto(g, v + 1, back=back))
                    nc.scalar.activation(p1[:, u % 4, :], bank_t[u % 2][0:S, :], ACT.Exp).then_inc(p1_ready.sem, 1)

                def turned(g, b):
                    act.wait_ge(on_turned.sem, on_turned.upto(g, b + 1))
                    nc.scalar.copy(ot[:, :], bank_w[:, 0:T]).then_inc(ot_ready.sem, 1)

                def group(g, first, more):
                    for u in range(UNITS):
                        exps(g, u)
                        if u % QUADS == 1 and not (first and u < 2 * QUADS):
                            turned(*batch_before(g, u, 2))
                        if more:
                            if u == 5:
                                keys(g + 1)
                            if u == 6:
                                values(g + 1)
                            if u == 7:
                                values2(g + 1)
                            if u == 9:
                                high(g + 1)

                keys(0)
                values(0)
                values2(0)
                high(0)
                group(0, True, True)
                with act.Fori(1, G - 1) as g:
                    group(g, False, True)
                group(G - 1, False, False)
                turned(G - 1, NB - 2)
                turned(G - 1, NB - 1)

            @block.vector
            def _(dve):
                def low(g):
                    if q_made.comes(g, back=1):
                        dve.wait_ge(q_made.sem, q_made.upto(g, back=1))
                    norm.vector_low(nc, dve, g, bank_m, xh[:, :], xl[:, :])

                def rotate_q(g, i):
                    table, out = (("cosq", qc), ("sinq", qs))[i]
                    dve.wait_ge(q_made.sem, q_made.upto(g, i + 1))
                    if qf_ready.comes(g, back=1):
                        dve.wait_ge(qf_ready.sem, qf_ready.upto(g, back=1))
                    nc.vector.tensor_tensor(
                        out.rearrange("d (b t) -> d b t", b=NB), bank_m[:, :].rearrange("d (b t) -> d b t", b=NB),
                        cc(table).rearrange("d (o t) -> d o t", o=1).to_broadcast([D, NB, T]), ALU.mult)\
                        .then_inc(qcs.sem, 1)

                def queries(g, b):
                    dve.wait_ge(qf_ready.sem, qf_ready.upto(g))
                    back, n = (0, b - 2) if b >= 2 else (1, b + NB - 2)
                    if s_full.comes(g, QUADS * (n + 1), back=back):
                        dve.wait_ge(s_full.sem, s_full.upto(g, QUADS * (n + 1), back=back))
                    for c in range(QUADS):
                        last = nc.vector.tensor_scalar(qz[:, b % 2, c, :], qf[:, b * T:(b + 1) * T],
                                                       cc("qmask")[:, c:c + 1], None, ALU.mult)
                    last.then_inc(qz_ready.sem, 1)

                def rotate_k(g, i):
                    table, out = (("cosk", kc), ("sink", ks))[i]
                    dve.wait_ge(k_made.sem, k_made.upto(g, i + 1))
                    if kf_ready.comes(g, back=1):
                        dve.wait_ge(kf_ready.sem, kf_ready.upto(g, back=1))
                    nc.vector.tensor_tensor(
                        out.rearrange("d (b s) -> d b s", b=NB), bank_m[:, 0:GS].rearrange("d (b s) -> d b s", b=NB),
                        cc(table).rearrange("d (o s) -> d o s", o=1).to_broadcast([D, NB, S]), ALU.mult)\
                        .then_inc(kcs.sem, 1)

                def rest_v(g):
                    dve.wait_ge(v_part.sem, v_part.upto(g, 1))
                    if v_third.comes(g, back=1):
                        dve.wait_ge(v_third.sem, v_third.upto(g, back=1))
                    v = vx_parts(g % 2)
                    nc.vector.tensor_tensor(vr1.rearrange("s (b h c) -> s b h c", b=NB, h=HEADS),
                                            bank_m[0:S, :].rearrange("s (b h c) -> s b h c", b=NB, h=HEADS),
                                            v[:, :, :, 0, 0:HD], ALU.subtract).then_inc(v_rest.sem, 1)

                def shift(g, u):
                    scores = bank_s[u % 2][:, 0:NQ * S].rearrange("t (j s) -> t j s", j=NQ)
                    dve.wait_ge(s_full.sem, s_full.upto(g, u + 1))
                    nc.vector.tensor_reduce(mx[:, u % 2, :], scores, AX.X, ALU.max).then_inc(s_max.sem, 1)
                    dve.wait_ge(s_max.sem, s_max.upto(g, u + 1))
                    back, v = lag(u, 2)
                    if t_full.comes(g, v + 1, back=back):
                        dve.wait_ge(t_full.sem, t_full.upto(g, v + 1, back=back))
                    nc.vector.tensor_tensor(ss[:, u % 2, :, :], scores,
                                            mx[:, u % 2, :].rearrange("t (j o) -> t j o", o=1).to_broadcast([T, NQ, S]),
                                            ALU.subtract).then_inc(ss_ready.sem, 1)

                def output(g, b):
                    dve.wait_ge(pv_done.sem, pv_done.upto(g, QUADS * (b + 1)))
                    parts = bank_o[b % 2][:, 0:HEADS * VP].rearrange("t (h n c) -> t h c n", h=HEADS, n=3)
                    nc.vector.tensor_reduce(o9[:, :, :], parts, AX.X, ALU.add).then_inc(o_sum.sem, 1)
                    dve.wait_ge(o_sum.sem, o_sum.upto(g, b + 1))
                    nc.vector.reciprocal(rec[:, :], o9[:, :, HD]).then_inc(o_rec.sem, 1)
                    dve.wait_ge(o_rec.sem, o_rec.upto(g, b + 1))
                    nc.vector.tensor_tensor(on[:, :, :], o9[:, :, 0:HD],
                                            rec.rearrange("t (h o) -> t h o", o=1).to_broadcast([T, HEADS, HD]),
                                            ALU.mult).then_inc(on_ready.sem, 1)

                def residual(g, b):
                    dve.wait_ge(w_done.sem, w_done.upto(g, b + 1))
                    nc.vector.scalar_tensor_tensor(out=x[:, g * NB + b, :], in0=bank_w[:, T:T + D], scalar=tg[:, 0:1],
                                                   in1=x[:, g * NB + b, :], op0=ALU.mult, op1=ALU.add)\
                        .then_inc(x_done.sem, 1)

                def group(g, first, more):
                    for u in range(UNITS):
                        shift(g, u)
                        if u % QUADS == 0 and not (first and u < 3 * QUADS):
                            residual(*batch_before(g, u, 3))
                        if u % QUADS == 0 and not (first and u < 2 * QUADS):
                            output(*batch_before(g, u, 2))
                        if more:
                            if u == 1:
                                rotate_k(g + 1, 0)
                            if u == 2:
                                dve.wait_ge(x_in.sem, x_in.upto(g + 1))
                                norm.vector_stats(nc, dve, g + 1)
                            if u == 3:
                                rotate_k(g + 1, 1)
                                norm.vector_guess(nc, dve, g + 1)
                            if 4 <= u < 4 + NEWTON:
                                norm.vector_newton(nc, dve, g + 1, u - 4)
                            if u == 7:
                                norm.vector_rows(nc, dve, g + 1)
                            if u == 7:
                                rest_v(g + 1)
                            if u == 10:
                                low(g + 1)
                            if u == 11:
                                rotate_q(g + 1, 0)
                            if u == 13:
                                rotate_q(g + 1, 1)
                            if u == 15:
                                queries(g + 1, 0)
                        if u % QUADS == 2 and u // QUADS < NB - 1:
                            queries(g, u // QUADS + 1)

                dve.wait_ge(const_in.sem, 64)
                dve.wait_ge(wq_high.sem, 1)
                nc.vector.tensor_tensor(wql[:, :], wa[:, WA["q"]:WA["q"] + 256], wqh[:, :].bitcast(F32),
                                        ALU.subtract).then_inc(wq_low.sem, 1)
                rotate_k(0, 0)
                rotate_k(0, 1)
                rest_v(0)
                dve.wait_ge(x_in.sem, x_in.upto(0))
                norm.vector_stats(nc, dve, 0)
                norm.vector_scale(nc, dve, 0)
                norm.vector_rows(nc, dve, 0)
                low(0)
                rotate_q(0, 0)
                rotate_q(0, 1)
                queries(0, 0)
                dve.wait_ge(g_tanh.sem, 1)
                group(0, True, True)
                with dve.Fori(1, G - 1) as g:
                    group(g, False, True)
                group(G - 1, False, False)
                residual(G - 1, NB - 3)
                output(G - 1, NB - 2)
                residual(G - 1, NB - 2)
                output(G - 1, NB - 1)
                residual(G - 1, NB - 1)

            @block.tensor
            def _(pe):
                def project_k(g, i):
                    pe.wait_ge(ctx_in.sem, ctx_in.upto(g))
                    if i:
                        pe.wait_ge(kcs.sem, kcs.upto(g, 1))
                    else:
                        if qcs.comes(g, back=1):
                            pe.wait_ge(qcs.sem, qcs.upto(g, back=1))
                    w = WA["kp" if i else "k"]
                    nc.tensor.matmul(bank_m[:, 0:GS], wa[:, w:w + 128], ctxt[:, :],
                                     start=True, stop=True).then_inc(k_made.sem, 1)

                def project_v(g):
                    pe.wait_ge(kcs.sem, kcs.upto(g))
                    for b in range(NB):
                        last = nc.tensor.matmul(bank_m[0:S, b * D:(b + 1) * D], ctxt[:, b * S:(b + 1) * S],
                                                wa[:, WA["v"]:WA["v"] + 128], start=True, stop=True)
                    last.then_inc(v_made.sem, 1)

                def turn_tokens(g):
                    pe.wait_ge(v_rest.sem, v_rest.upto(g))
                    norm.tensor_turn(nc, pe, g, bank_m)

                def project_q(g, i):
                    if i:
                        pe.wait_ge(qcs.sem, qcs.upto(g, 1))
                    else:
                        pe.wait_ge(norm.low.sem, norm.low.upto(g))
                    w = slice(128 * i, 128 * i + 128)
                    split_product(nc, bank_m[:, :], wqh[:, w], wql[:, w], xh[:, :], xl[:, :], True, True)\
                        .then_inc(q_made.sem, 1)

                def scores(g, u):
                    b, c = divmod(u, QUADS)
                    if c == 0:
                        pe.wait_ge(qz_ready.sem, qz_ready.upto(g, b + 1))
                    if u == 0:
                        pe.wait_ge(kb_ready.sem, kb_ready.upto(g))
                    back, v = lag(u, 2)
                    if ss_ready.comes(g, v + 1, back=back):
                        pe.wait_ge(ss_ready.sem, ss_ready.upto(g, v + 1, back=back))
                    nc.tensor.matmul(bank_s[u % 2][:, 0:NQ * S].rearrange("t (j s) -> t j s", j=NQ), qz[:, b % 2, c, :],
                                     kb[:, bass.ds(g % 2, 1), :, b, :].rearrange("d o j s -> d (o j) s"),
                                     start=True, stop=True).then_inc(s_full.sem, 1)

                def turn(g, u):
                    pe.wait_ge(ss_ready.sem, ss_ready.upto(g, u + 1))
                    back, v = lag(u, 2)
                    if p1_ready.comes(g, v + 1, back=back):
                        pe.wait_ge(p1_ready.sem, p1_ready.upto(g, v + 1, back=back))
                    for j in range(NQ):
                        last = nc.tensor.transpose(bank_t[u % 2][0:S, j * T:(j + 1) * T], ss[:, u % 2, j, :], ident)
                    last.then_inc(t_full.sem, 1)

                def weigh(g, u):
                    b, c = divmod(u, QUADS)
                    if u == 0:
                        pe.wait_ge(v_third.sem, v_third.upto(g))
                    if c == 0:
                        if b >= 2:
                            pe.wait_ge(o_sum.sem, o_sum.upto(g, b - 1))
                        else:
                            if o_sum.comes(g, b + NB - 1, back=1):
                                pe.wait_ge(o_sum.sem, o_sum.upto(g, b + NB - 1, back=1))
                    pe.wait_ge(p1_ready.sem, p1_ready.upto(g, u + 1))
                    pe.wait_ge(p2_ready.sem, p2_ready.upto(g, u + 1))
                    for j in range(NQ):
                        h = NQ * c + j
                        v = vx[:, bass.ds(g % 2, 1), b, h, :].rearrange("s o n -> s (o n)")
                        for i, p in enumerate((p1, p2)):
                            last = nc.tensor.matmul(bank_o[b % 2][:, h * VP:(h + 1) * VP], p[:, u % 4, j * T:(j + 1) * T],
                                                    v, start=(h == 0 and i == 0), stop=(h == HEADS - 1 and i == 1),
                                                    skip_group_check=True)
                    last.then_inc(pv_done.sem, 1)

                def out_turn(g, b):
                    pe.wait_ge(on_ready.sem, on_ready.upto(g, b + 1))
                    if b:
                        pe.wait_ge(x_done.sem, x_done.upto(g, b))
                    else:
                        if x_done.comes(g, NB, back=1):
                            pe.wait_ge(x_done.sem, x_done.upto(g, NB, back=1))
                    nc.tensor.transpose(bank_w[:, 0:T], on[:, :, :].rearrange("t h c -> t (h c)"), ident)\
                        .then_inc(on_turned.sem, 1)

                def out_project(g, b):
                    pe.wait_ge(ot_ready.sem, ot_ready.upto(g, b + 1))
                    nc.tensor.matmul(bank_w[:, T:T + D], one_row[:, :], bo[:, :], start=True, stop=False)
                    nc.tensor.matmul(bank_w[:, T:T + D], ot[:, :], wa[:, WA["o"]:WA["o"] + 128], start=False,
                                     stop=True).then_inc(w_done.sem, 1)

                def group(g, first, more):
                    for u in range(UNITS):
                        scores(g, u)
                        if not (first and u < 1):
                            back, v = lag(u, 1)
                            turn(g - back, v)
                        if not (first and u < 4):
                            back, v = lag(u, 4)
                            weigh(g - back, v)
                        if not (first and u < 2 * QUADS):
                            if u % QUADS == 1:
                                out_turn(*batch_before(g, u, 2))
                            if u % QUADS == 3:
                                out_project(*batch_before(g, u, 2))
                        if more:
                            if u == 0:
                                project_k(g + 1, 0)
                            if u == 2:
                                project_k(g + 1, 1)
                            if u == 5:
                                project_v(g + 1)
                            if u == 8:
                                turn_tokens(g + 1)
                            if u == 11:
                                project_q(g + 1, 0)
                            if u == 12:
                                project_q(g + 1, 1)

                pe.wait_ge(const_in.sem, 64)
                pe.wait_ge(zeroed.sem, 4)
                project_k(0, 0)
                project_k(0, 1)
                project_v(0)
                turn_tokens(0)
                pe.wait_ge(wq_low.sem, 1)
                project_q(0, 0)
                project_q(0, 1)
                group(0, True, True)
                with pe.Fori(1, G - 1) as g:
                    group(g, False, True)
                g = G - 1
                group(g, False, False)
                turn(g, UNITS - 1)
                for u in range(UNITS - 4, UNITS):
                    weigh(g, u)
                for b in range(NB - 2, NB):
                    out_turn(g, b)
                    out_project(g, b)


class Router:

    def __init__(self, signal, name, sb, k, tri, ident, extra):
        self.k, self.ident, self.n = k, ident, E0 + extra
        self.tri = tri
        self.lg = sb(f"{name}_lg", [T, NB, E0])
        self.top = sb(f"{name}_top", [T, NB])
        self.d = sb(f"{name}_d", [T, NB, E0])
        self.ex = sb(f"{name}_ex", [T, NB, E0])
        self.gr = sb(f"{name}_gr", [T, NB, E0, E0])
        self.eq = sb(f"{name}_eq", [T, NB, E0, E0])
        self.rank = sb(f"{name}_rank", [T, NB, E0])
        self.em = sb(f"{name}_em", [T, NB, E0])
        self.tot = sb(f"{name}_tot", [T, NB])
        self.parts = sb(f"{name}_parts", [T, NB, 2 * self.n])
        self.logits = signal(f"{name}_logits", 1)
        self.steps = signal(f"{name}_steps", 9)
        self.exp = signal(f"{name}_exp", 1)
        self.compared = signal(f"{name}_compared", 2)
        self.ranks = signal(f"{name}_ranks", 2)
        self.turned = signal(f"{name}_turned", 1)
        self.ready = signal(f"{name}_ready", 1)

    def wide(self, v):
        return v.rearrange("p (t o) -> p t o", o=1).to_broadcast([T, NB, E0])

    def vector_logits(self, nc, dve, g, bank, bias):
        if self.steps.comes(g, back=1):
            dve.wait_ge(self.steps.sem, self.steps.upto(g, back=1))
        if self.ranks.comes(g, back=1):
            dve.wait_ge(self.ranks.sem, self.ranks.upto(g, back=1))
        nc.vector.tensor_tensor(self.lg[:, :, :], bank[:, 0:NB * E0].rearrange("p (t e) -> p t e", e=E0),
                                bias.rearrange("p (o e) -> p o e", o=1).to_broadcast([T, NB, E0]), ALU.add)\
            .then_inc(self.logits.sem, 1)

    def vector_shift(self, nc, dve, g):
        dve.wait_ge(self.logits.sem, self.logits.upto(g))
        nc.vector.tensor_reduce(self.top[:, :], self.lg[:, :, :], AX.X, ALU.max).then_inc(self.steps.sem, 1)
        dve.wait_ge(self.steps.sem, self.steps.upto(g, 1))
        nc.vector.tensor_tensor(self.d[:, :, :], self.lg[:, :, :], self.wide(self.top), ALU.subtract)\
            .then_inc(self.steps.sem, 1)
        self.vector_compare(nc, dve, g)

    def scalar_exp(self, nc, act, g):
        act.wait_ge(self.steps.sem, self.steps.upto(g, 2))
        nc.scalar.activation(self.ex[:, :, :], self.d[:, :, :], ACT.Exp).then_inc(self.exp.sem, 1)

    def vector_compare(self, nc, dve, g):
        if self.steps.comes(g, 3, back=1):
            dve.wait_ge(self.steps.sem, self.steps.upto(g, 3, back=1))
        own = self.lg.rearrange("p t (e o) -> p t e o", o=1).to_broadcast([T, NB, E0, E0])
        other = self.lg.rearrange("p t (o e) -> p t o e", o=1).to_broadcast([T, NB, E0, E0])
        nc.vector.tensor_tensor(self.eq[:, :, :, :], other, own, ALU.is_equal).then_inc(self.compared.sem, 1)
        nc.vector.tensor_tensor(self.gr[:, :, :, :], other, own, ALU.is_gt).then_inc(self.compared.sem, 1)

    def gpsimd_ranks(self, nc, pool, g):
        tri = self.tri.rearrange("p (o n) -> p o n", o=1).to_broadcast([T, NB, E0 * E0])
        eq = self.eq.rearrange("p t e f -> p t (e f)")
        pool.wait_ge(self.compared.sem, self.compared.upto(g))
        nc.gpsimd.tensor_tensor(eq, eq, tri, ALU.mult).then_inc(self.ranks.sem, 1)
        pool.wait_ge(self.ranks.sem, self.ranks.upto(g, 1))
        nc.gpsimd.tensor_tensor(self.gr[:, :, :, :], self.gr[:, :, :, :], self.eq[:, :, :, :], ALU.add)\
            .then_inc(self.ranks.sem, 1)

    def vector_gates(self, nc, dve, g):
        n = self.n
        dve.wait_ge(self.ranks.sem, self.ranks.upto(g))
        nc.vector.tensor_reduce(self.rank[:, :, :], self.gr[:, :, :, :], AX.X, ALU.add).then_inc(self.steps.sem, 1)
        dve.wait_ge(self.steps.sem, self.steps.upto(g, 3))
        dve.wait_ge(self.exp.sem, self.exp.upto(g))
        nc.vector.scalar_tensor_tensor(out=self.em[:, :, :], in0=self.rank[:, :, :], scalar=self.k - 0.5,
                                       in1=self.ex[:, :, :], op0=ALU.is_lt, op1=ALU.mult).then_inc(self.steps.sem, 1)
        dve.wait_ge(self.steps.sem, self.steps.upto(g, 4))
        nc.vector.tensor_reduce(self.tot[:, :], self.em[:, :, :], AX.X, ALU.add).then_inc(self.steps.sem, 1)
        dve.wait_ge(self.steps.sem, self.steps.upto(g, 5))
        nc.vector.reciprocal(self.tot[:, :], self.tot[:, :]).then_inc(self.steps.sem, 1)
        dve.wait_ge(self.steps.sem, self.steps.upto(g, 6))
        if self.turned.comes(g, back=1):
            dve.wait_ge(self.turned.sem, self.turned.upto(g, back=1))
        nc.vector.tensor_tensor(self.d[:, :, :], self.em[:, :, :], self.wide(self.tot), ALU.mult)\
            .then_inc(self.steps.sem, 1)
        dve.wait_ge(self.steps.sem, self.steps.upto(g, 7))
        nc.vector.tensor_copy(self.parts[:, :, 0:E0].bitcast(F32R), self.d[:, :, :]).then_inc(self.steps.sem, 1)
        dve.wait_ge(self.steps.sem, self.steps.upto(g, 8))
        nc.vector.tensor_tensor(self.parts[:, :, n:n + E0].bitcast(F32R), self.d[:, :, :], self.parts[:, :, 0:E0],
                                ALU.subtract).then_inc(self.steps.sem, 1)

    def tensor_turn(self, nc, pe, g, bank):
        pe.wait_ge(self.steps.sem, self.steps.upto(g))
        for t in range(NB):
            last = nc.tensor.transpose(bank[0:2 * self.n, t * T:(t + 1) * T], self.parts[:, t, :], self.ident)
        last.then_inc(self.turned.sem, 1)

    def scalar_keep(self, nc, act, g, bank, out):
        act.wait_ge(self.turned.sem, self.turned.upto(g))
        nc.scalar.copy(out, bank[0:2 * self.n, 0:GT]).then_inc(self.ready.sem, 1)


def layer0_ffn(nc, x, cc, ident, tg, stats, mv, work, xn, xh, xl, ws_d, wf_d, sel0_d, signal_of):
    with ExitStack() as ctx:
        def sb(name, shape, dt=F32):
            return ctx.enter_context(nc.sbuf_tensor("f0_" + name, shape, dt))

        def pb(name):
            return ctx.enter_context(nc.psum_tensor("f0_" + name, [128, 512], F32))

        def signal(name, per):
            return signal_of("f0_" + name, per)

        ws = sb("ws", [128, NS_COLS])
        wh = sb("wh", [128, NS_COLS], F32R)
        wl = sb("wl", [128, NS_COLS], F32R)
        wf = sb("wf", [128, NF_COLS])
        sel_raw = sb("sel_raw", [2 * E0, E0 * 128])
        sel = sb("sel", [128, E0 * 128], F32R)
        half_b = sb("half_b", [128, 4])
        gl = sb("gl", [128, 2, D])
        te = sb("te", [128, 2, GT])
        sp = sb("sp", [128, 2, GT])
        c32 = sb("c32", [128, GT])
        cs = sb("cs", [128, 2, GT], F32R)
        gt = sb("gt", [128, 2, GT], F32R)
        r = sb("r", [EH0, 2, GT])
        hp = sb("hp", [EH0, 2, GT])
        hh = sb("hh", [EH0, 4, GT], F32R)
        hl = sb("hl", [EH0, 4, GT], F32R)
        ys = sb("ys", [128, GT], F32R)
        tm = sb("tm", [128, 2, GT])
        sm = sb("sm", [128, 2, GT])
        dec = sb("dec", [T, NB, D])
        dn = sb("dn", [T, NB, D])
        stats2 = sb("stats2", [128, NB, 6])
        mv2 = sb("mv2", [128, NB, 2])
        work2 = sb("work2", [128, 3, NB])

        def split(name, i, n=128, rows=128):
            a = WS[name][0] + i * n
            return wh[0:rows, a:a + n], wl[0:rows, a:a + n]

        def col(name, i=0, n=None, rows=128):
            a, b = WF[name]
            a, b = (a, b) if n is None else (a + i * n, a + (i + 1) * n)
            return wf[0:rows, a:b]

        bank_a = [pb("a0"), pb("a1")]
        bank_z = [pb("z0"), pb("z1")]
        bank_g = [pb("g0"), pb("g1")]
        bank_y = pb("y")
        bank_c = pb("c")

        norm = Norm(signal, "norm", lambda g, t: x[:, g * NB + t, :], stats, mv, work, xn, ident)
        scaled = signal("scaled", 2)
        norm2 = Norm(signal, "norm2", lambda g, t: dec[:, t, :], stats2, mv2, work2, dn, ident, turns=False)
        router = Router(signal, "router", sb, K0, cc("tri"), ident, 0)
        w_in = signal("w_in", 16)
        w_high = signal("w_high", 2)
        zeroed = signal("zeroed", 2)
        w_low = signal("w_low", 4)
        enc_made = signal("enc_made", 2)
        enc_tanh = signal("enc_tanh", 2)
        spikes = signal("spikes", 2)
        c_made = signal("c_made", 1)
        c_full = signal("c_full", 1)
        c_high = signal("c_high", 1)
        c_ready = signal("c_ready", 1)
        l_made = signal("l_made", 1)
        z_made = signal("z_made", E0)
        g_made = signal("g_made", E0)
        r_ready = signal("r_ready", E0)
        hp_ready = signal("hp_ready", E0)
        hh_ready = signal("hh_ready", E0)
        hl_ready = signal("hl_ready", E0)
        y_made = signal("y_made", E0)
        ys_high = signal("ys_high", 1)
        ys_ready = signal("ys_ready", 1)
        m_made = signal("m_made", 2)
        m_tanh = signal("m_tanh", 2)
        m_spikes = signal("m_spikes", 2)
        d_made = signal("d_made", 1)
        d_ready = signal("d_ready", 1)
        x_done = signal("x_done", 1)

        def before(e, by):
            return (0, e - by) if e >= by else (1, e - by + E0)

        with nc.Block() as block:

            @block.sync
            def _(sp_):
                sp_.dma_start(ws[:, :], ws_d).then_inc(w_in.sem, 16)
                sp_.dma_start(wf[:, :], wf_d).then_inc(w_in.sem, 16)
                sp_.dma_start(sel_raw[:, :], sel0_d).then_inc(w_in.sem, 16)

            @block.gpsimd
            def _(pool):
                def low(g, e):
                    pool.wait_ge(hh_ready.sem, hh_ready.upto(g, e + 1))
                    back, v = before(e, 4)
                    if y_made.comes(g, v + 1, back=back):
                        pool.wait_ge(y_made.sem, y_made.upto(g, v + 1, back=back))
                    nc.gpsimd.tensor_tensor(hl[:, e % 4, :], hp[:, e % 2, :], hh[:, e % 4, :].bitcast(F32),
                                            ALU.subtract).then_inc(hl_ready.sem, 1)

                def scale(g, i):
                    if i:
                        pool.wait_ge(scaled.sem, scaled.upto(g, 1))
                    else:
                        pool.wait_ge(norm2.rows.sem, norm2.rows.upto(g))
                    nc.gpsimd.tensor_tensor(dn[:, :, :], dn[:, :, :],
                                            gl[:, i:i + 1, :].to_broadcast([128, NB, D]),
                                            ALU.add if i else ALU.mult).then_inc(scaled.sem, 1)

                def group(g, behind, more):
                    for e in range(E0):
                        low(g, e)
                        if more and e == 5:
                            router.gpsimd_ranks(nc, pool, g + 1)
                        if behind >= 2 and e in (4, 5):
                            scale(g - 2, e - 4)

                nc.gpsimd.memset(sel[:, :].bitcast(F32), 0.0).then_inc(zeroed.sem, 1)
                nc.gpsimd.memset(gt[:, :, :].bitcast(F32), 0.0).then_inc(zeroed.sem, 1)
                router.gpsimd_ranks(nc, pool, 0)
                group(0, 0, True)
                group(1, 1, True)
                with pool.Fori(2, G - 1) as g:
                    group(g, 2, True)
                group(G - 1, 2, False)
                for g in (G - 2, G - 1):
                    scale(g, 0)
                    scale(g, 1)

            @block.scalar
            def _(act):
                act.wait_ge(w_in.sem, 48)
                nc.scalar.copy(wh[:, :], ws[:, :]).then_inc(w_high.sem, 1)
                act.wait_ge(zeroed.sem, zeroed.upto(0))
                nc.scalar.copy(sel[0:2 * E0, :], sel_raw[:, :]).then_inc(w_high.sem, 1)

                def enc_tanh_(g, i):
                    act.wait_ge(enc_made.sem, enc_made.upto(g, i + 1))
                    if spikes.comes(g, i + 1, back=1):
                        act.wait_ge(spikes.sem, spikes.upto(g, i + 1, back=1))
                    nc.scalar.activation(te[:, i, :], bank_a[1 - i][:, :], ACT.Tanh, bias=half_b[:, i:i + 1],
                                         scale=0.5).then_inc(enc_tanh.sem, 1)

                def input_parts(g):
                    act.wait_ge(c_made.sem, c_made.upto(g))
                    if l_made.comes(g, back=1):
                        act.wait_ge(l_made.sem, l_made.upto(g, back=1))
                    if c_ready.comes(g, back=1):
                        act.wait_ge(c_ready.sem, c_ready.upto(g, back=1))
                    nc.scalar.activation(c32[:, :], bank_a[1][:, :], ACT.Identity, bias=col("b_s2c"))\
                        .then_inc(c_full.sem, 1)
                    if z_made.comes(g, back=2):
                        act.wait_ge(z_made.sem, z_made.upto(g, back=2))
                    nc.scalar.activation(cs[:, bass.ds(g % 2, 1), :], bank_a[1].rearrange("p (o n) -> p o n", o=1),
                                         ACT.Identity, bias=col("b_s2c")).then_inc(c_high.sem, 1)

                def keep_gates(g):
                    if y_made.comes(g, back=2):
                        act.wait_ge(y_made.sem, y_made.upto(g, back=2))
                    router.scalar_keep(nc, act, g, bank_a[1], gt[0:2 * E0, bass.ds(g % 2, 1), :].rearrange("p o n -> p (o n)"))

                def relu(g, e):
                    act.wait_ge(z_made.sem, z_made.upto(g, e + 1))
                    back, v = before(e, 2)
                    if hp_ready.comes(g, v + 1, back=back):
                        act.wait_ge(hp_ready.sem, hp_ready.upto(g, v + 1, back=back))
                    nc.scalar.activation(r[:, e % 2, :], bank_z[e % 2][:, :], ACT.Relu, bias=col("b1", e, 1))\
                        .then_inc(r_ready.sem, 1)

                def high(g, e):
                    act.wait_ge(hp_ready.sem, hp_ready.upto(g, e + 1))
                    back, v = before(e, 4)
                    if y_made.comes(g, v + 1, back=back):
                        act.wait_ge(y_made.sem, y_made.upto(g, v + 1, back=back))
                    nc.scalar.copy(hh[:, e % 4, :], hp[:, e % 2, :]).then_inc(hh_ready.sem, 1)

                def out_high(g):
                    act.wait_ge(y_made.sem, y_made.upto(g))
                    if m_made.comes(g, back=1):
                        act.wait_ge(m_made.sem, m_made.upto(g, back=1))
                    nc.scalar.copy(ys[:, :], bank_y[:, :]).then_inc(ys_high.sem, 1)

                def m_tanh_(g, i):
                    act.wait_ge(m_made.sem, m_made.upto(g, i + 1))
                    if m_spikes.comes(g, i + 1, back=1):
                        act.wait_ge(m_spikes.sem, m_spikes.upto(g, i + 1, back=1))
                    nc.scalar.activation(tm[:, i, :], bank_c[:, :], ACT.Tanh, bias=half_b[:, 2 + i:3 + i],
                                         scale=0.5).then_inc(m_tanh.sem, 1)

                def group(g, behind, more):
                    for e in range(E0):
                        relu(g, e)
                        if e >= 1:
                            high(g, e - 1)
                        elif behind:
                            high(g - 1, E0 - 1)
                        if behind >= 1 and e == 3:
                            out_high(g - 1)
                        if more:
                            if e == 0:
                                norm.scalar_high(nc, act, g + 1, bank_a[0], xh[:, :])
                            if e == 2:
                                enc_tanh_(g + 1, 0)
                                enc_tanh_(g + 1, 1)
                            if e == 3:
                                input_parts(g + 1)
                            if e == 5:
                                router.scalar_exp(nc, act, g + 1)
                            if e == 7:
                                keep_gates(g + 1)
                        if behind >= 1:
                            if e == 4:
                                m_tanh_(g - 1, 0)
                            if e == 5:
                                m_tanh_(g - 1, 1)

                act.wait_ge(w_low.sem, w_low.upto(0))
                norm.scalar_high(nc, act, 0, bank_a[0], xh[:, :])
                enc_tanh_(0, 0)
                enc_tanh_(0, 1)
                input_parts(0)
                router.scalar_exp(nc, act, 0)
                keep_gates(0)
                group(0, 0, True)
                group(1, 1, True)
                with act.Fori(2, G - 1) as g:
                    group(g, 2, True)
                group(G - 1, 2, False)
                high(G - 1, E0 - 1)
                out_high(G - 1)
                m_tanh_(G - 1, 0)
                m_tanh_(G - 1, 1)

            @block.vector
            def _(dve):
                def encoder_spikes(g, i):
                    dve.wait_ge(enc_tanh.sem, enc_tanh.upto(g, i + 1))
                    if c_made.comes(g, back=1):
                        dve.wait_ge(c_made.sem, c_made.upto(g, back=1))
                    nc.vector.tensor_scalar(sp[:, i, :], te[:, i, :], 0.5, 0.5, ALU.mult, ALU.add)\
                        .then_inc(spikes.sem, 1)

                def input_low(g):
                    dve.wait_ge(c_full.sem, c_full.upto(g))
                    dve.wait_ge(c_high.sem, c_high.upto(g))
                    part = cs[M0:128, bass.ds(g % 2, 1), :].rearrange("p o n -> p (o n)")
                    nc.vector.tensor_tensor(part, c32[M0:128, :], part.bitcast(F32), ALU.subtract)\
                        .then_inc(c_ready.sem, 1)

                def logits(g):
                    dve.wait_ge(l_made.sem, l_made.upto(g))
                    router.vector_logits(nc, dve, g, bank_a[0], col("br"))
                    router.vector_shift(nc, dve, g)

                def gated(g, e):
                    dve.wait_ge(r_ready.sem, r_ready.upto(g, e + 1))
                    dve.wait_ge(g_made.sem, g_made.upto(g, e + 1))
                    back, v = before(e, 2)
                    if hl_ready.comes(g, v + 1, back=back):
                        dve.wait_ge(hl_ready.sem, hl_ready.upto(g, v + 1, back=back))
                    nc.vector.tensor_tensor(hp[:, e % 2, :], bank_g[e % 2][:, :], r[:, e % 2, :], ALU.mult)\
                        .then_inc(hp_ready.sem, 1)

                def out_low(g):
                    dve.wait_ge(ys_high.sem, ys_high.upto(g))
                    nc.vector.tensor_tensor(ys[M0:128, :], bank_y[M0:128, :], ys[M0:128, :].bitcast(F32), ALU.subtract)\
                        .then_inc(ys_ready.sem, 1)

                def moe_spikes(g, i):
                    dve.wait_ge(m_tanh.sem, m_tanh.upto(g, i + 1))
                    if d_made.comes(g, back=1):
                        dve.wait_ge(d_made.sem, d_made.upto(g, back=1))
                    nc.vector.tensor_scalar(sm[:, i, :], tm[:, i, :], 0.5, 0.5, ALU.mult, ALU.add)\
                        .then_inc(m_spikes.sem, 1)

                def decoded(g):
                    dve.wait_ge(d_made.sem, d_made.upto(g))
                    if norm2.rows.comes(g, back=1):
                        dve.wait_ge(norm2.rows.sem, norm2.rows.upto(g, back=1))
                    nc.vector.tensor_tensor(dec[:, :, :], bank_c.rearrange("p (t d) -> p t d", t=NB),
                                            col("b_dec").rearrange("p (o d) -> p o d", o=1).to_broadcast([128, NB, D]),
                                            ALU.add).then_inc(d_ready.sem, 1)

                def residual(g):
                    dve.wait_ge(scaled.sem, scaled.upto(g))
                    xg = x[:, bass.ds(g * NB, NB), :]
                    nc.vector.tensor_tensor(xg, xg, dn[:, :, :], ALU.add).then_inc(x_done.sem, 1)

                def group(g, behind, more):
                    for e in range(E0):
                        gated(g, e)
                        if behind >= 1 and e == 3:
                            out_low(g - 1)
                        if more:
                            if e == 1:
                                norm.vector_low(nc, dve, g + 1, bank_a[0], xh[:, :], xl[:, :])
                            if e == 3:
                                encoder_spikes(g + 1, 0)
                                encoder_spikes(g + 1, 1)
                            if e == 4:
                                input_low(g + 1)
                            if e == 5:
                                logits(g + 1)
                            if e == 6:
                                router.vector_gates(nc, dve, g + 1)
                        if behind >= 2:
                            if e == 0:
                                dve.wait_ge(d_ready.sem, d_ready.upto(g - 2))
                                norm2.vector_stats(nc, dve, g - 2)
                                norm2.vector_guess(nc, dve, g - 2)
                            if 1 <= e <= NEWTON:
                                norm2.vector_newton(nc, dve, g - 2, e - 1)
                            if e == 4:
                                norm2.vector_rows(nc, dve, g - 2)
                            if e == 7:
                                residual(g - 2)
                        if behind >= 1:
                            if e == 5:
                                moe_spikes(g - 1, 0)
                            if e == 6:
                                moe_spikes(g - 1, 1)
                            if e == 7:
                                decoded(g - 1)
                        if isinstance(g, int) and g + 2 >= G:
                            continue
                        if e == 4:
                            norm.vector_stats(nc, dve, g + 2)
                            norm.vector_guess(nc, dve, g + 2)
                        if 5 <= e < 5 + NEWTON:
                            norm.vector_newton(nc, dve, g + 2, e - 5)
                        if e == 7:
                            norm.vector_rows(nc, dve, g + 2)

                dve.wait_ge(w_in.sem, 48)
                nc.vector.tensor_scalar(half_b[:, 0:2], col("b_enc"), 0.5, None, ALU.mult).then_inc(w_low.sem, 1)
                nc.vector.tensor_scalar(half_b[:, 2:4], col("b_c2s"), 0.5, None, ALU.mult).then_inc(w_low.sem, 1)
                a, b = WF["ln_g"][0], WF["ln_b"][1]
                nc.vector.tensor_scalar(gl.rearrange("p a d -> p (a d)"), wf[:, a:b], tg[:, 2:3], None, ALU.mult)\
                    .then_inc(w_low.sem, 1)
                norm.vector_stats(nc, dve, 0)
                norm.vector_scale(nc, dve, 0)
                norm.vector_rows(nc, dve, 0)
                dve.wait_ge(w_high.sem, 1)
                nc.vector.tensor_tensor(wl[:, :], ws[:, :], wh[:, :].bitcast(F32), ALU.subtract).then_inc(w_low.sem, 1)
                norm.vector_low(nc, dve, 0, bank_a[0], xh[:, :], xl[:, :])
                norm.vector_stats(nc, dve, 1)
                norm.vector_scale(nc, dve, 1)
                encoder_spikes(0, 0)
                encoder_spikes(0, 1)
                norm.vector_rows(nc, dve, 1)
                input_low(0)
                logits(0)
                router.vector_gates(nc, dve, 0)
                group(0, 0, True)
                group(1, 1, True)
                with dve.Fori(2, G - 2) as g:
                    group(g, 2, True)
                group(G - 2, 2, True)
                group(G - 1, 2, False)

                def rest(g):
                    dve.wait_ge(d_ready.sem, d_ready.upto(g))
                    norm2.vector_stats(nc, dve, g)
                    norm2.vector_scale(nc, dve, g)
                    norm2.vector_rows(nc, dve, g)

                rest(G - 2)
                residual(G - 2)
                out_low(G - 1)
                moe_spikes(G - 1, 0)
                moe_spikes(G - 1, 1)
                decoded(G - 1)
                rest(G - 1)
                residual(G - 1)

            @block.tensor
            def _(pe):
                def turn_tokens(g):
                    if router.logits.comes(g, back=1):
                        pe.wait_ge(router.logits.sem, router.logits.upto(g, back=1))
                    norm.tensor_turn(nc, pe, g, bank_a[0])

                def encode(g, i):
                    pe.wait_ge(norm.low.sem, norm.low.upto(g))
                    if i == 0:
                        if router.ready.comes(g, back=1):
                            pe.wait_ge(router.ready.sem, router.ready.upto(g, back=1))
                    wide = split("enc", i)
                    split_product(nc, bank_a[1 - i][:, :], *wide, xh[:, :], xl[:, :], True, True)\
                        .then_inc(enc_made.sem, 1)

                def experts_input(g):
                    for i in range(2):
                        pe.wait_ge(spikes.sem, spikes.upto(g, i + 1))
                        last = nc.tensor.matmul(bank_a[1][:, :], col("s2c", i, 128), sp[:, i, :], start=i == 0,
                                                stop=i == 1)
                    last.then_inc(c_made.sem, 1)

                def make_logits(g):
                    pe.wait_ge(enc_tanh.sem, enc_tanh.upto(g))
                    pe.wait_ge(c_full.sem, c_full.upto(g))
                    for t in range(NB):
                        last = nc.tensor.matmul(bank_a[0][:, t * E0:(t + 1) * E0], c32[0:M0, t * T:(t + 1) * T],
                                                col("wr", rows=M0), start=True, stop=True)
                    last.then_inc(l_made.sem, 1)

                def turn_gates(g):
                    pe.wait_ge(c_high.sem, c_high.upto(g))
                    router.tensor_turn(nc, pe, g, bank_a[1])

                def hidden(g, e):
                    pe.wait_ge(c_ready.sem, c_ready.upto(g))
                    back, v = before(e, 2)
                    if r_ready.comes(g, v + 1, back=back):
                        pe.wait_ge(r_ready.sem, r_ready.upto(g, v + 1, back=back))
                    high_, low_ = split("w1", e)
                    both = cs[:, bass.ds(g % 2, 1), :].rearrange("p o n -> p (o n)")
                    nc.tensor.matmul(bank_z[e % 2][:, :], low_, both, start=True, stop=False)
                    nc.tensor.matmul(bank_z[e % 2][:, :], high_, both, start=False, stop=True).then_inc(z_made.sem, 1)

                def gates_of(g):
                    return gt[:, bass.ds(g % 2, 1), :].rearrange("p o n -> p (o n)")

                def spread_gate(g, e):
                    pe.wait_ge(router.ready.sem, router.ready.upto(g))
                    back, v = before(e, 2)
                    if hp_ready.comes(g, v + 1, back=back):
                        pe.wait_ge(hp_ready.sem, hp_ready.upto(g, v + 1, back=back))
                    nc.tensor.matmul(bank_g[e % 2][:, :], sel[:, e * 128:(e + 1) * 128], gates_of(g), start=True,
                                     stop=True).then_inc(g_made.sem, 1)

                def second_bias(g):
                    if ys_ready.comes(g, back=1):
                        pe.wait_ge(ys_ready.sem, ys_ready.upto(g, back=1))
                    high_, low_ = split("b2", 0)
                    nc.tensor.matmul(bank_y[:, :], low_, gates_of(g), start=True, stop=False)
                    nc.tensor.matmul(bank_y[:, :], high_, gates_of(g), start=False, stop=False)

                def output(g, e):
                    if e == 0:
                        second_bias(g)
                    pe.wait_ge(hh_ready.sem, hh_ready.upto(g, e + 1))
                    pe.wait_ge(hl_ready.sem, hl_ready.upto(g, e + 1))
                    split_product(nc, bank_y[:, :], *split("w2", e), hh[:, e % 4, :], hl[:, e % 4, :], False, e == E0 - 1)\
                        .then_inc(y_made.sem, 1)

                def to_spikes(g, i):
                    pe.wait_ge(ys_ready.sem, ys_ready.upto(g))
                    if i:
                        pe.wait_ge(m_tanh.sem, m_tanh.upto(g, 1))
                    else:
                        if d_ready.comes(g, back=1):
                            pe.wait_ge(d_ready.sem, d_ready.upto(g, back=1))
                    high_, low_ = split("c2s", i)
                    nc.tensor.matmul(bank_c[:, :], low_, ys[:, :], start=True, stop=False)
                    nc.tensor.matmul(bank_c[:, :], high_, ys[:, :], start=False, stop=True).then_inc(m_made.sem, 1)

                def decode(g):
                    pe.wait_ge(m_spikes.sem, m_spikes.upto(g))
                    for t in range(NB):
                        for i in range(2):
                            last = nc.tensor.matmul(bank_c[:, t * D:(t + 1) * D], sm[:, i, t * T:(t + 1) * T],
                                                    col("dec", i, D), start=i == 0, stop=i == 1)
                    last.then_inc(d_made.sem, 1)

                def group(g, behind, more):
                    for e in range(E0):
                        hidden(g, e)
                        spread_gate(g, e)
                        if e >= 3:
                            output(g, e - 3)
                        elif behind:
                            output(g - 1, e - 3 + E0)
                        if more:
                            if e == 0:
                                turn_tokens(g + 1)
                            if e == 2:
                                encode(g + 1, 0)
                                encode(g + 1, 1)
                            if e == 3:
                                experts_input(g + 1)
                            if e == 4:
                                make_logits(g + 1)
                            if e == 7:
                                turn_gates(g + 1)
                        if behind >= 1:
                            if e == 4:
                                to_spikes(g - 1, 0)
                            if e == 5:
                                to_spikes(g - 1, 1)
                            if e == 6:
                                decode(g - 1)

                pe.wait_ge(w_low.sem, 4)
                pe.wait_ge(w_high.sem, 2)
                turn_tokens(0)
                encode(0, 0)
                encode(0, 1)
                experts_input(0)
                make_logits(0)
                turn_gates(0)
                group(0, 0, True)
                group(1, 1, True)
                with pe.Fori(2, G - 1) as g:
                    group(g, 2, True)
                group(G - 1, 2, False)
                for e in range(E0 - 3, E0):
                    output(G - 1, e)
                to_spikes(G - 1, 0)
                to_spikes(G - 1, 1)
                decode(G - 1)


def layer1_attention(nc, x, ctxt, cc, ident, tg, stats, mv, work, xn, xh, xl, xh1, xl1, gt1, wh, wlo, wl_d, w123_d, ctxt_d,
                     signal_of):
    with ExitStack() as ctx:
        def sb(name, shape, dt=F32):
            return ctx.enter_context(nc.sbuf_tensor("a1_" + name, shape, dt))

        def pb(name):
            return ctx.enter_context(nc.psum_tensor("a1_" + name, [128, 512], F32))

        def signal(name, per):
            return signal_of("a1_" + name, per)

        wl = sb("wl", [128, NL_COLS])
        wqh = sb("wqh", [D, D], F32R)
        wql = sb("wql", [D, D], F32R)
        bqs = sb("bqs", [128, 1])
        bvt = sb("bvt", [128, D])
        raw = sb("raw", [128, 2, WPREP])
        qt = sb("qt", [D, GT])
        kt = sb("kt", [D, 2, GS])
        v = sb("v", [S, 2, GT])
        top = sb("top", [T, NB])
        ss = sb("ss", [T, NB, S])
        ex = sb("ex", [T, NB, S])
        tot = sb("tot", [T, NB])
        pt = sb("pt", [S, GT])
        x32 = sb("x32", [D, GT])
        xn2 = sb("xn2", [128, NB, D])
        stats2 = sb("stats2", [128, NB, 6])
        mv2 = sb("mv2", [128, NB, 2])
        work2 = sb("work2", [128, 3, NB])

        bank_a = [pb("a0"), pb("a1")]
        bank_b = [pb("b0"), pb("b1")]
        bank_c = [pb("c0"), pb("c1")]

        def col(name):
            a, b = WL[name]
            return wl[:, a:b]

        def x_tile(g, t):
            return x[:, g * NB + t, :]

        norm = Norm(signal, "norm", x_tile, stats, mv, work, xn, ident)
        norm2 = Norm(signal, "norm2", x_tile, stats2, mv2, work2, xn2, ident)
        router = Router(signal, "router", sb, K1, cc("tri"), ident, 1)
        w_in = signal("w_in", 16)
        raw_in = signal("raw_in", 16)
        ctx_in = signal("ctx_in", 16)
        w_high = signal("w_high", 1)
        w_low = signal("w_low", 5)
        zeroed = signal("zeroed", 1)
        raw_high = signal("raw_high", 1)
        raw_low = signal("raw_low", 1)
        q_made = signal("q_made", 1)
        q_ready = signal("q_ready", 1)
        k_made = signal("k_made", 1)
        k_ready = signal("k_ready", 1)
        v_made = signal("v_made", 1)
        v_ready = signal("v_ready", 1)
        s_made = signal("s_made", 1)
        s_top = signal("s_top", 1)
        ss_ready = signal("ss_ready", 1)
        ex_ready = signal("ex_ready", 1)
        tot_steps = signal("tot_steps", 3)
        p_turned = signal("p_turned", 1)
        pt_ready = signal("pt_ready", 1)
        o_made = signal("o_made", 1)
        x_bias = signal("x_bias", 1)
        x_done = signal("x_done", NB)
        x32_ready = signal("x32_ready", 1)
        l_made = signal("l_made", 1)

        with nc.Block() as block:

            @block.sync
            def _(sp):
                sp.dma_start(wl[:, :], wl_d).then_inc(w_in.sem, 16)

                def load(g):
                    if raw_low.comes(g, back=2):
                        sp.wait_ge(raw_low.sem, raw_low.upto(g, back=2))
                    sp.dma_start(raw[:, bass.ds(g % 2, 1), :].rearrange("p o n -> p (o n)"),
                                 w123_d[:, bass.ds(g * WPREP, WPREP)]).then_inc(raw_in.sem, 16)
                    if k_made.comes(g, back=1):
                        sp.wait_ge(k_made.sem, k_made.upto(g, back=1))
                    if v_made.comes(g, back=1):
                        sp.wait_ge(v_made.sem, v_made.upto(g, back=1))
                    sp.dma_start(ctxt[:, :], ctxt_d[:, bass.ds(g * GS, GS)]).then_inc(ctx_in.sem, 16)

                load(0)
                load(1)
                with sp.Fori(2, G) as g:
                    load(g)

            @block.gpsimd
            def _(pool):
                def bias(g):
                    pool.wait_ge(norm.rows.sem, norm.rows.upto(g))
                    xg = x[:, bass.ds(g * NB, NB), :]
                    nc.gpsimd.tensor_tensor(xg, xg, bvt.rearrange("p (o d) -> p o d", o=1).to_broadcast([T, NB, D]),
                                            ALU.add).then_inc(x_bias.sem, 1)

                def weights_low(g):
                    pool.wait_ge(raw_high.sem, raw_high.upto(g))
                    cols = bass.ds(g * WPREP, WPREP)
                    nc.gpsimd.tensor_tensor(wlo[:, cols], raw[:, bass.ds(g % 2, 1), :].rearrange("p o n -> p (o n)"),
                                            wh[:, cols].bitcast(F32), ALU.subtract).then_inc(raw_low.sem, 1)

                def step(ahead, now, behind):
                    if ahead is not None:
                        bias(ahead)
                    if now is not None:
                        weights_low(now)
                    if behind is not None:
                        router.gpsimd_ranks(nc, pool, behind)

                nc.gpsimd.memset(gt1[:, :].bitcast(F32), 0.0).then_inc(zeroed.sem, 1)
                pool.wait_ge(w_low.sem, w_low.upto(0))
                run(step, pool)

            @block.scalar
            def _(act):
                def tokens(g):
                    if q_made.comes(g, back=1):
                        act.wait_ge(q_made.sem, q_made.upto(g, back=1))
                    norm.scalar_high(nc, act, g, bank_a[0], xh[:, :])

                def queries(g):
                    act.wait_ge(q_made.sem, q_made.upto(g))
                    if s_made.comes(g, back=1):
                        act.wait_ge(s_made.sem, s_made.upto(g, back=1))
                    nc.scalar.activation(qt[:, :], bank_a[1][:, :], ACT.Identity, bias=bqs[:, :], scale=D ** -0.5)\
                        .then_inc(q_ready.sem, 1)

                def keys(g):
                    act.wait_ge(k_made.sem, k_made.upto(g))
                    if s_made.comes(g, back=2):
                        act.wait_ge(s_made.sem, s_made.upto(g, back=2))
                    nc.scalar.activation(kt[:, bass.ds(g % 2, 1), :], bank_a[0][:, 0:GS].rearrange("d (o n) -> d o n", o=1),
                                         ACT.Identity, bias=col("bk")).then_inc(k_ready.sem, 1)

                def values(g):
                    act.wait_ge(v_made.sem, v_made.upto(g))
                    if o_made.comes(g, back=2):
                        act.wait_ge(o_made.sem, o_made.upto(g, back=2))
                    nc.scalar.copy(v[:, bass.ds(g % 2, 1), :], bank_a[1][0:S, :].rearrange("d (o n) -> d o n", o=1))\
                        .then_inc(v_ready.sem, 1)

                def exps(g):
                    act.wait_ge(ss_ready.sem, ss_ready.upto(g))
                    if p_turned.comes(g, back=1):
                        act.wait_ge(p_turned.sem, p_turned.upto(g, back=1))
                    if tot_steps.comes(g, 1, back=1):
                        act.wait_ge(tot_steps.sem, tot_steps.upto(g, 1, back=1))
                    nc.scalar.activation(ex[:, :, :], ss[:, :, :], ACT.Exp).then_inc(ex_ready.sem, 1)

                def turned(g):
                    act.wait_ge(p_turned.sem, p_turned.upto(g))
                    if o_made.comes(g, back=1):
                        act.wait_ge(o_made.sem, o_made.upto(g, back=1))
                    nc.scalar.copy(pt[:, :], bank_b[1][0:S, :]).then_inc(pt_ready.sem, 1)

                def tokens2(g):
                    cols = bass.ds(g * GT, GT)
                    if l_made.comes(g, back=1):
                        act.wait_ge(l_made.sem, l_made.upto(g, back=1))
                    act.wait_ge(norm2.turned.sem, norm2.turned.upto(g))
                    nc.scalar.copy(x32[:, :], bank_c[0][:, :]).then_inc(x32_ready.sem, 1)
                    norm2.scalar_high(nc, act, g, bank_c[0], xh1[:, cols])

                def weights_high(g):
                    act.wait_ge(raw_in.sem, raw_in.upto(g))
                    nc.scalar.copy(wh[:, bass.ds(g * WPREP, WPREP)],
                                   raw[:, bass.ds(g % 2, 1), :].rearrange("p o n -> p (o n)")).then_inc(raw_high.sem, 1)

                def step(ahead, now, behind):
                    if now is not None:
                        exps(now)
                        weights_high(now)
                    if behind is not None:
                        tokens2(behind)
                    if now is not None:
                        turned(now)
                    if ahead is not None:
                        tokens(ahead)
                        keys(ahead)
                        queries(ahead)
                    if behind is not None:
                        router.scalar_exp(nc, act, behind)
                    if ahead is not None:
                        values(ahead)
                    if behind is not None:
                        router.scalar_keep(nc, act, behind, bank_c[0], gt1[0:2 * (E1 + 1), bass.ds(behind * GT, GT)])

                act.wait_ge(w_in.sem, w_in.upto(0))
                nc.scalar.copy(wqh[:, :], col("q")).then_inc(w_high.sem, 1)
                act.wait_ge(w_low.sem, w_low.upto(0))
                act.wait_ge(zeroed.sem, zeroed.upto(0))
                run(step, act)

            @block.vector
            def _(dve):
                def shift(g):
                    scores = bank_b[0][:, 0:GS].rearrange("t (b s) -> t b s", b=NB)
                    dve.wait_ge(s_made.sem, s_made.upto(g))
                    nc.vector.tensor_reduce(top[:, :], scores, AX.X, ALU.max).then_inc(s_top.sem, 1)
                    dve.wait_ge(s_top.sem, s_top.upto(g))
                    if ex_ready.comes(g, back=1):
                        dve.wait_ge(ex_ready.sem, ex_ready.upto(g, back=1))
                    nc.vector.tensor_tensor(ss[:, :, :], scores,
                                            top.rearrange("t (b o) -> t b o", o=1).to_broadcast([T, NB, S]),
                                            ALU.subtract).then_inc(ss_ready.sem, 1)

                def totals(g):
                    dve.wait_ge(ex_ready.sem, ex_ready.upto(g))
                    if x_done.comes(g, back=1):
                        dve.wait_ge(x_done.sem, x_done.upto(g, back=1))
                    nc.vector.tensor_reduce(tot[:, :], ex[:, :, :], AX.X, ALU.add).then_inc(tot_steps.sem, 1)
                    dve.wait_ge(tot_steps.sem, tot_steps.upto(g, 1))
                    nc.vector.reciprocal(tot[:, :], tot[:, :]).then_inc(tot_steps.sem, 1)
                    dve.wait_ge(tot_steps.sem, tot_steps.upto(g, 2))
                    nc.vector.tensor_scalar(tot[:, :], tot[:, :], tg[:, 1:2], None, ALU.mult).then_inc(tot_steps.sem, 1)

                def residual(g):
                    dve.wait_ge(o_made.sem, o_made.upto(g))
                    dve.wait_ge(tot_steps.sem, tot_steps.upto(g))
                    dve.wait_ge(x_bias.sem, x_bias.upto(g))
                    for t in range(NB):
                        nc.vector.scalar_tensor_tensor(out=x_tile(g, t), in0=bank_b[0][:, t * D:(t + 1) * D],
                                                       scalar=tot[:, t:t + 1], in1=x_tile(g, t), op0=ALU.mult,
                                                       op1=ALU.add).then_inc(x_done.sem, 1)

                def step(ahead, now, behind):
                    if now is not None:
                        shift(now)
                    if behind is not None:
                        norm2.vector_stats(nc, dve, behind)
                        norm2.vector_scale(nc, dve, behind)
                        norm2.vector_rows(nc, dve, behind)
                    if now is not None:
                        totals(now)
                    if ahead is not None:
                        norm.vector_stats(nc, dve, ahead)
                        norm.vector_scale(nc, dve, ahead)
                        norm.vector_rows(nc, dve, ahead)
                    if behind is not None:
                        cols = bass.ds(behind * GT, GT)
                        norm2.vector_low(nc, dve, behind, bank_c[0], xh1[:, cols], xl1[:, cols])
                    if ahead is not None:
                        norm.vector_low(nc, dve, ahead, bank_a[0], xh[:, :], xl[:, :])
                    if behind is not None:
                        dve.wait_ge(l_made.sem, l_made.upto(behind))
                        router.vector_logits(nc, dve, behind, bank_c[1], col("rb"))
                        router.vector_shift(nc, dve, behind)
                    if now is not None:
                        residual(now)
                    if behind is not None:
                        router.vector_gates(nc, dve, behind)

                dve.wait_ge(w_in.sem, w_in.upto(0))
                nc.vector.memset(router.parts[:, :, E1:E1 + 1], 1.0).then_inc(w_low.sem, 1)
                nc.vector.memset(router.parts[:, :, 2 * E1 + 1:2 * E1 + 2], 0.0).then_inc(w_low.sem, 1)
                nc.vector.tensor_scalar(bqs[:, :], col("bq"), D ** -0.5, None, ALU.mult).then_inc(w_low.sem, 1)
                nc.vector.tensor_scalar(bvt[:, :], col("bv"), tg[:, 1:2], None, ALU.mult).then_inc(w_low.sem, 1)
                dve.wait_ge(w_high.sem, w_high.upto(0))
                nc.vector.tensor_tensor(wql[:, :], col("q"), wqh[:, :].bitcast(F32), ALU.subtract).then_inc(w_low.sem, 1)
                run(step, dve)

            @block.tensor
            def _(pe):
                def turn_tokens(g):
                    if k_ready.comes(g, back=1):
                        pe.wait_ge(k_ready.sem, k_ready.upto(g, back=1))
                    norm.tensor_turn(nc, pe, g, bank_a[0])

                def queries(g):
                    pe.wait_ge(norm.low.sem, norm.low.upto(g))
                    if v_ready.comes(g, back=1):
                        pe.wait_ge(v_ready.sem, v_ready.upto(g, back=1))
                    split_product(nc, bank_a[1][:, :], wqh[:, :], wql[:, :], xh[:, :], xl[:, :], True, True)\
                        .then_inc(q_made.sem, 1)

                def keys(g):
                    pe.wait_ge(ctx_in.sem, ctx_in.upto(g))
                    pe.wait_ge(norm.low.sem, norm.low.upto(g))
                    nc.tensor.matmul(bank_a[0][:, 0:GS], col("k"), ctxt[:, :], start=True, stop=True)\
                        .then_inc(k_made.sem, 1)

                def values(g):
                    pe.wait_ge(q_ready.sem, q_ready.upto(g))
                    for b in range(NB):
                        last = nc.tensor.matmul(bank_a[1][0:S, b * D:(b + 1) * D], ctxt[:, b * S:(b + 1) * S], col("v"),
                                                start=True, stop=True)
                    last.then_inc(v_made.sem, 1)

                def scores(g):
                    pe.wait_ge(q_ready.sem, q_ready.upto(g))
                    pe.wait_ge(k_ready.sem, k_ready.upto(g))
                    if x_done.comes(g, back=1):
                        pe.wait_ge(x_done.sem, x_done.upto(g, back=1))
                    for b in range(NB):
                        last = nc.tensor.matmul(bank_b[0][:, b * S:(b + 1) * S], qt[:, b * T:(b + 1) * T],
                                                kt[:, bass.ds(g % 2, 1), b * S:(b + 1) * S].rearrange("d o n -> d (o n)"),
                                                start=True, stop=True)
                    last.then_inc(s_made.sem, 1)

                def turn_weights(g):
                    pe.wait_ge(ex_ready.sem, ex_ready.upto(g))
                    if pt_ready.comes(g, back=1):
                        pe.wait_ge(pt_ready.sem, pt_ready.upto(g, back=1))
                    for b in range(NB):
                        last = nc.tensor.transpose(bank_b[1][0:S, b * T:(b + 1) * T], ex[:, b, :], ident)
                    last.then_inc(p_turned.sem, 1)

                def outputs(g):
                    pe.wait_ge(pt_ready.sem, pt_ready.upto(g))
                    pe.wait_ge(v_ready.sem, v_ready.upto(g))
                    for b in range(NB):
                        last = nc.tensor.matmul(bank_b[0][:, b * D:(b + 1) * D], pt[:, b * T:(b + 1) * T],
                                                v[:, bass.ds(g % 2, 1), b * D:(b + 1) * D].rearrange("s o n -> s (o n)"),
                                                start=True, stop=True)
                    last.then_inc(o_made.sem, 1)

                def turn_tokens2(g):
                    if router.ready.comes(g, back=1):
                        pe.wait_ge(router.ready.sem, router.ready.upto(g, back=1))
                    norm2.tensor_turn(nc, pe, g, bank_c[0])

                def logits(g):
                    pe.wait_ge(x32_ready.sem, x32_ready.upto(g))
                    if router.logits.comes(g, back=1):
                        pe.wait_ge(router.logits.sem, router.logits.upto(g, back=1))
                    for t in range(NB):
                        last = nc.tensor.matmul(bank_c[1][:, t * E1:(t + 1) * E1], x32[:, t * T:(t + 1) * T], col("wg"),
                                                start=True, stop=True)
                    last.then_inc(l_made.sem, 1)

                def turn_gates(g):
                    pe.wait_ge(norm2.low.sem, norm2.low.upto(g))
                    router.tensor_turn(nc, pe, g, bank_c[0])

                def step(ahead, now, behind):
                    if now is not None:
                        scores(now)
                    if behind is not None:
                        turn_tokens2(behind)
                    if now is not None:
                        turn_weights(now)
                    if ahead is not None:
                        turn_tokens(ahead)
                    if behind is not None:
                        logits(behind)
                    if now is not None:
                        outputs(now)
                    if ahead is not None:
                        keys(ahead)
                        queries(ahead)
                        values(ahead)
                    if behind is not None:
                        turn_gates(behind)

                pe.wait_ge(w_low.sem, w_low.upto(0))
                run(step, pe)


def run(step, eng):
    step(0, None, None)
    step(1, 0, None)
    step(2, 1, 0)
    with eng.Fori(2, G - 1) as g:
        step(g + 1, g, g - 1)
    step(None, G - 1, G - 2)
    step(None, None, G - 1)


def layer1_ffn(nc, x, ident, tg, xh1, xl1, gt1, wh, wlo, sel1_d, out_d, signal_of):
    LAG = 3
    with ExitStack() as ctx:
        def sb(name, shape, dt=F32):
            return ctx.enter_context(nc.sbuf_tensor("f1_" + name, shape, dt))

        def pb(name):
            return ctx.enter_context(nc.psum_tensor("f1_" + name, [128, 512], F32))

        def signal(name, per):
            return signal_of("f1_" + name, per)

        N1 = 2 * (E1 + 1)
        sel_raw = sb("sel_raw", [N1, W1C // 2])
        sel = sb("sel", [128, W1C], F32R)
        si = sb("si", [128, 2, GT])
        ab = sb("ab", [128, 2, GT])
        ag = sb("ag", [128, 2, GT])
        ah = sb("ah", [128, 4, GT], F32R)
        al = sb("al", [128, 4, GT], F32R)
        od = sb("od", [D, GT])

        bank_1 = [pb("h10"), pb("h11")]
        bank_2 = [pb("h20"), pb("h21")]
        bank_g = pb("g")
        bank_d = pb("d")
        bank_x = pb("x")

        sel_in = signal("sel_in", 16)
        zeroed = signal("zeroed", 1)
        sel_ready = signal("sel_ready", 1)
        h1_made = signal("h1_made", CH)
        h2_made = signal("h2_made", CH)
        g_made = signal("g_made", CH)
        si_ready = signal("si_ready", CH)
        ab_ready = signal("ab_ready", CH)
        ag_ready = signal("ag_ready", CH)
        ah_ready = signal("ah_ready", CH)
        al_ready = signal("al_ready", CH)
        d_made = signal("d_made", CH)
        od_ready = signal("od_ready", 1)
        od_turned = signal("od_turned", 1)
        x_done = signal("x_done", 1)
        stored = signal("stored", 16)

        def before(c, by):
            return (0, c - by) if c >= by else (1, c - by + CH)

        def weight(which, c):
            a = which * W1C + c * 128
            return wh[:, a:a + 128], wlo[:, a:a + 128]

        with nc.Block() as block:

            @block.sync
            def _(sp):
                for i in range(2):
                    if sel_ready.comes(i, back=1):
                        sp.wait_ge(sel_ready.sem, sel_ready.upto(i, back=1))
                    sp.dma_start(sel_raw[:, :], sel1_d[:, i * W1C // 2:(i + 1) * W1C // 2]).then_inc(sel_in.sem, 16)
                with sp.Fori(0, G) as g:
                    sp.wait_ge(x_done.sem, x_done.upto(g))
                    sp.dma_start(out_d[bass.ds(g * NB, NB)].rearrange("b t d -> t b d"),
                                 x[:, bass.ds(g * NB, NB), :]).then_inc(stored.sem, 16)
                sp.wait_ge(stored.sem, 16 * G)

            @block.gpsimd
            def _(pool):
                nc.gpsimd.memset(sel[:, :].bitcast(F32), 0.0).then_inc(zeroed.sem, 1)
                with pool.Fori(0, G) as g:
                    for c in range(CH):
                        pool.wait_ge(ah_ready.sem, ah_ready.upto(g, c + 1))
                        nc.gpsimd.tensor_tensor(al[:, c % 4, :], ag[:, c % 2, :], ah[:, c % 4, :].bitcast(F32),
                                                ALU.subtract).then_inc(al_ready.sem, 1)

            @block.scalar
            def _(act):
                def silu(g, c, first):
                    act.wait_ge(h1_made.sem, h1_made.upto(g, c + 1))
                    back, v = before(c, 2)
                    if not (first and back):
                        if ab_ready.comes(g, v + 1, back=back):
                            act.wait_ge(ab_ready.sem, ab_ready.upto(g, v + 1, back=back))
                    nc.scalar.activation(si[:, c % 2, :], bank_1[c % 2][:, :], ACT.Silu).then_inc(si_ready.sem, 1)

                def high(g, c, first):
                    act.wait_ge(ag_ready.sem, ag_ready.upto(g, c + 1))
                    back, v = before(c, 4)
                    if not (first and back):
                        if d_made.comes(g, v + 1, back=back):
                            act.wait_ge(d_made.sem, d_made.upto(g, v + 1, back=back))
                    nc.scalar.copy(ah[:, c % 4, :], ag[:, c % 2, :]).then_inc(ah_ready.sem, 1)

                def output(g):
                    act.wait_ge(d_made.sem, d_made.upto(g))
                    nc.scalar.copy(od[:, :], bank_d[:, :]).then_inc(od_ready.sem, 1)

                def group(g, first):
                    for c in range(CH):
                        silu(g, c, first)
                        if c >= 1:
                            high(g, c - 1, first)
                        elif not first:
                            high(g - 1, CH - 1, False)
                        if c == LAG and not first:
                            output(g - 1)

                act.wait_ge(zeroed.sem, zeroed.upto(0))
                for i in range(2):
                    act.wait_ge(sel_in.sem, sel_in.upto(i))
                    nc.scalar.copy(sel[0:N1, i * W1C // 2:(i + 1) * W1C // 2], sel_raw[:, :]).then_inc(sel_ready.sem, 1)
                group(0, True)
                with act.Fori(1, G) as g:
                    group(g, False)
                high(G - 1, CH - 1, False)
                output(G - 1)

            @block.vector
            def _(dve):
                def product(g, c, first):
                    dve.wait_ge(si_ready.sem, si_ready.upto(g, c + 1))
                    dve.wait_ge(h2_made.sem, h2_made.upto(g, c + 1))
                    back, v = before(c, 2)
                    if not (first and back):
                        if ag_ready.comes(g, v + 1, back=back):
                            dve.wait_ge(ag_ready.sem, ag_ready.upto(g, v + 1, back=back))
                    nc.vector.tensor_tensor(ab[:, c % 2, :], bank_2[c % 2][:, :], si[:, c % 2, :], ALU.mult)\
                        .then_inc(ab_ready.sem, 1)

                def gated(g, c, first):
                    dve.wait_ge(g_made.sem, g_made.upto(g, c + 1))
                    dve.wait_ge(ab_ready.sem, ab_ready.upto(g, c + 1))
                    back, v = before(c, 2)
                    if not (first and back):
                        if al_ready.comes(g, v + 1, back=back):
                            dve.wait_ge(al_ready.sem, al_ready.upto(g, v + 1, back=back))
                    nc.vector.tensor_tensor(ag[:, c % 2, :], bank_g[:, :], ab[:, c % 2, :], ALU.mult)\
                        .then_inc(ag_ready.sem, 1)

                def residual(g):
                    dve.wait_ge(od_turned.sem, od_turned.upto(g))
                    xg = x[:, bass.ds(g * NB, NB), :]
                    nc.vector.scalar_tensor_tensor(out=xg, in0=bank_x.rearrange("t (b d) -> t b d", b=NB),
                                                   scalar=tg[:, 3:4], in1=xg, op0=ALU.mult, op1=ALU.add)\
                        .then_inc(x_done.sem, 1)

                def group(g, first):
                    for c in range(CH):
                        product(g, c, first)
                        gated(g, c, first)
                        if c == LAG + 2 and not first:
                            residual(g - 1)

                group(0, True)
                with dve.Fori(1, G) as g:
                    group(g, False)
                residual(G - 1)

            @block.tensor
            def _(pe):
                def up(g, c, first):
                    cols = bass.ds(g * GT, GT)
                    back, v = before(c, 2)
                    for which, bank, made, read in ((0, bank_1, h1_made, si_ready), (1, bank_2, h2_made, ab_ready)):
                        if not (first and back):
                            if read.comes(g, v + 1, back=back):
                                pe.wait_ge(read.sem, read.upto(g, v + 1, back=back))
                        split_product(nc, bank[c % 2][:, :], *weight(which, c), xh1[:, cols], xl1[:, cols], True, True)\
                            .then_inc(made.sem, 1)

                def spread_gate(g, c, first):
                    back, v = before(c, 1)
                    if not (first and back):
                        if ag_ready.comes(g, v + 1, back=back):
                            pe.wait_ge(ag_ready.sem, ag_ready.upto(g, v + 1, back=back))
                    nc.tensor.matmul(bank_g[:, :], sel[:, c * 128:(c + 1) * 128], gt1[:, bass.ds(g * GT, GT)],
                                     start=True, stop=True).then_inc(g_made.sem, 1)

                def down(g, c):
                    if c == 0:
                        if od_ready.comes(g, back=1):
                            pe.wait_ge(od_ready.sem, od_ready.upto(g, back=1))
                    pe.wait_ge(ah_ready.sem, ah_ready.upto(g, c + 1))
                    pe.wait_ge(al_ready.sem, al_ready.upto(g, c + 1))
                    split_product(nc, bank_d[:, :], *weight(2, c), ah[:, c % 4, :], al[:, c % 4, :], c == 0, c == CH - 1)\
                        .then_inc(d_made.sem, 1)

                def turn_output(g):
                    pe.wait_ge(od_ready.sem, od_ready.upto(g))
                    for b in range(NB):
                        last = nc.tensor.transpose(bank_x[:, b * D:(b + 1) * D], od[:, b * T:(b + 1) * T], ident)
                    last.then_inc(od_turned.sem, 1)

                def group(g, first):
                    for c in range(CH):
                        up(g, c, first)
                        if c >= LAG:
                            down(g, c - LAG)
                        elif not first:
                            down(g - 1, c - LAG + CH)
                        spread_gate(g, c, first)
                        if c == LAG + 1 and not first:
                            turn_output(g - 1)

                pe.wait_ge(sel_ready.sem, sel_ready.upto(1))
                group(0, True)
                with pe.Fori(1, G) as g:
                    group(g, False)
                for c in range(CH - LAG, CH):
                    down(G - 1, c)
                turn_output(G - 1)


def _constants():
    inv_freq = (1.0 / 10000.0 ** (np.arange(0, HD, 2, dtype=np.float32) / HD)).astype(np.float32)
    freqs = np.arange(T, dtype=np.float32)[:, None] * inv_freq[None, :]
    emb = np.concatenate([freqs, freqs], axis=-1)
    cos, sin = np.cos(emb).astype(np.float32), np.sin(emb).astype(np.float32)
    sin[:, :HD // 2] *= -1.0
    cos, sin = np.tile(cos.T, (HEADS, 1)), np.tile(sin.T, (HEADS, 1))
    c = np.zeros((128, NC_COLS), np.float32)

    def put(name, value):
        a, b = CC[name]
        c[:, a:b] = value

    scale = np.float32(HD ** -0.5)
    put("ident", np.eye(128, dtype=np.float32))
    put("cosq", cos * scale)
    put("sinq", sin * scale)
    put("cosk", cos[:, :S])
    put("sink", sin[:, :S])
    put("mask", ((np.arange(128)[:, None] // HD) % NQ == np.arange(NQ)[None, :]).astype(np.float32))
    put("qmask", (np.arange(128)[:, None] // (NQ * HD) == np.arange(QUADS)[None, :]).astype(np.float32))
    put("tri", (np.arange(8)[None, :] < np.arange(8)[:, None]).astype(np.float32).reshape(1, 64))
    n0 = 2 * E0
    sel0 = np.zeros((n0, E0, 128), np.float32)
    for e in range(E0):
        sel0[e, e] = sel0[E0 + e, e] = 1.0
    n1 = E1 + 1
    sel1 = np.zeros((2 * n1, W1C), np.float32)
    for e in range(n1):
        sel1[e, e * H1:(e + 1) * H1] = sel1[n1 + e, e * H1:(e + 1) * H1] = 1.0
    return c, sel0.reshape(n0, E0 * 128), sel1


def _pack(at, total, parts, rows=128):
    out = np.zeros((rows, total), np.float32)
    for name, value in parts.items():
        a, b = at[name]
        value = np.asarray(value)
        out[:value.shape[0], a:b] = value.reshape(value.shape[0], -1)
    return out


def _layout(i):
    swap = np.arange(D).reshape(HEADS, 2, HD // 2)[:, ::-1].reshape(-1)
    wq, wkv = i["L0_xattn_Wq"], i["L0_xattn_Wkv"]
    wk, wv = wkv[:, :D], wkv[:, D:]
    const, sel0, sel1 = _constants()
    rows = lambda v: np.broadcast_to(v.reshape(1, -1), (128, v.size))
    twice = lambda a, axis: np.concatenate([a, a], axis)
    w1 = np.transpose(i["L0_ffn_W1"], (1, 0, 2)).reshape(M0, E0 * EH0)
    w2 = twice(np.transpose(i["L0_ffn_W2"], (1, 0, 2)), 2)
    ws = _pack(WS, NS_COLS, {
        "enc": i["L0_ffn_W_enc"], "w1": twice(w1, 0), "w2": w2, "c2s": twice(i["L0_ffn_W_c2s"], 0),
        "b2": twice(twice(i["L0_ffn_b2"], 1), 0)})
    wf = _pack(WF, NF_COLS, {
        "s2c": twice(i["L0_ffn_W_s2c"].reshape(2, 128, M0).transpose(1, 0, 2), 2), "wr": i["L0_ffn_Wr"],
        "dec": i["L0_ffn_W_dec"].reshape(2, 128, D).transpose(1, 0, 2), "b_enc": i["L0_ffn_b_enc"].reshape(2, 128).T,
        "b_s2c": twice(i["L0_ffn_b_s2c"], 0).reshape(128, 1), "b1": i["L0_ffn_b1"].T,
        "b_c2s": i["L0_ffn_b_c2s"].reshape(2, 128).T, "br": rows(i["L0_ffn_br"]), "b_dec": rows(i["L0_ffn_b_dec"]),
        "ln_g": rows(i["L0_ffn_ln_g"]), "ln_b": rows(i["L0_ffn_ln_b"])})
    wl = _pack(WL, NL_COLS, {
        "q": i["L1_xattn_Wq"].T, "k": i["L1_xattn_Wk"].T, "v": i["L1_xattn_Wv"].T,
        "bq": i["L1_xattn_bq"].reshape(128, 1), "bk": i["L1_xattn_bk"].reshape(128, 1), "bv": rows(i["L1_xattn_bv"]),
        "wg": i["L1_ffn_Wg"].T, "rb": rows(i["L1_ffn_routing_bias"])})
    n = (E1 + 1) * H1
    w123 = np.zeros((128, 3, W1C), np.float32)
    w123[:, 0, :n] = np.concatenate([i["L1_ffn_W1"].reshape(-1, D), i["L1_ffn_Ws1"]]).T
    w123[:, 1, :n] = np.concatenate([i["L1_ffn_W2"].reshape(-1, D), i["L1_ffn_Ws2"]]).T
    w3 = np.zeros((W1C, D), np.float32)
    w3[:n] = np.concatenate([np.transpose(i["L1_ffn_W3"], (0, 2, 1)).reshape(-1, D), i["L1_ffn_Ws3"].T])
    w123[:, 2, :] = w3.reshape(CH, 128, D).transpose(1, 0, 2).reshape(128, W1C)
    return {
        "x": i["x"], "ctxt": i["ctx_1024"].reshape(B * S, D).T, "gates": np.broadcast_to(
            np.concatenate([i["g_xattn"], i["g_ffn"]]).reshape(1, 4), (128, 4)),
        "wa": np.concatenate([wq, wq[:, swap], wk, wk[:, swap], wv, i["L0_xattn_Wo"]], 1),
        "bo": i["L0_xattn_bo"].reshape(1, D), "const": const, "ws": ws, "wf": wf, "wl": wl,
        "sel0": sel0, "sel1": sel1, "w123": w123.reshape(128, 3 * W1C)}


def kernel(**inputs):
    from concourse import bacc
    from concourse.bass_utils import run_bass_kernel_spmd

    laid_out = _layout({name: np.asarray(a) for name, a in inputs.items()})
    nc = bacc.Bacc("TRN2", target_bir_lowering=False, num_devices=1)
    arrays, args = {}, []
    for name, a in laid_out.items():
        arrays[f"in_{name}"] = np.ascontiguousarray(a)
        args.append(nc.dram_tensor(f"in_{name}", a.shape, F32, kind="ExternalInput").ap())
    args.append(nc.dram_tensor("out_x", (B, T, D), F32, kind="ExternalOutput").ap())
    build(nc, *args)
    return run_bass_kernel_spmd(nc, [arrays], core_ids=[0]).results[0]["out_x"]
```

```python
from contextlib import ExitStack

import numpy as np

import concourse.bass as bass
from concourse import mybir

B, T, S, D = 32, 128, 77, 128
NB = 4
G = B // NB
GT = NB * T
GS = NB * S
HEADS = 16
HD = D // HEADS
QUADS = HEADS // NB
NQ = 4
UNITS = NB * QUADS
VP = 3 * (HD + 1)
E0, M0, EH0, H0 = 8, 64, 128, 256
E1, K1, H1 = 8, 4, D * 2 * 4 // 3
K0 = 2
CH = -(-(E1 + 1) * H1 // 128)
W1C = CH * 128
EPS = 1e-5
RSQRT_MAGIC = 0x5F3759DF
NEWTON = 3
STEPS = 3 + 3 * NEWTON

ALU = mybir.AluOpType
ACT = mybir.ActivationFunctionType
AX = mybir.AxisListType
F32 = mybir.dt.float32
F32R = mybir.dt.float32r
BF16 = mybir.dt.bfloat16
F16 = mybir.dt.float16
I32 = mybir.dt.int32

WA = {n: i * 128 for i, n in enumerate(("q", "qp", "k", "kp", "v", "o"))}
CC, _at = {}, 0
for _n, _w in (("ident", 128), ("cosq", T), ("sinq", T), ("cosk", S), ("sink", S), ("mask", NQ), ("qmask", QUADS), ("tri", 64)):
    CC[_n] = (_at, _at + _w)
    _at += _w
NC_COLS = _at
WS, _at = {}, 0
for _n, _w in (("enc", H0), ("w1", E0 * EH0), ("w2", E0 * 2 * M0), ("c2s", H0), ("b2", 2 * M0)):
    WS[_n] = (_at, _at + _w)
    _at += _w
NS_COLS = _at
WPARTS = 4
WF, _at = {}, 0
for _n, _w in (("s2c", 2 * 2 * M0), ("wr", E0), ("dec", 2 * D), ("b_enc", 2), ("b_s2c", 1), ("b1", E0),
               ("b_c2s", 2), ("br", E0), ("b_dec", D), ("ln_g", D), ("ln_b", D)):
    WF[_n] = (_at, _at + _w)
    _at += _w
NF_COLS = _at
WL, _at = {}, 0
for _n, _w in (("q", D), ("k", D), ("v", D), ("bq", 1), ("bk", 1), ("bv", D), ("wg", E1), ("rb", E1)):
    WL[_n] = (_at, _at + _w)
    _at += _w
NL_COLS = _at


class Signal:

    def __init__(self, sem, per):
        self.sem, self.per = sem, per

    def upto(self, g, k=None, back=0):
        return g * self.per + ((self.per if k is None else k) - back * self.per)

    def comes(self, g, k=None, back=0):
        return not isinstance(g, int) or self.upto(g, k, back) > 0


def build(nc, x_d, ctxt_d, gates_d, wa_d, bo_d, const_d, ws_d, wf_d, wl_d, sel0_d, sel1_d, w123_d, out_d):
    ctx = ExitStack()
    with ctx:
        def sb(name, shape, dt=F32):
            return ctx.enter_context(nc.sbuf_tensor(name, shape, dt))

        def signal(name, per):
            return Signal(ctx.enter_context(nc.semaphore(name)), per)

        x = sb("x", [T, B, D])
        ctxt = sb("ctxt", [D, GS])
        const = sb("const", [128, NC_COLS])
        tg = sb("tg", [128, 4])
        g_raw = sb("g_raw", [128, 4])
        stats = sb("stats", [128, NB, 6])
        mv = sb("mv", [128, NB, 2])
        work = sb("work", [128, 3, NB])
        xn = sb("xn", [128, NB, D])
        xh = sb("xh", [D, GT], F32R)
        xl = sb("xl", [D, GT], F32R)

        def cc(name):
            a, b = CC[name]
            return const[:, a:b]

        ident = cc("ident")

        w123 = sb("w123", [128, W1C])
        w123_in = ctx.enter_context(nc.semaphore("w123_in"))
        x_in = signal("x_in", 16)
        x_rest_in = signal("x_rest_in", 16)
        f0 = dict(ws=sb("ws", [128, W1C]), wh=sb("f0_wh", [128, W1C], F32R), wl=sb("f0_wl", [128, W1C], F32R),
                  wf=sb("wf", [128, NF_COLS]), sel_raw=sb("sel0_raw", [2 * E0, E0 * 128]),
                  w_in=signal("f0_w_in", 48), w_high=signal("f0_w_high", WPARTS), w_low=signal("f0_w_low", WPARTS))
        layer0_attention(nc, f0, ws_d, wf_d, sel0_d, x, ctxt, const, cc, ident, tg, g_raw, stats, mv, work, xn, xh, xl,
                         x_d, ctxt_d, gates_d, wa_d, bo_d, const_d, x_in, x_rest_in, signal)
        banks = [ctx.enter_context(nc.psum_tensor(f"bank_{n}", [128, 512], F32)) for n in "pr"]
        a1 = Attention1(nc, ctx, x, ctxt, cc, ident, tg, stats, mv, work, xn, xh, xl, *banks, signal)
        layer0_ffn(nc, f0, a1, x, cc, ident, tg, stats, mv, work, xn, xh, xl, w123, w123_d, w123_in, wl_d, ctxt_d,
                   signal)
        layer1(nc, f0, a1, x, ident, tg, ctxt, w123, w123_d, ctxt_d, sel1_d, out_d, w123_in, signal)


class Norm:

    def __init__(self, signal, name, tile, stats, mv, work, xn, ident, turns=True):
        self.tile, self.stats, self.mv, self.work, self.xn, self.ident = tile, stats, mv, work, xn, ident
        self.bn = signal(f"{name}_bn", NB + 1)
        self.newton = signal(f"{name}_newton", NB + STEPS)
        self.rows = signal(f"{name}_rows", NB)
        self.turned = signal(f"{name}_turned", 1)
        self.high = signal(f"{name}_high", 1)
        self.low = signal(f"{name}_low", 1)
        self.turns = turns

    def vector_stats(self, nc, dve, g, tiles=range(NB)):
        for t in tiles:
            nc.vector.bn_stats(self.stats[:, t, :], self.tile(g, t)).then_inc(self.bn.sem, 1)

    def vector_moments(self, nc, dve, g):
        dve.wait_ge(self.bn.sem, self.bn.upto(g, NB))
        dve.sem_inc(self.bn.sem, 1)
        for t in range(NB):
            nc.vector.bn_aggr(self.mv[:, t, :], self.stats[:, t, :]).then_inc(self.newton.sem, 1)

    def vector_step(self, nc, dve, g, i):
        v, a, y = self.work[:, 0, :], self.work[:, 1, :], self.work[:, 2, :]
        dve.wait_ge(self.newton.sem, self.newton.upto(g, NB + i))
        if i == 0:
            step = nc.vector.tensor_scalar(v, self.mv[:, :, 1], EPS, None, ALU.add)
        elif i == 1:
            step = nc.vector.tensor_scalar(a.bitcast(I32), v.bitcast(I32), 1, None, ALU.logical_shift_right)
        elif i == 2:
            step = nc.vector.tensor_scalar(y.bitcast(I32), a.bitcast(I32), -1, RSQRT_MAGIC, ALU.mult, ALU.add)
        elif i % 3 == 0:
            step = nc.vector.tensor_tensor(a, y, y, ALU.mult)
        elif i % 3 == 1:
            step = nc.vector.scalar_tensor_tensor(out=a, in0=a, scalar=-0.5, in1=v, op0=ALU.mult, op1=ALU.mult)
        else:
            step = nc.vector.scalar_tensor_tensor(out=y, in0=a, scalar=1.5, in1=y, op0=ALU.add, op1=ALU.mult)
        step.then_inc(self.newton.sem, 1)

    def vector_scale(self, nc, dve, g):
        for i in range(STEPS):
            self.vector_step(nc, dve, g, i)

    def vector_rows(self, nc, dve, g, tiles=range(NB)):
        dve.wait_ge(self.newton.sem, self.newton.upto(g))
        if self.turns:
            if self.turned.comes(g, back=1):
                dve.wait_ge(self.turned.sem, self.turned.upto(g, back=1))
        for t in tiles:
            nc.vector.tensor_scalar(self.xn[:, t, :], self.tile(g, t), self.mv[:, t, 0:1],
                                    self.work[:, 2, t:t + 1], ALU.subtract, ALU.mult).then_inc(self.rows.sem, 1)

    def tensor_turn(self, nc, pe, g, bank):
        for t in range(NB):
            pe.wait_ge(self.rows.sem, self.rows.upto(g, t + 1))
            last = nc.tensor.transpose(bank[:, t * D:(t + 1) * D], self.xn[:, t, :], self.ident)
        last.then_inc(self.turned.sem, 1)

    def scalar_high(self, nc, act, g, bank, high):
        act.wait_ge(self.turned.sem, self.turned.upto(g))
        nc.scalar.copy(high, bank[:, 0:GT]).then_inc(self.high.sem, 1)

    def vector_low(self, nc, dve, g, bank, high, low):
        dve.wait_ge(self.high.sem, self.high.upto(g))
        nc.vector.tensor_tensor(low, bank[:, 0:GT], high.bitcast(F32), ALU.subtract).then_inc(self.low.sem, 1)


def split_product(nc, out, w_high, w_low, m_high, m_low, start, stop, **kw):
    nc.tensor.matmul(out, w_low, m_high, start=start, stop=False, **kw)
    nc.tensor.matmul(out, w_high, m_low, start=False, stop=False, **kw)
    return nc.tensor.matmul(out, w_high, m_high, start=False, stop=stop, **kw)


PLAN = {"k0": 1, "rk0": 1, "k1": 2, "rk1": 3, "kf": 2, "kb": 5, "turn": 6, "high": 5, "low": 7, "q0": 9, "rq0": 10,
        "q1": 11, "rq1": 12, "qf": 10, "v": 13, "v1": 11, "rest": 14, "v2": 13, "v3": 13, "ahead": 5}



def layer0_attention(nc, f0, ws_d, wf_d, sel0_d, x, ctxt, const, cc, ident, tg, g_raw, stats, mv, work, xn, xh, xl,
                     x_d, ctxt_d, gates_d, wa_d, bo_d, const_d, x_in, x_rest_in, signal_of):
    with ExitStack() as ctx:
        def sb(name, shape, dt=F32):
            return ctx.enter_context(nc.sbuf_tensor("a0_" + name, shape, dt))

        def pb(name):
            return ctx.enter_context(nc.psum_tensor("a0_" + name, [128, 512], F32))

        def signal(name, per):
            return signal_of("a0_" + name, per)

        wa = sb("wa", [D, 6 * 128])
        bo = sb("bo", [1, D])
        one_row = sb("one_row", [1, T])
        wqh = sb("wqh", [D, 2 * 128], F32R)
        wql = sb("wql", [D, 2 * 128], F32R)
        qc = sb("qc", [D, GT])
        qs = sb("qs", [D, GT])
        qf = sb("qf", [D, 2, GT])
        kc = sb("kc", [D, GS])
        ks = sb("ks", [D, GS])
        kf = sb("kf", [D, GS])
        kb = sb("kb", [D, 2, NQ, NB, S])
        qz = sb("qz", [D, 2, QUADS, T])
        vr1 = sb("vr1", [S, GT])
        vx = sb("vx", [S, 2, NB, HEADS, VP], BF16)
        mx = sb("mx", [T, 2, NQ])
        ss = sb("ss", [T, 2, NQ, S])
        p32 = sb("p32", [S, 2, NQ * T])
        p1 = sb("p1", [S, 4, NQ * T], F16)
        p2 = sb("p2", [S, 4, NQ * T], F16)
        o9 = sb("o9", [T, HEADS, HD + 1])
        rec = sb("rec", [T, HEADS])
        on = sb("on", [T, HEADS, HD])
        ot = sb("ot", [D, T])

        bank_s = [pb("s0"), pb("s1")]
        bank_t = [pb("t0"), pb("t1")]
        bank_o = [pb("o0"), pb("o1")]
        bank_w = pb("w")
        bank_m = pb("m")

        w_in, w_high, w_low = f0["w_in"], f0["w_high"], f0["w_low"]

        def w_part(name, i):
            return f0[name][:, i * NS_COLS // WPARTS:(i + 1) * NS_COLS // WPARTS]

        norm = Norm(signal, "norm", lambda g, t: x[:, g * NB + t, :], stats, mv, work, xn, ident)
        const_in = signal("const_in", 16)
        ctx_in = signal("ctx_in", 16)
        zeroed = signal("zeroed", 1)
        wq_high = signal("wq_high", 2)
        wq_low = signal("wq_low", 1)
        q_made = signal("q_made", 2)
        qcs = signal("qcs", 2)
        k_made = signal("k_made", 2)
        kcs = signal("kcs", 2)
        kf_ready = signal("kf_ready", 1)
        kb_ready = signal("kb_ready", NQ)
        v_made = signal("v_made", 1)
        v_part = signal("v_part", 2)
        v_rest = signal("v_rest", 1)
        v_third = signal("v_third", 1)
        qf_ready = signal("qf_ready", 2)
        qz_ready = signal("qz_ready", UNITS)
        s_full = signal("s_full", UNITS)
        s_max = signal("s_max", UNITS)
        ss_ready = signal("ss_ready", UNITS)
        t_full = signal("t_full", UNITS)
        p1_ready = signal("p1_ready", UNITS)
        p2_ready = signal("p2_ready", UNITS)
        pv_done = signal("pv_done", UNITS)
        o_sum = signal("o_sum", NB)
        o_rec = signal("o_rec", NB)
        on_ready = signal("on_ready", NB)
        on_turned = signal("on_turned", NB)
        ot_ready = signal("ot_ready", NB)
        w_done = signal("w_done", NB)
        x_done = signal("x_done", NB)

        def vx_parts(par):
            return vx[:, bass.ds(par, 1), :, :, :].rearrange("s o b h (n c) -> s (o b) h n c", n=3)

        def lag(u, by):
            return (0, u - by) if u >= by else (1, u - by + UNITS)

        def batch_before(g, u, by):
            b = u // QUADS - by
            return (g, b) if b >= 0 else (g - 1, b + NB)

        with nc.Block() as block:

            @block.sync
            def _(sp):
                sp.dma_start(const[:, :], const_d).then_inc(const_in.sem, 16)
                sp.dma_start(x[:, 0:NB, :], x_d[0:NB].rearrange("b t d -> t b d")).then_inc(x_in.sem, 16)
                sp.dma_start(wa[:, :], wa_d).then_inc(const_in.sem, 16)
                sp.dma_start(bo[:, :], bo_d).then_inc(const_in.sem, 16)
                sp.dma_start(g_raw[:, :], gates_d).then_inc(const_in.sem, 16)
                sp.dma_start(ctxt[:, :], ctxt_d[:, 0:GS]).then_inc(ctx_in.sem, 16)
                sp.dma_start(x[:, NB:B, :], x_d[NB:B].rearrange("b t d -> t b d")).then_inc(x_rest_in.sem, 16)
                with sp.Fori(1, G) as g:
                    if k_made.comes(g, back=1):
                        sp.wait_ge(k_made.sem, k_made.upto(g, back=1))
                    if v_made.comes(g, back=1):
                        sp.wait_ge(v_made.sem, v_made.upto(g, back=1))
                    sp.dma_start(ctxt[:, :], ctxt_d[:, bass.ds(g * GS, GS)]).then_inc(ctx_in.sem, 16)
                for to, of in ((f0["ws"], ws_d), (f0["wf"], wf_d), (f0["sel_raw"], sel0_d)):
                    sp.dma_start(to[:, 0:of.shape[1]], of).then_inc(w_in.sem, 16)

            @block.gpsimd
            def _(pool):
                nc.gpsimd.memset(vx[:, :, :, :, :], 0.0).then_inc(zeroed.sem, 1)
                nc.gpsimd.memset(one_row[:, :], 1.0).then_inc(zeroed.sem, 1)
                pool.wait_ge(zeroed.sem, 2)
                for par in range(2):
                    nc.gpsimd.memset(vx[:, par, :, :, HD:HD + 1], 1.0).then_inc(zeroed.sem, 1)
                pool.wait_ge(zeroed.sem, 4)

                def keys(g):
                    pool.wait_ge(kcs.sem, kcs.upto(g))
                    if kb_ready.comes(g, back=1):
                        pool.wait_ge(kb_ready.sem, kb_ready.upto(g, back=1))
                    nc.gpsimd.tensor_tensor(kf[:, :], kc[:, :], ks[:, :], ALU.add).then_inc(kf_ready.sem, 1)

                def third(g):
                    pool.wait_ge(v_part.sem, v_part.upto(g))
                    v = vx_parts(g % 2)
                    nc.gpsimd.tensor_tensor(v[:, :, :, 2, 0:HD], vr1.rearrange("s (b h c) -> s b h c", b=NB, h=HEADS),
                                            v[:, :, :, 1, 0:HD], ALU.subtract).then_inc(v_third.sem, 1)

                def queries(g):
                    pool.wait_ge(qcs.sem, qcs.upto(g))
                    if qz_ready.comes(g, back=2):
                        pool.wait_ge(qz_ready.sem, qz_ready.upto(g, back=2))
                    nc.gpsimd.tensor_tensor(qf[:, bass.ds(g % 2, 1), :].rearrange("d o n -> d (o n)"), qc[:, :], qs[:, :], ALU.add).then_inc(qf_ready.sem, 1)

                def second_part(g, u):
                    back, v = lag(u, 4)
                    pool.wait_ge(p1_ready.sem, p1_ready.upto(g, u + 1))
                    if pv_done.comes(g, v + 1, back=back):
                        pool.wait_ge(pv_done.sem, pv_done.upto(g, v + 1, back=back))
                    nc.gpsimd.tensor_tensor(p2[:, u % 4, :], p32[:, u % 2, :], p1[:, u % 4, :],
                                            ALU.subtract).then_inc(p2_ready.sem, 1)

                def group(g, more):
                    for u in range(UNITS):
                        second_part(g, u)
                        if more:
                            if u == PLAN["kf"]:
                                keys(g + 1)
                            if u == PLAN["qf"]:
                                queries(g + 1)
                            if u == PLAN["v3"]:
                                third(g + 1)

                keys(0)
                queries(0)
                third(0)
                group(0, True)
                with pool.Fori(1, G - 1) as g:
                    group(g, True)
                group(G - 1, False)

            @block.scalar
            def _(act):
                act.wait_ge(const_in.sem, 64)
                nc.scalar.activation(tg[:, :], g_raw[:, :], ACT.Tanh).then_inc(wq_high.sem, 1)
                nc.scalar.copy(wqh[:, :], wa[:, WA["q"]:WA["q"] + 256]).then_inc(wq_high.sem, 1)
                act.wait_ge(zeroed.sem, 4)

                def high(g):
                    if q_made.comes(g, back=1):
                        act.wait_ge(q_made.sem, q_made.upto(g, back=1))
                    norm.scalar_high(nc, act, g, bank_m, xh[:, :])

                def keys(g, j):
                    act.wait_ge(kf_ready.sem, kf_ready.upto(g))
                    if s_full.comes(g, back=2):
                        act.wait_ge(s_full.sem, s_full.upto(g, back=2))
                    nc.scalar.activation(kb[:, bass.ds(g % 2, 1), j, :, :], kf.rearrange("d (o b s) -> d o b s", o=1, b=NB),
                                         ACT.Copy, scale=cc("mask")[:, j:j + 1]).then_inc(kb_ready.sem, 1)

                def queries(g, u):
                    b, c = divmod(u, QUADS)
                    if u == 0:
                        act.wait_ge(qf_ready.sem, qf_ready.upto(g, 1))
                        act.sem_inc(qf_ready.sem, 1)
                    nc.scalar.activation(qz[:, b % 2, c, :].rearrange("d (o t) -> d o t", o=1),
                                         qf[:, bass.ds(g % 2, 1), b * T:(b + 1) * T], ACT.Copy,
                                         scale=cc("qmask")[:, c:c + 1]).then_inc(qz_ready.sem, 1)

                def values(g):
                    act.wait_ge(v_made.sem, v_made.upto(g))
                    if pv_done.comes(g, back=2):
                        act.wait_ge(pv_done.sem, pv_done.upto(g, back=2))
                    v = vx_parts(g % 2)
                    nc.scalar.copy(v[:, :, :, 0, 0:HD],
                                   bank_m[0:S, :].rearrange("s (b h c) -> s b h c", b=NB, h=HEADS)).then_inc(v_part.sem, 1)

                def values2(g):
                    act.wait_ge(v_rest.sem, v_rest.upto(g))
                    v = vx_parts(g % 2)
                    nc.scalar.copy(v[:, :, :, 1, 0:HD],
                                   vr1.rearrange("s (b h c) -> s b h c", b=NB, h=HEADS)).then_inc(v_part.sem, 1)

                def exps(g, u):
                    act.wait_ge(t_full.sem, t_full.upto(g, u + 1))
                    back, v = lag(u, 2)
                    if p2_ready.comes(g, v + 1, back=back):
                        act.wait_ge(p2_ready.sem, p2_ready.upto(g, v + 1, back=back))
                    nc.scalar.activation(p32[:, u % 2, :], bank_t[u % 2][0:S, :], ACT.Exp)
                    back, v = lag(u, 4)
                    if pv_done.comes(g, v + 1, back=back):
                        act.wait_ge(pv_done.sem, pv_done.upto(g, v + 1, back=back))
                    nc.scalar.activation(p1[:, u % 4, :], bank_t[u % 2][0:S, :], ACT.Exp).then_inc(p1_ready.sem, 1)

                def turned(g, b):
                    act.wait_ge(on_turned.sem, on_turned.upto(g, b + 1))
                    nc.scalar.copy(ot[:, :], bank_w[:, 0:T]).then_inc(ot_ready.sem, 1)

                def group(g, first, more):
                    for u in range(UNITS):
                        exps(g, u)
                        if u % QUADS == 2 and not (first and u < 2 * QUADS):
                            turned(*batch_before(g, u, 2))
                        if u + PLAN["ahead"] < UNITS:
                            queries(g, u + PLAN["ahead"])
                        if more:
                            if PLAN["kb"] <= u < PLAN["kb"] + NQ:
                                keys(g + 1, u - PLAN["kb"])
                            if u == PLAN["high"]:
                                high(g + 1)
                            if u == PLAN["v1"]:
                                values(g + 1)
                            if u == PLAN["v2"]:
                                values2(g + 1)
                        elif u % 3 == 0 and u // 3 < WPARTS:
                            act.wait_ge(w_in.sem, w_in.upto(0))
                            nc.scalar.copy(w_part("wh", u // 3), w_part("ws", u // 3)).then_inc(w_high.sem, 1)
                        if more:
                            if u + PLAN["ahead"] >= UNITS:
                                queries(g + 1, u + PLAN["ahead"] - UNITS)

                high(0)
                for j in range(NQ):
                    keys(0, j)
                for u in range(PLAN["ahead"]):
                    queries(0, u)
                values(0)
                values2(0)
                group(0, True, True)
                with act.Fori(1, G - 1) as g:
                    group(g, False, True)
                group(G - 1, False, False)
                turned(G - 1, NB - 2)
                turned(G - 1, NB - 1)

            @block.vector
            def _(dve):
                def low(g):
                    if q_made.comes(g, back=1):
                        dve.wait_ge(q_made.sem, q_made.upto(g, back=1))
                    norm.vector_low(nc, dve, g, bank_m, xh[:, :], xl[:, :])

                def rotate_q(g, i):
                    table, out = (("cosq", qc), ("sinq", qs))[i]
                    dve.wait_ge(q_made.sem, q_made.upto(g, i + 1))
                    if qf_ready.comes(g, back=1):
                        dve.wait_ge(qf_ready.sem, qf_ready.upto(g, back=1))
                    nc.vector.tensor_tensor(
                        out.rearrange("d (b t) -> d b t", b=NB), bank_m[:, :].rearrange("d (b t) -> d b t", b=NB),
                        cc(table).rearrange("d (o t) -> d o t", o=1).to_broadcast([D, NB, T]), ALU.mult)\
                        .then_inc(qcs.sem, 1)

                def rotate_k(g, i):
                    table, out = (("cosk", kc), ("sink", ks))[i]
                    dve.wait_ge(k_made.sem, k_made.upto(g, i + 1))
                    if kf_ready.comes(g, back=1):
                        dve.wait_ge(kf_ready.sem, kf_ready.upto(g, back=1))
                    nc.vector.tensor_tensor(
                        out.rearrange("d (b s) -> d b s", b=NB), bank_m[:, 0:GS].rearrange("d (b s) -> d b s", b=NB),
                        cc(table).rearrange("d (o s) -> d o s", o=1).to_broadcast([D, NB, S]), ALU.mult)\
                        .then_inc(kcs.sem, 1)

                def rest_v(g):
                    dve.wait_ge(v_part.sem, v_part.upto(g, 1))
                    if v_third.comes(g, back=1):
                        dve.wait_ge(v_third.sem, v_third.upto(g, back=1))
                    v = vx_parts(g % 2)
                    nc.vector.tensor_tensor(vr1.rearrange("s (b h c) -> s b h c", b=NB, h=HEADS),
                                            bank_m[0:S, :].rearrange("s (b h c) -> s b h c", b=NB, h=HEADS),
                                            v[:, :, :, 0, 0:HD], ALU.subtract).then_inc(v_rest.sem, 1)

                def scores_of(u):
                    return bank_s[u % 2][:, 0:NQ * S].rearrange("t (j s) -> t j s", j=NQ)

                def maximum(g, u):
                    dve.wait_ge(s_full.sem, s_full.upto(g, u + 1))
                    nc.vector.tensor_reduce(mx[:, u % 2, :], scores_of(u), AX.X, ALU.max).then_inc(s_max.sem, 1)

                def shift(g, u):
                    dve.wait_ge(s_max.sem, s_max.upto(g, u + 1))
                    back, v = lag(u, 2)
                    if t_full.comes(g, v + 1, back=back):
                        dve.wait_ge(t_full.sem, t_full.upto(g, v + 1, back=back))
                    nc.vector.tensor_tensor(ss[:, u % 2, :, :], scores_of(u),
                                            mx[:, u % 2, :].rearrange("t (j o) -> t j o", o=1).to_broadcast([T, NQ, S]),
                                            ALU.subtract).then_inc(ss_ready.sem, 1)

                def output_sum(g, b):
                    dve.wait_ge(pv_done.sem, pv_done.upto(g, QUADS * (b + 1)))
                    parts = bank_o[b % 2][:, 0:HEADS * VP].rearrange("t (h n c) -> t h c n", h=HEADS, n=3)
                    nc.vector.tensor_reduce(o9[:, :, :], parts, AX.X, ALU.add).then_inc(o_sum.sem, 1)

                def output_inverse(g, b):
                    dve.wait_ge(o_sum.sem, o_sum.upto(g, b + 1))
                    nc.vector.reciprocal(rec[:, :], o9[:, :, HD]).then_inc(o_rec.sem, 1)

                def output_divide(g, b):
                    dve.wait_ge(o_rec.sem, o_rec.upto(g, b + 1))
                    nc.vector.tensor_tensor(on[:, :, :], o9[:, :, 0:HD],
                                            rec.rearrange("t (h o) -> t h o", o=1).to_broadcast([T, HEADS, HD]),
                                            ALU.mult).then_inc(on_ready.sem, 1)

                def residual(g, b):
                    dve.wait_ge(w_done.sem, w_done.upto(g, b + 1))
                    nc.vector.scalar_tensor_tensor(out=x[:, g * NB + b, :], in0=bank_w[:, T:T + D], scalar=tg[:, 0:1],
                                                   in1=x[:, g * NB + b, :], op0=ALU.mult, op1=ALU.add)\
                        .then_inc(x_done.sem, 1)

                def between(g, u, first, more):
                    if u % QUADS == 1 and not (first and u < 2 * QUADS):
                        output_inverse(*batch_before(g, u, 2))
                    if not more:
                        return
                    if u == 0:
                        dve.wait_ge(x_rest_in.sem, x_rest_in.upto(0))
                        norm.vector_stats(nc, dve, g + 1)
                    if 1 <= u <= 4:
                        norm.vector_step(nc, dve, g + 1, 3 * (u - 1))
                    if u == 5:
                        norm.vector_rows(nc, dve, g + 1, range(NB // 2))
                    if u == PLAN["low"]:
                        low(g + 1)
                    if u == PLAN["rq0"]:
                        rotate_q(g + 1, 0)
                    if u == PLAN["rq1"]:
                        rotate_q(g + 1, 1)
                    if u == PLAN["rest"]:
                        rest_v(g + 1)

                def group(g, first, more):
                    for u in range(UNITS):
                        maximum(g, u)
                        between(g, u, first, more)
                        shift(g, u)
                        if more and u == 0:
                            norm.vector_moments(nc, dve, g + 1)
                        if more and 1 <= u <= 4:
                            norm.vector_step(nc, dve, g + 1, 3 * (u - 1) + 1)
                        if u % QUADS == 0 and not (first and u < 2 * QUADS):
                            output_sum(*batch_before(g, u, 2))
                        if u % QUADS == 1 and not (first and u < 2 * QUADS):
                            output_divide(*batch_before(g, u, 2))
                        if u % QUADS == 1 and not (first and u < 3 * QUADS):
                            residual(*batch_before(g, u, 3))
                        if not more and u % 3 == 1 and u // 3 < WPARTS:
                            dve.wait_ge(w_high.sem, u // 3 + 1)
                            nc.vector.tensor_tensor(w_part("wl", u // 3), w_part("ws", u // 3),
                                                    w_part("wh", u // 3).bitcast(F32), ALU.subtract).then_inc(w_low.sem, 1)
                        if more:
                            if u == PLAN["rk0"]:
                                rotate_k(g + 1, 0)
                            if u == PLAN["rk1"]:
                                rotate_k(g + 1, 1)
                            if 1 <= u <= 4:
                                norm.vector_step(nc, dve, g + 1, 3 * (u - 1) + 2)
                            if u == 5:
                                norm.vector_rows(nc, dve, g + 1, range(NB // 2, NB))

                dve.wait_ge(const_in.sem, 64)
                dve.wait_ge(wq_high.sem, 2)
                nc.vector.tensor_tensor(wql[:, :], wa[:, WA["q"]:WA["q"] + 256], wqh[:, :].bitcast(F32),
                                        ALU.subtract).then_inc(wq_low.sem, 1)
                dve.wait_ge(x_in.sem, x_in.upto(0))
                norm.vector_stats(nc, dve, 0)
                norm.vector_moments(nc, dve, 0)
                for i in range(STEPS):
                    norm.vector_step(nc, dve, 0, i)
                    if i == STEPS // 2:
                        rotate_k(0, 0)
                norm.vector_rows(nc, dve, 0)
                rotate_k(0, 1)
                low(0)
                rotate_q(0, 0)
                rotate_q(0, 1)
                rest_v(0)
                group(0, True, True)
                with dve.Fori(1, G - 1) as g:
                    group(g, False, True)
                group(G - 1, False, False)
                residual(G - 1, NB - 3)
                for b in (NB - 2, NB - 1):
                    output_sum(G - 1, b)
                    output_inverse(G - 1, b)
                    output_divide(G - 1, b)
                    residual(G - 1, b)

            @block.tensor
            def _(pe):
                def project_k(g, i):
                    pe.wait_ge(ctx_in.sem, ctx_in.upto(g))
                    if i:
                        pe.wait_ge(kcs.sem, kcs.upto(g, 1))
                    else:
                        if v_rest.comes(g, back=1):
                            pe.wait_ge(v_rest.sem, v_rest.upto(g, back=1))
                    w = WA["kp" if i else "k"]
                    nc.tensor.matmul(bank_m[:, 0:GS], wa[:, w:w + 128], ctxt[:, :],
                                     start=True, stop=True).then_inc(k_made.sem, 1)

                def project_v(g):
                    pe.wait_ge(qcs.sem, qcs.upto(g))
                    for b in range(NB):
                        last = nc.tensor.matmul(bank_m[0:S, b * D:(b + 1) * D], ctxt[:, b * S:(b + 1) * S],
                                                wa[:, WA["v"]:WA["v"] + 128], start=True, stop=True)
                    last.then_inc(v_made.sem, 1)

                def turn_tokens(g):
                    pe.wait_ge(kcs.sem, kcs.upto(g))
                    norm.tensor_turn(nc, pe, g, bank_m)

                def project_q(g, i):
                    if i:
                        pe.wait_ge(qcs.sem, qcs.upto(g, 1))
                    else:
                        pe.wait_ge(norm.low.sem, norm.low.upto(g))
                    w = slice(128 * i, 128 * i + 128)
                    split_product(nc, bank_m[:, :], wqh[:, w], wql[:, w], xh[:, :], xl[:, :], True, True)\
                        .then_inc(q_made.sem, 1)

                def scores(g, u):
                    b, c = divmod(u, QUADS)
                    pe.wait_ge(qz_ready.sem, qz_ready.upto(g, u + 1))
                    if u == 0:
                        pe.wait_ge(kb_ready.sem, kb_ready.upto(g))
                    back, v = lag(u, 2)
                    if ss_ready.comes(g, v + 1, back=back):
                        pe.wait_ge(ss_ready.sem, ss_ready.upto(g, v + 1, back=back))
                    nc.tensor.matmul(bank_s[u % 2][:, 0:NQ * S].rearrange("t (j s) -> t j s", j=NQ), qz[:, b % 2, c, :],
                                     kb[:, bass.ds(g % 2, 1), :, b, :].rearrange("d o j s -> d (o j) s"),
                                     start=True, stop=True).then_inc(s_full.sem, 1)

                def turn(g, u):
                    pe.wait_ge(ss_ready.sem, ss_ready.upto(g, u + 1))
                    back, v = lag(u, 2)
                    if p1_ready.comes(g, v + 1, back=back):
                        pe.wait_ge(p1_ready.sem, p1_ready.upto(g, v + 1, back=back))
                    for j in range(NQ):
                        last = nc.tensor.transpose(bank_t[u % 2][0:S, j * T:(j + 1) * T], ss[:, u % 2, j, :], ident)
                    last.then_inc(t_full.sem, 1)

                def weigh(g, u):
                    b, c = divmod(u, QUADS)
                    if u == 0:
                        pe.wait_ge(v_third.sem, v_third.upto(g))
                    if c == 0:
                        if b >= 2:
                            pe.wait_ge(o_sum.sem, o_sum.upto(g, b - 1))
                        else:
                            if o_sum.comes(g, b + NB - 1, back=1):
                                pe.wait_ge(o_sum.sem, o_sum.upto(g, b + NB - 1, back=1))
                    pe.wait_ge(p1_ready.sem, p1_ready.upto(g, u + 1))
                    pe.wait_ge(p2_ready.sem, p2_ready.upto(g, u + 1))
                    for j in range(NQ):
                        h = NQ * c + j
                        v = vx[:, bass.ds(g % 2, 1), b, h, :].rearrange("s o n -> s (o n)")
                        for i, p in enumerate((p1, p2)):
                            last = nc.tensor.matmul(bank_o[b % 2][:, h * VP:(h + 1) * VP], p[:, u % 4, j * T:(j + 1) * T],
                                                    v, start=(h == 0 and i == 0), stop=(h == HEADS - 1 and i == 1),
                                                    skip_group_check=True)
                    last.then_inc(pv_done.sem, 1)

                def out_turn(g, b):
                    pe.wait_ge(on_ready.sem, on_ready.upto(g, b + 1))
                    if b:
                        pe.wait_ge(x_done.sem, x_done.upto(g, b))
                    else:
                        if x_done.comes(g, NB, back=1):
                            pe.wait_ge(x_done.sem, x_done.upto(g, NB, back=1))
                    nc.tensor.transpose(bank_w[:, 0:T], on[:, :, :].rearrange("t h c -> t (h c)"), ident)\
                        .then_inc(on_turned.sem, 1)

                def out_project(g, b):
                    pe.wait_ge(ot_ready.sem, ot_ready.upto(g, b + 1))
                    nc.tensor.matmul(bank_w[:, T:T + D], one_row[:, :], bo[:, :], start=True, stop=False)
                    nc.tensor.matmul(bank_w[:, T:T + D], ot[:, :], wa[:, WA["o"]:WA["o"] + 128], start=False,
                                     stop=True).then_inc(w_done.sem, 1)

                def group(g, first, more):
                    for u in range(UNITS):
                        scores(g, u)
                        if not (first and u < 1):
                            back, v = lag(u, 1)
                            turn(g - back, v)
                        if not (first and u < 4):
                            back, v = lag(u, 4)
                            weigh(g - back, v)
                        if u % QUADS == 2 and not (first and u < 2 * QUADS):
                            out_turn(*batch_before(g, u, 2))
                        if u % QUADS == 0 and not (first and u < 3 * QUADS):
                            out_project(*batch_before(g, u, 3))
                        if more:
                            if u == PLAN["k0"]:
                                project_k(g + 1, 0)
                            if u == PLAN["k1"]:
                                project_k(g + 1, 1)
                            if u == PLAN["turn"]:
                                turn_tokens(g + 1)
                            if u == PLAN["q0"]:
                                project_q(g + 1, 0)
                            if u == PLAN["q1"]:
                                project_q(g + 1, 1)
                            if u == PLAN["v"]:
                                project_v(g + 1)

                pe.wait_ge(const_in.sem, 64)
                pe.wait_ge(zeroed.sem, 4)
                project_k(0, 0)
                project_k(0, 1)
                turn_tokens(0)
                pe.wait_ge(wq_low.sem, 1)
                project_q(0, 0)
                project_q(0, 1)
                project_v(0)
                group(0, True, True)
                with pe.Fori(1, G - 1) as g:
                    group(g, False, True)
                g = G - 1
                group(g, False, False)
                turn(g, UNITS - 1)
                for u in range(UNITS - 4, UNITS):
                    weigh(g, u)
                out_project(g, NB - 3)
                for b in range(NB - 2, NB):
                    out_turn(g, b)
                    out_project(g, b)


class Router:

    def __init__(self, signal, name, sb, k, tri, ident, extra):
        self.k, self.ident, self.n = k, ident, E0 + extra
        self.tri = tri
        self.lg = sb(f"{name}_lg", [T, NB, E0])
        self.top = sb(f"{name}_top", [T, NB])
        self.d = sb(f"{name}_d", [T, NB, E0])
        self.ex = sb(f"{name}_ex", [T, NB, E0])
        self.gr = sb(f"{name}_gr", [T, NB, E0, E0])
        self.eq = sb(f"{name}_eq", [T, NB, E0, E0])
        self.rank = sb(f"{name}_rank", [T, NB, E0])
        self.em = sb(f"{name}_em", [T, NB, E0])
        self.tot = sb(f"{name}_tot", [T, NB])
        self.parts = sb(f"{name}_parts", [T, NB, 2 * self.n])
        self.logits = signal(f"{name}_logits", 1)
        self.steps = signal(f"{name}_steps", 9)
        self.exp = signal(f"{name}_exp", 1)
        self.compared = signal(f"{name}_compared", 2)
        self.ranks = signal(f"{name}_ranks", 2)
        self.turned = signal(f"{name}_turned", 1)
        self.ready = signal(f"{name}_ready", 1)

    def wide(self, v):
        return v.rearrange("p (t o) -> p t o", o=1).to_broadcast([T, NB, E0])

    def vector_logits(self, nc, dve, g, bank, bias):
        if self.steps.comes(g, back=1):
            dve.wait_ge(self.steps.sem, self.steps.upto(g, back=1))
        if self.ranks.comes(g, back=1):
            dve.wait_ge(self.ranks.sem, self.ranks.upto(g, back=1))
        nc.vector.tensor_tensor(self.lg[:, :, :], bank[:, 0:NB * E0].rearrange("p (t e) -> p t e", e=E0),
                                bias.rearrange("p (o e) -> p o e", o=1).to_broadcast([T, NB, E0]), ALU.add)\
            .then_inc(self.logits.sem, 1)

    def vector_shift(self, nc, dve, g):
        own = self.lg.rearrange("p t (e o) -> p t e o", o=1).to_broadcast([T, NB, E0, E0])
        other = self.lg.rearrange("p t (o e) -> p t o e", o=1).to_broadcast([T, NB, E0, E0])
        dve.wait_ge(self.logits.sem, self.logits.upto(g))
        nc.vector.tensor_reduce(self.top[:, :], self.lg[:, :, :], AX.X, ALU.max).then_inc(self.steps.sem, 1)
        if self.steps.comes(g, 3, back=1):
            dve.wait_ge(self.steps.sem, self.steps.upto(g, 3, back=1))
        nc.vector.tensor_tensor(self.eq[:, :, :, :], other, own, ALU.is_equal).then_inc(self.compared.sem, 1)
        dve.wait_ge(self.steps.sem, self.steps.upto(g, 1))
        nc.vector.tensor_tensor(self.d[:, :, :], self.lg[:, :, :], self.wide(self.top), ALU.subtract)\
            .then_inc(self.steps.sem, 1)
        nc.vector.tensor_tensor(self.gr[:, :, :, :], other, own, ALU.is_gt).then_inc(self.compared.sem, 1)

    def scalar_exp(self, nc, act, g):
        act.wait_ge(self.steps.sem, self.steps.upto(g, 2))
        nc.scalar.activation(self.ex[:, :, :], self.d[:, :, :], ACT.Exp).then_inc(self.exp.sem, 1)

    def gpsimd_ranks(self, nc, pool, g):
        tri = self.tri.rearrange("p (o n) -> p o n", o=1).to_broadcast([T, NB, E0 * E0])
        eq = self.eq.rearrange("p t e f -> p t (e f)")
        pool.wait_ge(self.compared.sem, self.compared.upto(g))
        nc.gpsimd.tensor_tensor(eq, eq, tri, ALU.mult).then_inc(self.ranks.sem, 1)
        pool.wait_ge(self.ranks.sem, self.ranks.upto(g, 1))
        nc.gpsimd.tensor_tensor(self.gr[:, :, :, :], self.gr[:, :, :, :], self.eq[:, :, :, :], ALU.add)\
            .then_inc(self.ranks.sem, 1)

    def vector_gates(self, nc, dve, g):
        dve.wait_ge(self.ranks.sem, self.ranks.upto(g))
        nc.vector.tensor_reduce(self.rank[:, :, :], self.gr[:, :, :, :], AX.X, ALU.add).then_inc(self.steps.sem, 1)
        dve.wait_ge(self.steps.sem, self.steps.upto(g, 3))
        dve.wait_ge(self.exp.sem, self.exp.upto(g))
        nc.vector.scalar_tensor_tensor(out=self.em[:, :, :], in0=self.rank[:, :, :], scalar=self.k - 0.5,
                                       in1=self.ex[:, :, :], op0=ALU.is_lt, op1=ALU.mult).then_inc(self.steps.sem, 1)
        dve.wait_ge(self.steps.sem, self.steps.upto(g, 4))
        nc.vector.tensor_reduce(self.tot[:, :], self.em[:, :, :], AX.X, ALU.add).then_inc(self.steps.sem, 1)

    def vector_gates2(self, nc, dve, g):
        n = self.n
        dve.wait_ge(self.steps.sem, self.steps.upto(g, 5))
        nc.vector.reciprocal(self.tot[:, :], self.tot[:, :]).then_inc(self.steps.sem, 1)
        dve.wait_ge(self.steps.sem, self.steps.upto(g, 6))
        if self.turned.comes(g, back=1):
            dve.wait_ge(self.turned.sem, self.turned.upto(g, back=1))
        nc.vector.tensor_tensor(self.d[:, :, :], self.em[:, :, :], self.wide(self.tot), ALU.mult)\
            .then_inc(self.steps.sem, 1)
        nc.vector.tensor_tensor(self.parts[:, :, 0:E0].bitcast(F32R), self.em[:, :, :], self.wide(self.tot), ALU.mult)\
            .then_inc(self.steps.sem, 1)
        dve.wait_ge(self.steps.sem, self.steps.upto(g, 8))
        nc.vector.tensor_tensor(self.parts[:, :, n:n + E0].bitcast(F32R), self.d[:, :, :], self.parts[:, :, 0:E0],
                                ALU.subtract).then_inc(self.steps.sem, 1)

    def tensor_turn(self, nc, pe, g, bank):
        pe.wait_ge(self.steps.sem, self.steps.upto(g))
        for t in range(NB):
            last = nc.tensor.transpose(bank[0:2 * self.n, t * T:(t + 1) * T], self.parts[:, t, :], self.ident)
        last.then_inc(self.turned.sem, 1)

    def scalar_keep(self, nc, act, g, bank, out):
        act.wait_ge(self.turned.sem, self.turned.upto(g))
        nc.scalar.copy(out, bank[0:2 * self.n, 0:GT]).then_inc(self.ready.sem, 1)


LPLAN = {"rate": 2, "stats": 1, "steps": 2, "rows": 9, "bias": 10, "turn": 13, "high": 12, "low": 13, "k": 12,
         "kc": 13, "q": 16, "qc": 17, "v": 17, "vc": 19, "s": 19, "shift": 19, "exp": 21, "tot": 24, "pturn": 22,
         "pc": 24, "o": 25, "res": 25, "stats2": 27, "steps2": 29, "rows2": 35, "turn2": 37, "high2": 37, "low2": 39,
         "wg": 39, "lg": 38, "ranks": 38, "rexp": 40, "gates": 43, "gates2": 44, "gturn": 46, "keep": 47}
TPLAN = {"rate": 6, "w1a": 12, "w1b": 14, "stats": 0, "steps": 1, "rows": 3, "bias": 3, "turn": 4, "high": 4,
         "low": 5, "k": 4, "kc": 5, "q": 6, "qc": 6, "v": 7, "vc": 7, "s": 8, "shift": 8, "exp": 9, "tot": 9,
         "pturn": 10, "pc": 10, "o": 11, "res": 11, "stats2": 12, "steps2": 13, "rows2": 15, "turn2": 16,
         "high2": 16, "low2": 16, "wg": 17, "lg": 17, "ranks": 17, "rexp": 17, "gates": 18, "gates2": 18,
         "gturn": 19, "keep": 19}


class Attention1:

    def __init__(self, nc, ctx, x, ctxt, cc, ident, tg, stats, mv, work, xn, xh, xl, bank_p, bank_r, signal_of):
        def sb(name, shape, dt=F32):
            return ctx.enter_context(nc.sbuf_tensor("a1_" + name, shape, dt))

        def signal(name, per):
            return signal_of("a1_" + name, per)

        def x_tile(g, t):
            return x[:, g * NB + t, :]

        self.nc, self.x, self.ctxt, self.ident, self.tg, self.xh, self.xl = nc, x, ctxt, ident, tg, xh, xl
        self.x_tile = x_tile
        self.bank_p = bank_p
        self.bank_r = bank_r
        self.xh1 = sb("xh1", [D, 2, GT], F32R)
        self.xl1 = sb("xl1", [D, 2, GT], F32R)
        self.gt1 = sb("gt1", [128, 2, GT], F32R)
        self.w1h = sb("w1h", [128, W1C], F32R)
        self.w1l = sb("w1l", [128, W1C], F32R)
        self.wl = sb("wl", [128, NL_COLS])
        self.wqh = sb("wqh", [D, D], F32R)
        self.wql = sb("wql", [D, D], F32R)
        self.bqs = sb("bqs", [128, 1])
        self.bvt = sb("bvt", [128, D])
        self.qt = sb("qt", [D, GT])
        self.kt = sb("kt", [D, 2, GS])
        self.v = sb("v", [S, 2, GT])
        self.top = sb("top", [T, NB])
        self.ss = sb("ss", [T, NB, S])
        self.ex = sb("ex", [T, NB, S])
        self.tot = sb("tot", [T, NB])
        self.pt = sb("pt", [S, GT])
        self.x32 = sb("x32", [D, GT])
        self.xn2 = sb("xn2", [128, NB, D])
        self.stats2 = sb("stats2", [128, NB, 6])
        self.mv2 = sb("mv2", [128, NB, 2])
        self.work2 = sb("work2", [128, 3, NB])
        self.norm = Norm(signal, "norm", x_tile, stats, mv, work, xn, ident)
        self.norm2 = Norm(signal, "norm2", x_tile, self.stats2, self.mv2, self.work2, self.xn2, ident)
        self.router = Router(signal, "router", sb, K1, cc("tri"), ident, 1)
        self.w_in = signal("w_in", 16)
        self.w1_in = signal("w1_in", 16)
        self.ctx_in = signal("ctx_in", 16)
        self.w_high = signal("w_high", 1)
        self.w_low = signal("w_low", 5)
        self.q_made = signal("q_made", 1)
        self.q_ready = signal("q_ready", 1)
        self.k_made = signal("k_made", 1)
        self.k_ready = signal("k_ready", 1)
        self.v_made = signal("v_made", 1)
        self.v_ready = signal("v_ready", 1)
        self.s_made = signal("s_made", 1)
        self.s_top = signal("s_top", 1)
        self.ss_ready = signal("ss_ready", 1)
        self.ex_ready = signal("ex_ready", 1)
        self.tot_steps = signal("tot_steps", 3)
        self.p_turned = signal("p_turned", 1)
        self.pt_ready = signal("pt_ready", 1)
        self.o_made = signal("o_made", 1)
        self.x_bias = signal("x_bias", 1)
        self.xa_done = signal("xa_done", NB + 1)
        self.x32_ready = signal("x32_ready", 1)
        self.l_made = signal("l_made", 1)
        self.h2_made = signal("h2_made", CH)
        self.g_made = signal("g_made", CH)
        self.x_done = signal("x_done", 1)
        self.zeroed = signal("zeroed", 2)
        self.w1_high = signal("w1_high", 2)
        self.w1_low = signal("w1_low", 2)
        self.w3_in = signal("w3_in", 16)

    def col(self, name):
        a, b = WL[name]
        return self.wl[:, a:b]

    def of_parity(self, t, g):
        return t[:, bass.ds(g % 2, 1), :].rearrange("p o n -> p (o n)")

    def gpsimd(self, nc, pool):
        gt1, bvt, norm, router, x_bias = self.gt1, self.bvt, self.norm, self.router, self.x_bias
        zeroed, w_low, x = self.zeroed, self.w_low, self.x

        def bias(g):
            pool.wait_ge(w_low.sem, w_low.upto(0))
            pool.wait_ge(norm.rows.sem, norm.rows.upto(g))
            xg = x[:, bass.ds(g * NB, NB), :]
            nc.gpsimd.tensor_tensor(xg, xg, bvt.rearrange("p (o d) -> p o d", o=1).to_broadcast([T, NB, D]),
                                    ALU.add).then_inc(x_bias.sem, 1)

        def prepare():
            nc.gpsimd.memset(gt1[:, :, :].bitcast(F32), 0.0).then_inc(zeroed.sem, 1)

        def ahead(g, i, plan):
            if i == plan["bias"]:
                bias(g)
            if i == plan["ranks"]:
                router.gpsimd_ranks(nc, pool, g)

        return prepare, ahead

    def scalar(self, nc, act):
        xh1, gt1, wqh, bqs, qt = self.xh1, self.gt1, self.wqh, self.bqs, self.qt
        kt, v, ss, ex, pt = self.kt, self.v, self.ss, self.ex, self.pt
        x32, norm, norm2, router, w_in = self.x32, self.norm, self.norm2, self.router, self.w_in
        w_high, q_made, q_ready, k_made, k_ready = self.w_high, self.q_made, self.q_ready, self.k_made, self.k_ready
        v_made, v_ready, s_made, ss_ready, ex_ready = self.v_made, self.v_ready, self.s_made, self.ss_ready, self.ex_ready
        tot_steps, p_turned, pt_ready, o_made, x32_ready = self.tot_steps, self.p_turned, self.pt_ready, self.o_made, self.x32_ready
        l_made, h2_made, g_made, bank_p, bank_r = self.l_made, self.h2_made, self.g_made, self.bank_p, self.bank_r
        of_parity, col = self.of_parity, self.col

        def tokens(g):
            if q_made.comes(g, back=1):
                act.wait_ge(q_made.sem, q_made.upto(g, back=1))
            norm.scalar_high(nc, act, g, bank_p, self.xh[:, :])

        def queries(g):
            act.wait_ge(q_made.sem, q_made.upto(g))
            if s_made.comes(g, back=1):
                act.wait_ge(s_made.sem, s_made.upto(g, back=1))
            nc.scalar.activation(qt[:, :], bank_p[:, :], ACT.Identity, bias=bqs[:, :], scale=D ** -0.5)\
                .then_inc(q_ready.sem, 1)

        def keys(g):
            act.wait_ge(k_made.sem, k_made.upto(g))
            if s_made.comes(g, back=2):
                act.wait_ge(s_made.sem, s_made.upto(g, back=2))
            nc.scalar.activation(kt[:, bass.ds(g % 2, 1), :], bank_r[:, 0:GS].rearrange("d (o n) -> d o n", o=1),
                                 ACT.Identity, bias=col("bk")).then_inc(k_ready.sem, 1)

        def values(g):
            act.wait_ge(v_made.sem, v_made.upto(g))
            if o_made.comes(g, back=2):
                act.wait_ge(o_made.sem, o_made.upto(g, back=2))
            nc.scalar.copy(v[:, bass.ds(g % 2, 1), :], bank_r[0:S, :].rearrange("d (o n) -> d o n", o=1))\
                .then_inc(v_ready.sem, 1)

        def exps(g):
            act.wait_ge(ss_ready.sem, ss_ready.upto(g))
            if p_turned.comes(g, back=1):
                act.wait_ge(p_turned.sem, p_turned.upto(g, back=1))
            if tot_steps.comes(g, 1, back=1):
                act.wait_ge(tot_steps.sem, tot_steps.upto(g, 1, back=1))
            nc.scalar.activation(ex[:, :, :], ss[:, :, :], ACT.Exp).then_inc(ex_ready.sem, 1)

        def turned(g):
            act.wait_ge(p_turned.sem, p_turned.upto(g))
            if o_made.comes(g, back=1):
                act.wait_ge(o_made.sem, o_made.upto(g, back=1))
            nc.scalar.copy(pt[:, :], bank_r[0:S, :]).then_inc(pt_ready.sem, 1)

        def tokens2(g):
            if l_made.comes(g, back=1):
                act.wait_ge(l_made.sem, l_made.upto(g, back=1))
            act.wait_ge(norm2.turned.sem, norm2.turned.upto(g))
            nc.scalar.copy(x32[:, :], bank_r[:, :]).then_inc(x32_ready.sem, 1)
            if h2_made.comes(g, back=2):
                act.wait_ge(h2_made.sem, h2_made.upto(g, back=2))
            norm2.scalar_high(nc, act, g, bank_r, of_parity(xh1, g))

        def keep_gates(g):
            if g_made.comes(g, back=2):
                act.wait_ge(g_made.sem, g_made.upto(g, back=2))
            router.scalar_keep(nc, act, g, bank_r, gt1[0:2 * (E1 + 1), bass.ds(g % 2, 1), :].rearrange("p o n -> p (o n)"))

        def prepare():
            act.wait_ge(w_in.sem, w_in.upto(0))
            nc.scalar.copy(wqh[:, :], col("q")).then_inc(w_high.sem, 1)

        def ahead(g, i, plan):
            if i == plan["high"]:
                tokens(g)
            if i == plan["kc"]:
                keys(g)
            if i == plan["qc"]:
                queries(g)
            if i == plan["vc"]:
                values(g)
            if i == plan["exp"]:
                exps(g)
            if i == plan["pc"]:
                turned(g)
            if i == plan["high2"]:
                tokens2(g)
            if i == plan["rexp"]:
                router.scalar_exp(nc, act, g)
            if i == plan["keep"]:
                keep_gates(g)

        return prepare, ahead

    def vector(self, nc, dve):
        xh1, xl1, wqh, wql, bqs = self.xh1, self.xl1, self.wqh, self.wql, self.bqs
        bvt, top, ss, ex, tot = self.bvt, self.top, self.ss, self.ex, self.tot
        norm, norm2, router, w_in, w_high = self.norm, self.norm2, self.router, self.w_in, self.w_high
        w_low, s_made, s_top, ss_ready, ex_ready = self.w_low, self.s_made, self.s_top, self.ss_ready, self.ex_ready
        tot_steps, o_made, x_bias, xa_done, l_made = self.tot_steps, self.o_made, self.x_bias, self.xa_done, self.l_made
        tg, bank_p, bank_r, of_parity, x_tile = self.tg, self.bank_p, self.bank_r, self.of_parity, self.x_tile
        col = self.col

        def shift(g):
            scores = bank_p[:, 0:GS].rearrange("t (b s) -> t b s", b=NB)
            dve.wait_ge(s_made.sem, s_made.upto(g))
            nc.vector.tensor_reduce(top[:, :], scores, AX.X, ALU.max).then_inc(s_top.sem, 1)
            dve.wait_ge(s_top.sem, s_top.upto(g))
            if ex_ready.comes(g, back=1):
                dve.wait_ge(ex_ready.sem, ex_ready.upto(g, back=1))
            nc.vector.tensor_tensor(ss[:, :, :], scores,
                                    top.rearrange("t (b o) -> t b o", o=1).to_broadcast([T, NB, S]),
                                    ALU.subtract).then_inc(ss_ready.sem, 1)

        def totals(g):
            dve.wait_ge(ex_ready.sem, ex_ready.upto(g))
            if xa_done.comes(g, back=1):
                dve.wait_ge(xa_done.sem, xa_done.upto(g, back=1))
            nc.vector.tensor_reduce(tot[:, :], ex[:, :, :], AX.X, ALU.add).then_inc(tot_steps.sem, 1)
            dve.wait_ge(tot_steps.sem, tot_steps.upto(g, 1))
            nc.vector.reciprocal(tot[:, :], tot[:, :]).then_inc(tot_steps.sem, 1)
            dve.wait_ge(tot_steps.sem, tot_steps.upto(g, 2))
            nc.vector.tensor_scalar(tot[:, :], tot[:, :], tg[:, 1:2], None, ALU.mult).then_inc(tot_steps.sem, 1)

        def residual(g):
            dve.wait_ge(o_made.sem, o_made.upto(g))
            dve.wait_ge(tot_steps.sem, tot_steps.upto(g))
            dve.wait_ge(x_bias.sem, x_bias.upto(g))
            for t in range(NB):
                nc.vector.scalar_tensor_tensor(out=x_tile(g, t), in0=bank_p[:, t * D:(t + 1) * D],
                                               scalar=tot[:, t:t + 1], in1=x_tile(g, t), op0=ALU.mult,
                                               op1=ALU.add).then_inc(xa_done.sem, 1)

        def logits(g):
            dve.wait_ge(l_made.sem, l_made.upto(g))
            router.vector_logits(nc, dve, g, bank_p, col("rb"))
            router.vector_shift(nc, dve, g)

        def prepare():
            dve.wait_ge(w_in.sem, w_in.upto(0))
            nc.vector.memset(router.parts[:, :, E1:E1 + 1], 1.0).then_inc(w_low.sem, 1)
            nc.vector.memset(router.parts[:, :, 2 * E1 + 1:2 * E1 + 2], 0.0).then_inc(w_low.sem, 1)
            nc.vector.tensor_scalar(bqs[:, :], col("bq"), D ** -0.5, None, ALU.mult).then_inc(w_low.sem, 1)
            nc.vector.tensor_scalar(bvt[:, :], col("bv"), tg[:, 1:2], None, ALU.mult).then_inc(w_low.sem, 1)
            dve.wait_ge(w_high.sem, w_high.upto(0))
            nc.vector.tensor_tensor(wql[:, :], col("q"), wqh[:, :].bitcast(F32), ALU.subtract)\
                .then_inc(w_low.sem, 1)

        def ahead(g, i, plan):
            for at, n in (("stats", norm), ("stats2", norm2)):
                if i == plan[at]:
                    if n is norm2:
                        dve.wait_ge(xa_done.sem, xa_done.upto(g, NB))
                        dve.sem_inc(xa_done.sem, 1)
                    n.vector_stats(nc, dve, g)
                    n.vector_moments(nc, dve, g)
            for at, n in (("steps", norm), ("steps2", norm2)):
                rate = plan["rate"]
                for j in range(rate * (i - plan[at]), min(rate * (i - plan[at] + 1), STEPS)):
                    if j >= 0:
                        n.vector_step(nc, dve, g, j)
            if i == plan["rows"]:
                norm.vector_rows(nc, dve, g)
            if i == plan["low"]:
                norm.vector_low(nc, dve, g, bank_p, self.xh[:, :], self.xl[:, :])
            if i == plan["shift"]:
                shift(g)
            if i == plan["tot"]:
                totals(g)
            if i == plan["res"]:
                residual(g)
            if i == plan["rows2"]:
                norm2.vector_rows(nc, dve, g)
            if i == plan["low2"]:
                norm2.vector_low(nc, dve, g, bank_r, of_parity(xh1, g), of_parity(xl1, g))
            if i == plan["lg"]:
                logits(g)
            if i == plan["gates"]:
                router.vector_gates(nc, dve, g)
            if i == plan["gates2"]:
                router.vector_gates2(nc, dve, g)

        return prepare, ahead

    def tensor(self, nc, pe):
        wqh, wql, qt, kt, v = self.wqh, self.wql, self.qt, self.kt, self.v
        ex, pt, x32, norm, norm2 = self.ex, self.pt, self.x32, self.norm, self.norm2
        router, ctx_in, q_made, q_ready, k_made = self.router, self.ctx_in, self.q_made, self.q_ready, self.k_made
        k_ready, v_made, v_ready, s_made, ss_ready = self.k_ready, self.v_made, self.v_ready, self.s_made, self.ss_ready
        ex_ready, p_turned, pt_ready, o_made, xa_done = self.ex_ready, self.p_turned, self.pt_ready, self.o_made, self.xa_done
        x32_ready, l_made, x_done, ctxt, ident = self.x32_ready, self.l_made, self.x_done, self.ctxt, self.ident
        bank_p, bank_r, col = self.bank_p, self.bank_r, self.col

        def turn_tokens(g):
            if router.logits.comes(g, back=1):
                pe.wait_ge(router.logits.sem, router.logits.upto(g, back=1))
            if x_done.comes(g, back=2):
                pe.wait_ge(x_done.sem, x_done.upto(g, back=2))
            norm.tensor_turn(nc, pe, g, bank_p)

        def queries(g):
            pe.wait_ge(norm.low.sem, norm.low.upto(g))
            split_product(nc, bank_p[:, :], wqh[:, :], wql[:, :], self.xh[:, :], self.xl[:, :], True, True)\
                .then_inc(q_made.sem, 1)

        def keys(g):
            pe.wait_ge(ctx_in.sem, ctx_in.upto(g))
            if router.ready.comes(g, back=1):
                pe.wait_ge(router.ready.sem, router.ready.upto(g, back=1))
            nc.tensor.matmul(bank_r[:, 0:GS], col("k"), ctxt[:, :], start=True, stop=True)\
                .then_inc(k_made.sem, 1)

        def values(g):
            pe.wait_ge(k_ready.sem, k_ready.upto(g))
            for b in range(NB):
                last = nc.tensor.matmul(bank_r[0:S, b * D:(b + 1) * D], ctxt[:, b * S:(b + 1) * S], col("v"),
                                        start=True, stop=True)
            last.then_inc(v_made.sem, 1)

        def scores(g):
            pe.wait_ge(q_ready.sem, q_ready.upto(g))
            pe.wait_ge(k_ready.sem, k_ready.upto(g))
            for b in range(NB):
                last = nc.tensor.matmul(bank_p[:, b * S:(b + 1) * S], qt[:, b * T:(b + 1) * T],
                                        kt[:, bass.ds(g % 2, 1), b * S:(b + 1) * S].rearrange("d o n -> d (o n)"),
                                        start=True, stop=True)
            last.then_inc(s_made.sem, 1)

        def turn_weights(g):
            pe.wait_ge(ex_ready.sem, ex_ready.upto(g))
            pe.wait_ge(v_ready.sem, v_ready.upto(g))
            for b in range(NB):
                last = nc.tensor.transpose(bank_r[0:S, b * T:(b + 1) * T], ex[:, b, :], ident)
            last.then_inc(p_turned.sem, 1)

        def attend(g):
            pe.wait_ge(pt_ready.sem, pt_ready.upto(g))
            pe.wait_ge(v_ready.sem, v_ready.upto(g))
            for b in range(NB):
                last = nc.tensor.matmul(bank_p[:, b * D:(b + 1) * D], pt[:, b * T:(b + 1) * T],
                                        v[:, bass.ds(g % 2, 1), b * D:(b + 1) * D].rearrange("s o n -> s (o n)"),
                                        start=True, stop=True)
            last.then_inc(o_made.sem, 1)

        def turn_tokens2(g):
            pe.wait_ge(pt_ready.sem, pt_ready.upto(g))
            norm2.tensor_turn(nc, pe, g, bank_r)

        def logits(g):
            pe.wait_ge(x32_ready.sem, x32_ready.upto(g))
            pe.wait_ge(xa_done.sem, xa_done.upto(g, NB))
            for t in range(NB):
                last = nc.tensor.matmul(bank_p[:, t * E1:(t + 1) * E1], x32[:, t * T:(t + 1) * T], col("wg"),
                                        start=True, stop=True)
            last.then_inc(l_made.sem, 1)

        def turn_gates(g):
            pe.wait_ge(norm2.low.sem, norm2.low.upto(g))
            router.tensor_turn(nc, pe, g, bank_r)

        def ahead(g, i, plan):
            if i == plan["turn"]:
                turn_tokens(g)
            if i == plan["k"]:
                keys(g)
            if i == plan["q"]:
                queries(g)
            if i == plan["v"]:
                values(g)
            if i == plan["s"]:
                scores(g)
            if i == plan["pturn"]:
                turn_weights(g)
            if i == plan["o"]:
                attend(g)
            if i == plan["turn2"]:
                turn_tokens2(g)
            if i == plan["wg"]:
                logits(g)
            if i == plan["gturn"]:
                turn_gates(g)

        return ahead


FPLAN = {"turn": 0, "high": 0, "low": 0, "enc0": 2, "enc1": 4, "tanh0": 4, "tanh1": 4, "spikes0": 3, "spikes1": 3,
         "s2c": 6, "input": 7, "input_low": 7, "wr": 8, "logits": 8, "exp": 10, "ranks": 7, "gates": 12,
         "turn_gates": 14, "keep": 15, "out_high": 5, "out_low": 5, "m0": 9, "m_tanh0": 9, "m_spikes0": 10, "m1": 11,
         "m_tanh1": 11, "m_spikes1": 11, "decode": 14, "decoded": 14, "stats": 1, "scale": 9, "scale2": 9,
         "residual": 13}


def layer0_ffn(nc, f0, a1, x, cc, ident, tg, stats, mv, work, xn, xh, xl, w123, w123_d, w123_in, wl_d, ctxt_d,
               signal_of):
    with ExitStack() as ctx:
        def sb(name, shape, dt=F32):
            return ctx.enter_context(nc.sbuf_tensor("f0_" + name, shape, dt))

        def pb(name):
            return ctx.enter_context(nc.psum_tensor("f0_" + name, [128, 512], F32))

        def signal(name, per):
            return signal_of("f0_" + name, per)

        wh, wl, wf, sel_raw = f0["wh"], f0["wl"], f0["wf"], f0["sel_raw"]
        sel = sb("sel", [128, E0 * 128], F32R)
        half_b = sb("half_b", [128, 4])
        gl = sb("gl", [128, 2, D])
        te = sb("te", [128, 2, GT])
        sp = sb("sp", [128, 2, GT])
        c32 = sb("c32", [128, GT])
        cs = sb("cs", [128, 2, GT], F32R)
        gt = sb("gt", [128, 2, GT], F32R)
        r = sb("r", [EH0, 2, GT])
        hp = sb("hp", [EH0, 2, GT])
        hh = sb("hh", [EH0, 4, GT], F32R)
        hl = sb("hl", [EH0, 4, GT], F32R)
        ys = sb("ys", [128, GT], F32R)
        tm = sb("tm", [128, 2, GT])
        sm = sb("sm", [128, 2, GT])
        dec = sb("dec", [T, NB, D])
        dn = sb("dn", [T, NB, D])
        stats2 = sb("stats2", [128, NB, 6])
        mv2 = sb("mv2", [128, NB, 2])
        work2 = sb("work2", [128, 3, NB])

        def split(name, i, n=128, rows=128):
            a = WS[name][0] + i * n
            return wh[0:rows, a:a + n], wl[0:rows, a:a + n]

        def col(name, i=0, n=None, rows=128):
            a, b = WF[name]
            a, b = (a, b) if n is None else (a + i * n, a + (i + 1) * n)
            return wf[0:rows, a:b]

        bank_a = [a1.bank_p, a1.bank_r]
        bank_z = [pb("z0"), pb("z1")]
        bank_g = [pb("g0"), pb("g1")]
        bank_y = pb("y")
        bank_c = pb("c")

        norm = Norm(signal, "norm", lambda g, t: x[:, g * NB + t, :], stats, mv, work, xn, ident)
        scaled = signal("scaled", 2)
        norm2 = Norm(signal, "norm2", lambda g, t: dec[:, t, :], stats2, mv2, work2, dn, ident, turns=False)
        router = Router(signal, "router", sb, K0, cc("tri"), ident, 0)
        zeroed = signal("zeroed", 2)
        sel_ready = signal("sel_ready", 1)
        biases = signal("biases", 3)
        enc_made = signal("enc_made", 2)
        enc_tanh = signal("enc_tanh", 2)
        spikes = signal("spikes", 2)
        c_made = signal("c_made", 1)
        c_full = signal("c_full", 1)
        c_high = signal("c_high", 1)
        c_ready = signal("c_ready", 1)
        l_made = signal("l_made", 1)
        z_made = signal("z_made", E0)
        g_made = signal("g_made", E0)
        r_ready = signal("r_ready", E0)
        hp_ready = signal("hp_ready", E0)
        hh_ready = signal("hh_ready", E0)
        hl_ready = signal("hl_ready", E0)
        y_made = signal("y_made", E0)
        ys_high = signal("ys_high", 1)
        ys_ready = signal("ys_ready", 1)
        m_made = signal("m_made", 2)
        m_tanh = signal("m_tanh", 2)
        m_spikes = signal("m_spikes", 2)
        d_made = signal("d_made", 1)
        d_ready = signal("d_ready", 1)
        x_done = signal("x_done", 1)

        def before(e, by):
            return (0, e - by) if e >= by else (1, e - by + E0)

        with nc.Block() as block:

            @block.sync
            def _(sp_):
                sp_.dma_start(a1.wl[:, :], wl_d).then_inc(a1.w_in.sem, 16)
                sp_.dma_start(a1.ctxt[:, :], ctxt_d[:, 0:GS]).then_inc(a1.ctx_in.sem, 16)
                sp_.dma_start(w123[:, :], w123_d[:, 0:W1C]).then_inc(a1.w1_in.sem, 16)
                sp_.dma_start(f0["ws"][:, :], w123_d[:, W1C:2 * W1C]).then_inc(w123_in, 16)
                sp_.wait_ge(a1.w1_low.sem, a1.w1_low.upto(0))
                sp_.dma_start(w123[:, :], w123_d[:, 2 * W1C:3 * W1C]).then_inc(a1.w3_in.sem, 16)

            @block.gpsimd
            def _(pool):
                def low(g, e):
                    pool.wait_ge(hh_ready.sem, hh_ready.upto(g, e + 1))
                    back, v = before(e, 4)
                    if y_made.comes(g, v + 1, back=back):
                        pool.wait_ge(y_made.sem, y_made.upto(g, v + 1, back=back))
                    nc.gpsimd.tensor_tensor(hl[:, e % 4, :], hp[:, e % 2, :], hh[:, e % 4, :].bitcast(F32),
                                            ALU.subtract).then_inc(hl_ready.sem, 1)

                def scale(g, i):
                    if i:
                        pool.wait_ge(scaled.sem, scaled.upto(g, 1))
                    else:
                        pool.wait_ge(norm2.rows.sem, norm2.rows.upto(g))
                    nc.gpsimd.tensor_tensor(dn[:, :, :], dn[:, :, :],
                                            gl[:, i:i + 1, :].to_broadcast([128, NB, D]),
                                            ALU.add if i else ALU.mult).then_inc(scaled.sem, 1)

                prepare, ahead1 = a1.gpsimd(nc, pool)

                def others(g, i, behind, more):
                    if not more:
                        ahead1(0, i, TPLAN)
                    if more and i == FPLAN["ranks"]:
                        router.gpsimd_ranks(nc, pool, g + 1)
                    if behind >= 2 and i == FPLAN["scale"]:
                        scale(g - 2, 0)
                    if behind >= 2 and i == FPLAN["scale2"]:
                        scale(g - 2, 1)

                def group(g, behind, more):
                    for e in range(E0):
                        low(g, e)
                        others(g, 2 * e, behind, more)
                        others(g, 2 * e + 1, behind, more)

                nc.gpsimd.memset(sel[:, :].bitcast(F32), 0.0).then_inc(zeroed.sem, 1)
                nc.gpsimd.memset(gt[:, :, :].bitcast(F32), 0.0).then_inc(zeroed.sem, 1)
                router.gpsimd_ranks(nc, pool, 0)
                group(0, 0, True)
                group(1, 1, True)
                with pool.Fori(2, G - 1) as g:
                    group(g, 2, True)
                prepare()
                group(G - 1, 2, False)
                for i in range(2):
                    n = slice(i * W1C // 2, (i + 1) * W1C // 2)
                    pool.wait_ge(a1.w1_high.sem, a1.w1_high.upto(0, i + 1))
                    nc.gpsimd.tensor_tensor(a1.w1l[:, n], w123[:, n], a1.w1h[:, n].bitcast(F32), ALU.subtract)\
                        .then_inc(a1.w1_low.sem, 1)
                for n, (g, i) in enumerate(((G - 2, 0), (G - 2, 1), (G - 1, 0), (G - 1, 1))):
                    ahead1(0, 2 * E0 + 2 * n, TPLAN)
                    ahead1(0, 2 * E0 + 2 * n + 1, TPLAN)
                    scale(g, i)
                for n in range(8, 16):
                    ahead1(0, 2 * E0 + n, TPLAN)

            @block.scalar
            def _(act):
                act.wait_ge(zeroed.sem, zeroed.upto(0))
                nc.scalar.copy(sel[0:2 * E0, :], sel_raw[:, :]).then_inc(sel_ready.sem, 1)

                def enc_tanh_(g, i):
                    act.wait_ge(enc_made.sem, enc_made.upto(g, i + 1))
                    if spikes.comes(g, i + 1, back=1):
                        act.wait_ge(spikes.sem, spikes.upto(g, i + 1, back=1))
                    nc.scalar.activation(te[:, i, :], bank_a[1 - i][:, :], ACT.Tanh, bias=half_b[:, i:i + 1],
                                         scale=0.5).then_inc(enc_tanh.sem, 1)

                def input_parts(g):
                    act.wait_ge(c_made.sem, c_made.upto(g))
                    if l_made.comes(g, back=1):
                        act.wait_ge(l_made.sem, l_made.upto(g, back=1))
                    if c_ready.comes(g, back=1):
                        act.wait_ge(c_ready.sem, c_ready.upto(g, back=1))
                    nc.scalar.activation(c32[:, :], bank_a[1][:, :], ACT.Identity, bias=col("b_s2c"))\
                        .then_inc(c_full.sem, 1)
                    if z_made.comes(g, back=2):
                        act.wait_ge(z_made.sem, z_made.upto(g, back=2))
                    nc.scalar.activation(cs[:, bass.ds(g % 2, 1), :], bank_a[1].rearrange("p (o n) -> p o n", o=1),
                                         ACT.Identity, bias=col("b_s2c")).then_inc(c_high.sem, 1)

                def keep_gates(g):
                    if y_made.comes(g, back=2):
                        act.wait_ge(y_made.sem, y_made.upto(g, back=2))
                    router.scalar_keep(nc, act, g, bank_a[1], gt[0:2 * E0, bass.ds(g % 2, 1), :].rearrange("p o n -> p (o n)"))

                def relu(g, e):
                    act.wait_ge(z_made.sem, z_made.upto(g, e + 1))
                    back, v = before(e, 2)
                    if hp_ready.comes(g, v + 1, back=back):
                        act.wait_ge(hp_ready.sem, hp_ready.upto(g, v + 1, back=back))
                    nc.scalar.activation(r[:, e % 2, :], bank_z[e % 2][:, :], ACT.Relu, bias=col("b1", e, 1))\
                        .then_inc(r_ready.sem, 1)

                def high(g, e):
                    act.wait_ge(hp_ready.sem, hp_ready.upto(g, e + 1))
                    back, v = before(e, 4)
                    if y_made.comes(g, v + 1, back=back):
                        act.wait_ge(y_made.sem, y_made.upto(g, v + 1, back=back))
                    nc.scalar.copy(hh[:, e % 4, :], hp[:, e % 2, :]).then_inc(hh_ready.sem, 1)

                def out_high(g):
                    act.wait_ge(y_made.sem, y_made.upto(g))
                    if m_made.comes(g, back=1):
                        act.wait_ge(m_made.sem, m_made.upto(g, back=1))
                    nc.scalar.copy(ys[:, :], bank_y[:, :]).then_inc(ys_high.sem, 1)

                def m_tanh_(g, i):
                    act.wait_ge(m_made.sem, m_made.upto(g, i + 1))
                    if m_spikes.comes(g, i + 1, back=1):
                        act.wait_ge(m_spikes.sem, m_spikes.upto(g, i + 1, back=1))
                    nc.scalar.activation(tm[:, i, :], bank_c[:, :], ACT.Tanh, bias=half_b[:, 2 + i:3 + i],
                                         scale=0.5).then_inc(m_tanh.sem, 1)

                prepare, ahead1 = a1.scalar(nc, act)

                def others(g, i, behind, more):
                    if not more:
                        if i == TPLAN["high"]:
                            act.wait_ge(enc_made.sem, enc_made.upto(G - 1))
                        ahead1(0, i, TPLAN)
                        if i in (TPLAN["w1a"], TPLAN["w1b"]):
                            n = slice(0, W1C // 2) if i == TPLAN["w1a"] else slice(W1C // 2, W1C)
                            act.wait_ge(a1.w1_in.sem, a1.w1_in.upto(0))
                            nc.scalar.copy(a1.w1h[:, n], w123[:, n]).then_inc(a1.w1_high.sem, 1)
                    if behind >= 1 and i == FPLAN["out_high"]:
                        out_high(g - 1)
                    if behind >= 1 and i == FPLAN["m_tanh0"]:
                        m_tanh_(g - 1, 0)
                    if behind >= 1 and i == FPLAN["m_tanh1"]:
                        m_tanh_(g - 1, 1)
                    if not more:
                        return
                    if i == FPLAN["high"]:
                        norm.scalar_high(nc, act, g + 1, bank_a[0], xh[:, :])
                    if i == FPLAN["tanh0"]:
                        enc_tanh_(g + 1, 0)
                    if i == FPLAN["tanh1"]:
                        enc_tanh_(g + 1, 1)
                    if i == FPLAN["input"]:
                        input_parts(g + 1)
                    if i == FPLAN["exp"]:
                        router.scalar_exp(nc, act, g + 1)
                    if i == FPLAN["keep"]:
                        keep_gates(g + 1)

                def group(g, behind, more):
                    for e in range(E0):
                        relu(g, e)
                        others(g, 2 * e, behind, more)
                        if e >= 1:
                            high(g, e - 1)
                        elif behind:
                            high(g - 1, E0 - 1)
                        others(g, 2 * e + 1, behind, more)

                norm.scalar_high(nc, act, 0, bank_a[0], xh[:, :])
                act.wait_ge(biases.sem, biases.upto(0))
                enc_tanh_(0, 0)
                enc_tanh_(0, 1)
                input_parts(0)
                router.scalar_exp(nc, act, 0)
                keep_gates(0)
                group(0, 0, True)
                group(1, 1, True)
                with act.Fori(2, G - 1) as g:
                    group(g, 2, True)
                prepare()
                group(G - 1, 2, False)
                high(G - 1, E0 - 1)
                out_high(G - 1)
                ahead1(0, 16, TPLAN)
                m_tanh_(G - 1, 0)
                ahead1(0, 17, TPLAN)
                m_tanh_(G - 1, 1)
                for i in range(18, 32):
                    ahead1(0, i, TPLAN)

            @block.vector
            def _(dve):
                def encoder_spikes(g, i):
                    dve.wait_ge(enc_tanh.sem, enc_tanh.upto(g, i + 1))
                    if c_made.comes(g, back=1):
                        dve.wait_ge(c_made.sem, c_made.upto(g, back=1))
                    nc.vector.tensor_scalar(sp[:, i, :], te[:, i, :], 0.5, 0.5, ALU.mult, ALU.add)\
                        .then_inc(spikes.sem, 1)

                def input_low(g):
                    dve.wait_ge(c_full.sem, c_full.upto(g))
                    dve.wait_ge(c_high.sem, c_high.upto(g))
                    part = cs[M0:128, bass.ds(g % 2, 1), :].rearrange("p o n -> p (o n)")
                    nc.vector.tensor_tensor(part, c32[M0:128, :], part.bitcast(F32), ALU.subtract)\
                        .then_inc(c_ready.sem, 1)

                def logits(g):
                    dve.wait_ge(l_made.sem, l_made.upto(g))
                    router.vector_logits(nc, dve, g, bank_a[0], col("br"))
                    router.vector_shift(nc, dve, g)

                def gated(g, e):
                    dve.wait_ge(r_ready.sem, r_ready.upto(g, e + 1))
                    dve.wait_ge(g_made.sem, g_made.upto(g, e + 1))
                    back, v = before(e, 2)
                    if hl_ready.comes(g, v + 1, back=back):
                        dve.wait_ge(hl_ready.sem, hl_ready.upto(g, v + 1, back=back))
                    nc.vector.tensor_tensor(hp[:, e % 2, :], bank_g[e % 2][:, :], r[:, e % 2, :], ALU.mult)\
                        .then_inc(hp_ready.sem, 1)

                def out_low(g):
                    dve.wait_ge(ys_high.sem, ys_high.upto(g))
                    nc.vector.tensor_tensor(ys[M0:128, :], bank_y[M0:128, :], ys[M0:128, :].bitcast(F32), ALU.subtract)\
                        .then_inc(ys_ready.sem, 1)

                def moe_spikes(g, i):
                    dve.wait_ge(m_tanh.sem, m_tanh.upto(g, i + 1))
                    if d_made.comes(g, back=1):
                        dve.wait_ge(d_made.sem, d_made.upto(g, back=1))
                    nc.vector.tensor_scalar(sm[:, i, :], tm[:, i, :], 0.5, 0.5, ALU.mult, ALU.add)\
                        .then_inc(m_spikes.sem, 1)

                def decoded(g):
                    dve.wait_ge(d_made.sem, d_made.upto(g))
                    if norm2.rows.comes(g, back=1):
                        dve.wait_ge(norm2.rows.sem, norm2.rows.upto(g, back=1))
                    nc.vector.tensor_tensor(dec[:, :, :], bank_c.rearrange("p (t d) -> p t d", t=NB),
                                            col("b_dec").rearrange("p (o d) -> p o d", o=1).to_broadcast([128, NB, D]),
                                            ALU.add).then_inc(d_ready.sem, 1)

                def residual(g):
                    dve.wait_ge(scaled.sem, scaled.upto(g))
                    xg = x[:, bass.ds(g * NB, NB), :]
                    nc.vector.tensor_tensor(xg, xg, dn[:, :, :], ALU.add).then_inc(x_done.sem, 1)

                prepare, ahead1 = a1.vector(nc, dve)

                def others(g, i, behind, more, more2):
                    if not more:
                        if i == TPLAN["rows"]:
                            dve.wait_ge(norm.turned.sem, norm.turned.upto(G - 1))
                        if i == TPLAN["low"]:
                            dve.wait_ge(enc_made.sem, enc_made.upto(G - 1))
                        ahead1(0, i, TPLAN)
                    if behind >= 1 and i == FPLAN["out_low"]:
                        out_low(g - 1)
                    if more and i == FPLAN["low"]:
                        norm.vector_low(nc, dve, g + 1, bank_a[0], xh[:, :], xl[:, :])
                    if more and i == FPLAN["spikes0"]:
                        encoder_spikes(g + 1, 0)
                    if more and i == FPLAN["spikes1"]:
                        encoder_spikes(g + 1, 1)
                    if more and i == FPLAN["input_low"]:
                        input_low(g + 1)
                    if more and i == FPLAN["logits"]:
                        logits(g + 1)
                    if behind >= 1 and i == FPLAN["m_spikes0"]:
                        moe_spikes(g - 1, 0)
                    if more and i == FPLAN["gates"]:
                        router.vector_gates(nc, dve, g + 1)
                        router.vector_gates2(nc, dve, g + 1)
                    if behind >= 1 and i == FPLAN["m_spikes1"]:
                        moe_spikes(g - 1, 1)
                    if behind >= 1 and i == FPLAN["decoded"]:
                        decoded(g - 1)
                    if behind >= 2 and i == FPLAN["residual"]:
                        residual(g - 2)
                    k = i - FPLAN["stats"]
                    if k == 0:
                        if behind >= 2:
                            dve.wait_ge(d_ready.sem, d_ready.upto(g - 2))
                            norm2.vector_stats(nc, dve, g - 2)
                        if more2:
                            norm.vector_stats(nc, dve, g + 2)
                        if behind >= 2:
                            norm2.vector_moments(nc, dve, g - 2)
                        if more2:
                            norm.vector_moments(nc, dve, g + 2)
                    if 1 <= k <= STEPS // 2:
                        for j in (2 * k - 2, 2 * k - 1):
                            if behind >= 2:
                                norm2.vector_step(nc, dve, g - 2, j)
                            if more2:
                                norm.vector_step(nc, dve, g + 2, j)
                    if behind >= 2 and k == STEPS // 2 + 1:
                        norm2.vector_rows(nc, dve, g - 2)
                    if more2 and k == STEPS // 2 + 2:
                        norm.vector_rows(nc, dve, g + 2)

                def group(g, behind, more, more2):
                    for e in range(E0):
                        gated(g, e)
                        others(g, 2 * e, behind, more, more2)
                        others(g, 2 * e + 1, behind, more, more2)

                nc.vector.tensor_scalar(half_b[:, 0:2], col("b_enc"), 0.5, None, ALU.mult).then_inc(biases.sem, 1)
                nc.vector.tensor_scalar(half_b[:, 2:4], col("b_c2s"), 0.5, None, ALU.mult).then_inc(biases.sem, 1)
                a, b = WF["ln_g"][0], WF["ln_b"][1]
                nc.vector.tensor_scalar(gl.rearrange("p a d -> p (a d)"), wf[:, a:b], tg[:, 2:3], None, ALU.mult)\
                    .then_inc(biases.sem, 1)
                norm.vector_stats(nc, dve, 0)
                norm.vector_moments(nc, dve, 0)
                norm.vector_scale(nc, dve, 0)
                norm.vector_rows(nc, dve, 0)
                norm.vector_low(nc, dve, 0, bank_a[0], xh[:, :], xl[:, :])
                norm.vector_stats(nc, dve, 1)
                norm.vector_moments(nc, dve, 1)
                norm.vector_scale(nc, dve, 1)
                encoder_spikes(0, 0)
                encoder_spikes(0, 1)
                norm.vector_rows(nc, dve, 1)
                input_low(0)
                logits(0)
                router.vector_gates(nc, dve, 0)
                router.vector_gates2(nc, dve, 0)
                group(0, 0, True, True)
                group(1, 1, True, True)
                with dve.Fori(2, G - 2) as g:
                    group(g, 2, True, True)
                group(G - 2, 2, True, False)
                prepare()
                group(G - 1, 2, False, False)

                out_low(G - 1)
                dve.wait_ge(d_ready.sem, d_ready.upto(G - 2))
                norm2.vector_stats(nc, dve, G - 2)
                norm2.vector_moments(nc, dve, G - 2)
                for i in range(STEPS):
                    norm2.vector_step(nc, dve, G - 2, i)
                    if i == STEPS // 3:
                        moe_spikes(G - 1, 0)
                        ahead1(0, 16, TPLAN)
                norm2.vector_rows(nc, dve, G - 2)
                ahead1(0, 17, TPLAN)
                moe_spikes(G - 1, 1)
                ahead1(0, 18, TPLAN)
                decoded(G - 1)
                ahead1(0, 19, TPLAN)
                ahead1(0, 20, TPLAN)
                dve.wait_ge(d_ready.sem, d_ready.upto(G - 1))
                norm2.vector_stats(nc, dve, G - 1)
                norm2.vector_moments(nc, dve, G - 1)
                norm2.vector_scale(nc, dve, G - 1)
                residual(G - 2)
                dve.wait_ge(x_done.sem, x_done.upto(G - 2))
                norm2.vector_rows(nc, dve, G - 1)
                ahead1(0, 21, TPLAN)
                ahead1(0, 22, TPLAN)
                residual(G - 1)
                for i in range(23, 32):
                    ahead1(0, i, TPLAN)

            @block.tensor
            def _(pe):
                def turn_tokens(g):
                    if router.logits.comes(g, back=1):
                        pe.wait_ge(router.logits.sem, router.logits.upto(g, back=1))
                    norm.tensor_turn(nc, pe, g, bank_a[0])

                def encode(g, i):
                    pe.wait_ge(norm.low.sem, norm.low.upto(g))
                    if i == 0:
                        if router.ready.comes(g, back=1):
                            pe.wait_ge(router.ready.sem, router.ready.upto(g, back=1))
                    wide = split("enc", i)
                    split_product(nc, bank_a[1 - i][:, :], *wide, xh[:, :], xl[:, :], True, True)\
                        .then_inc(enc_made.sem, 1)

                def experts_input(g):
                    for i in range(2):
                        pe.wait_ge(spikes.sem, spikes.upto(g, i + 1))
                        last = nc.tensor.matmul(bank_a[1][:, :], col("s2c", i, 128), sp[:, i, :], start=i == 0,
                                                stop=i == 1)
                    last.then_inc(c_made.sem, 1)

                def make_logits(g):
                    pe.wait_ge(enc_tanh.sem, enc_tanh.upto(g))
                    pe.wait_ge(c_full.sem, c_full.upto(g))
                    for t in range(NB):
                        last = nc.tensor.matmul(bank_a[0][:, t * E0:(t + 1) * E0], c32[0:M0, t * T:(t + 1) * T],
                                                col("wr", rows=M0), start=True, stop=True)
                    last.then_inc(l_made.sem, 1)

                def turn_gates(g):
                    pe.wait_ge(c_high.sem, c_high.upto(g))
                    router.tensor_turn(nc, pe, g, bank_a[1])

                def hidden(g, e):
                    pe.wait_ge(c_ready.sem, c_ready.upto(g))
                    back, v = before(e, 2)
                    if r_ready.comes(g, v + 1, back=back):
                        pe.wait_ge(r_ready.sem, r_ready.upto(g, v + 1, back=back))
                    high_, low_ = split("w1", e)
                    both = cs[:, bass.ds(g % 2, 1), :].rearrange("p o n -> p (o n)")
                    nc.tensor.matmul(bank_z[e % 2][:, :], low_, both, start=True, stop=False)
                    nc.tensor.matmul(bank_z[e % 2][:, :], high_, both, start=False, stop=True).then_inc(z_made.sem, 1)

                def gates_of(g):
                    return gt[:, bass.ds(g % 2, 1), :].rearrange("p o n -> p (o n)")

                def spread_gate(g, e):
                    pe.wait_ge(router.ready.sem, router.ready.upto(g))
                    back, v = before(e, 2)
                    if hp_ready.comes(g, v + 1, back=back):
                        pe.wait_ge(hp_ready.sem, hp_ready.upto(g, v + 1, back=back))
                    nc.tensor.matmul(bank_g[e % 2][:, :], sel[:, e * 128:(e + 1) * 128], gates_of(g), start=True,
                                     stop=True).then_inc(g_made.sem, 1)

                def second_bias(g):
                    if ys_ready.comes(g, back=1):
                        pe.wait_ge(ys_ready.sem, ys_ready.upto(g, back=1))
                    high_, low_ = split("b2", 0)
                    nc.tensor.matmul(bank_y[:, :], low_, gates_of(g), start=True, stop=False)
                    nc.tensor.matmul(bank_y[:, :], high_, gates_of(g), start=False, stop=False)

                def output(g, e):
                    if e == 0:
                        second_bias(g)
                    pe.wait_ge(hh_ready.sem, hh_ready.upto(g, e + 1))
                    pe.wait_ge(hl_ready.sem, hl_ready.upto(g, e + 1))
                    split_product(nc, bank_y[:, :], *split("w2", e), hh[:, e % 4, :], hl[:, e % 4, :], False, e == E0 - 1)\
                        .then_inc(y_made.sem, 1)

                def to_spikes(g, i):
                    pe.wait_ge(ys_ready.sem, ys_ready.upto(g))
                    if i:
                        pe.wait_ge(m_tanh.sem, m_tanh.upto(g, 1))
                    else:
                        if d_ready.comes(g, back=1):
                            pe.wait_ge(d_ready.sem, d_ready.upto(g, back=1))
                    high_, low_ = split("c2s", i)
                    nc.tensor.matmul(bank_c[:, :], low_, ys[:, :], start=True, stop=False)
                    nc.tensor.matmul(bank_c[:, :], high_, ys[:, :], start=False, stop=True).then_inc(m_made.sem, 1)

                def decode(g):
                    pe.wait_ge(m_spikes.sem, m_spikes.upto(g))
                    for t in range(NB):
                        for i in range(2):
                            last = nc.tensor.matmul(bank_c[:, t * D:(t + 1) * D], sm[:, i, t * T:(t + 1) * T],
                                                    col("dec", i, D), start=i == 0, stop=i == 1)
                    last.then_inc(d_made.sem, 1)

                ahead1 = a1.tensor(nc, pe)

                def others(g, i, behind, more):
                    if not more:
                        if i == TPLAN["turn"]:
                            pe.wait_ge(router.logits.sem, router.logits.upto(G - 1))
                        if i == TPLAN["k"]:
                            pe.wait_ge(router.ready.sem, router.ready.upto(G - 1))
                        ahead1(0, i, TPLAN)
                    if behind >= 1 and i == FPLAN["m0"]:
                        to_spikes(g - 1, 0)
                    if behind >= 1 and i == FPLAN["m1"]:
                        to_spikes(g - 1, 1)
                    if behind >= 1 and i == FPLAN["decode"]:
                        decode(g - 1)
                    if not more:
                        return
                    if i == FPLAN["turn"]:
                        turn_tokens(g + 1)
                    if i == FPLAN["enc0"]:
                        encode(g + 1, 0)
                    if i == FPLAN["enc1"]:
                        encode(g + 1, 1)
                    if i == FPLAN["s2c"]:
                        experts_input(g + 1)
                    if i == FPLAN["wr"]:
                        make_logits(g + 1)
                    if i == FPLAN["turn_gates"]:
                        turn_gates(g + 1)

                def group(g, behind, more):
                    for e in range(E0):
                        hidden(g, e)
                        spread_gate(g, e)
                        others(g, 2 * e, behind, more)
                        if e >= 3:
                            output(g, e - 3)
                        elif behind:
                            output(g - 1, e - 3 + E0)
                        others(g, 2 * e + 1, behind, more)

                turn_tokens(0)
                encode(0, 0)
                encode(0, 1)
                experts_input(0)
                make_logits(0)
                turn_gates(0)
                pe.wait_ge(sel_ready.sem, sel_ready.upto(0))
                group(0, 0, True)
                group(1, 1, True)
                with pe.Fori(2, G - 1) as g:
                    group(g, 2, True)
                pe.wait_ge(a1.w_low.sem, a1.w_low.upto(0))
                group(G - 1, 2, False)
                for e in range(E0 - 3, E0):
                    output(G - 1, e)
                ahead1(0, 16, TPLAN)
                to_spikes(G - 1, 0)
                ahead1(0, 17, TPLAN)
                to_spikes(G - 1, 1)
                ahead1(0, 18, TPLAN)
                decode(G - 1)
                for i in range(19, 32):
                    ahead1(0, i, TPLAN)


def layer1(nc, f0, a1, x, ident, tg, ctxt, w123, w123_d, ctxt_d, sel1_d, out_d, w123_in, signal_of):
    LAG = 3
    with ExitStack() as ctx:
        def sb(name, shape, dt=F32):
            return ctx.enter_context(nc.sbuf_tensor("l1_" + name, shape, dt))

        def pb(name):
            return ctx.enter_context(nc.psum_tensor("l1_" + name, [128, 512], F32))

        def signal(name, per):
            return signal_of("l1_" + name, per)

        wh = [a1.w1h, sb("w2h", [128, W1C], F32R), f0["wh"]]
        wlo = [a1.w1l, sb("w2l", [128, W1C], F32R), f0["wl"]]
        came_to = [w123, f0["ws"], w123]
        xh1, xl1, gt1, of_parity = a1.xh1, a1.xl1, a1.gt1, a1.of_parity
        bank_p, bank_r, norm2, router = a1.bank_p, a1.bank_r, a1.norm2, a1.router
        w3_in, w1_low, zeroed = a1.w3_in, a1.w1_low, a1.zeroed
        ctx_in, k_made, v_made, h2_made, g_made, x_done = a1.ctx_in, a1.k_made, a1.v_made, a1.h2_made, a1.g_made, a1.x_done
        n1 = 2 * (E1 + 1)
        sel = sb("sel", [128, W1C], F32R)
        si, ab, ag = (f0["ws"][:, 2 * i * GT:2 * (i + 1) * GT].rearrange("p (a n) -> p a n", a=2) for i in range(3))
        ah = sb("ah", [128, 4, GT], F32R)
        al = sb("al", [128, 4, GT], F32R)
        od = w123[:, 0:GT]

        bank_1 = [pb("h10"), pb("h11")]
        bank_2 = [pb("h20"), pb("h21")]
        bank_g = pb("g")
        bank_d = pb("d")

        part_high = signal("part_high", 1)
        part_low_v = signal("part_low_v", 1)
        part_low_p = signal("part_low_p", 1)
        sel_in = signal("sel_in", 16)
        h1_made = signal("h1_made", CH)
        si_ready = signal("si_ready", CH)
        ab_ready = signal("ab_ready", CH)
        ag_ready = signal("ag_ready", CH)
        ah_ready = signal("ah_ready", CH)
        al_ready = signal("al_ready", CH)
        d_made = signal("d_made", CH)
        od_ready = signal("od_ready", 1)
        od_turned = signal("od_turned", 1)
        stored = signal("stored", 16)

        def before(c, by):
            return (0, c - by) if c >= by else (1, c - by + CH)

        def weight(which, c):
            return wh[which][:, c * 128:(c + 1) * 128], wlo[which][:, c * 128:(c + 1) * 128]

        def part(tiles, i):
            return tiles[1 + i // 2][:, i % 2 * W1C // 2:(i % 2 + 1) * W1C // 2]

        with nc.Block() as block:

            @block.sync
            def _(sp):
                def load(g):
                    if k_made.comes(g, back=1):
                        sp.wait_ge(k_made.sem, k_made.upto(g, back=1))
                    if v_made.comes(g, back=1):
                        sp.wait_ge(v_made.sem, v_made.upto(g, back=1))
                    sp.dma_start(ctxt[:, :], ctxt_d[:, bass.ds(g * GS, GS)]).then_inc(ctx_in.sem, 16)

                def store(g):
                    sp.wait_ge(x_done.sem, x_done.upto(g))
                    sp.dma_start(out_d[bass.ds(g * NB, NB)].rearrange("b t d -> t b d"),
                                 x[:, bass.ds(g * NB, NB), :]).then_inc(stored.sem, 16)

                load(1)
                with sp.Fori(1, G - 1) as g:
                    load(g + 1)
                    store(g - 1)
                store(G - 2)
                store(G - 1)
                sp.wait_ge(stored.sem, 16 * G)

            @block.gpsimd
            def _(pool):
                _, ahead = a1.gpsimd(nc, pool)

                def low(g, c):
                    pool.wait_ge(ah_ready.sem, ah_ready.upto(g, c + 1))
                    nc.gpsimd.tensor_tensor(al[:, c % 4, :], ag[:, c % 2, :], ah[:, c % 4, :].bitcast(F32),
                                            ALU.subtract).then_inc(al_ready.sem, 1)

                def group(g, more):
                    for c in range(CH):
                        low(g, c)
                        if more:
                            ahead(g + 1, 2 * c, LPLAN)
                            ahead(g + 1, 2 * c + 1, LPLAN)

                nc.gpsimd.memset(sel[:, :].bitcast(F32), 0.0).then_inc(zeroed.sem, 1)
                pool.wait_ge(zeroed.sem, zeroed.upto(0))
                pool.dma_start(sel[0:n1, :], sel1_d.bitcast(F32R)).then_inc(sel_in.sem, 16)
                pool.wait_ge(part_high.sem, part_high.upto(3))
                nc.gpsimd.tensor_tensor(part(wlo, 3), part(came_to, 3), part(wh, 3).bitcast(F32), ALU.subtract)\
                    .then_inc(part_low_p.sem, 1)
                with pool.Fori(0, G - 1) as g:
                    group(g, True)
                group(G - 1, False)

            @block.scalar
            def _(act):
                _, ahead = a1.scalar(nc, act)

                def weights_high(i):
                    if i == 0:
                        act.wait_ge(w123_in, 16)
                    if i == 2:
                        act.wait_ge(w3_in.sem, w3_in.upto(0))
                    nc.scalar.copy(part(wh, i), part(came_to, i)).then_inc(part_high.sem, 1)

                def silu(g, c, first):
                    if first and c == 0:
                        act.wait_ge(part_low_v.sem, part_low_v.upto(1))
                    act.wait_ge(h1_made.sem, h1_made.upto(g, c + 1))
                    back, v = before(c, 2)
                    if not (first and back):
                        if ab_ready.comes(g, v + 1, back=back):
                            act.wait_ge(ab_ready.sem, ab_ready.upto(g, v + 1, back=back))
                    nc.scalar.activation(si[:, c % 2, :], bank_1[c % 2][:, :], ACT.Silu).then_inc(si_ready.sem, 1)

                def high(g, c, first):
                    act.wait_ge(ag_ready.sem, ag_ready.upto(g, c + 1))
                    back, v = before(c, 4)
                    if not (first and back):
                        if d_made.comes(g, v + 1, back=back):
                            act.wait_ge(d_made.sem, d_made.upto(g, v + 1, back=back))
                    nc.scalar.copy(ah[:, c % 4, :], ag[:, c % 2, :]).then_inc(ah_ready.sem, 1)

                def output(g):
                    act.wait_ge(d_made.sem, d_made.upto(g))
                    nc.scalar.copy(od[:, :], bank_d[:, :]).then_inc(od_ready.sem, 1)

                def group(g, first, more):
                    for c in range(CH):
                        silu(g, c, first)
                        if more:
                            ahead(g + 1, 2 * c, LPLAN)
                        if c >= 1:
                            high(g, c - 1, first)
                        elif not first:
                            high(g - 1, CH - 1, False)
                        if c == LAG and not first:
                            output(g - 1)
                        if more:
                            ahead(g + 1, 2 * c + 1, LPLAN)

                for i in range(4):
                    weights_high(i)
                group(0, True, True)
                with act.Fori(1, G - 1) as g:
                    group(g, False, True)
                group(G - 1, False, False)
                high(G - 1, CH - 1, False)
                output(G - 1)

            @block.vector
            def _(dve):
                def product(g, c, first):
                    dve.wait_ge(si_ready.sem, si_ready.upto(g, c + 1))
                    dve.wait_ge(h2_made.sem, h2_made.upto(g, c + 1))
                    back, v = before(c, 2)
                    if not (first and back):
                        if ag_ready.comes(g, v + 1, back=back):
                            dve.wait_ge(ag_ready.sem, ag_ready.upto(g, v + 1, back=back))
                    nc.vector.tensor_tensor(ab[:, c % 2, :], bank_2[c % 2][:, :], si[:, c % 2, :], ALU.mult)\
                        .then_inc(ab_ready.sem, 1)

                def gated(g, c, first):
                    dve.wait_ge(g_made.sem, g_made.upto(g, c + 1))
                    dve.wait_ge(ab_ready.sem, ab_ready.upto(g, c + 1))
                    back, v = before(c, 2)
                    if not (first and back):
                        if al_ready.comes(g, v + 1, back=back):
                            dve.wait_ge(al_ready.sem, al_ready.upto(g, v + 1, back=back))
                    nc.vector.tensor_tensor(ag[:, c % 2, :], bank_g[:, :], ab[:, c % 2, :], ALU.mult)\
                        .then_inc(ag_ready.sem, 1)

                def add_output(g):
                    dve.wait_ge(od_turned.sem, od_turned.upto(g))
                    xg = x[:, bass.ds(g * NB, NB), :]
                    nc.vector.scalar_tensor_tensor(out=xg, in0=bank_p.rearrange("t (b d) -> t b d", b=NB),
                                                   scalar=tg[:, 3:4], in1=xg, op0=ALU.mult, op1=ALU.add)\
                        .then_inc(x_done.sem, 1)

                _, ahead = a1.vector(nc, dve)

                def weights_low(i):
                    dve.wait_ge(part_high.sem, part_high.upto(i))
                    nc.vector.tensor_tensor(part(wlo, i), part(came_to, i), part(wh, i).bitcast(F32), ALU.subtract)\
                        .then_inc(part_low_v.sem, 1)

                def group(g, first, more):
                    for c in range(CH):
                        product(g, c, first)
                        if more:
                            ahead(g + 1, 2 * c, LPLAN)
                        gated(g, c, first)
                        if c == LAG + 2 and not first:
                            add_output(g - 1)
                        if more:
                            ahead(g + 1, 2 * c + 1, LPLAN)

                for i in range(3):
                    weights_low(i)
                group(0, True, True)
                with dve.Fori(1, G - 1) as g:
                    group(g, False, True)
                group(G - 1, False, False)
                add_output(G - 1)

            @block.tensor
            def _(pe):
                ahead = a1.tensor(nc, pe)

                def up(g, c, first):
                    if c == 0:
                        pe.wait_ge(norm2.low.sem, norm2.low.upto(g))
                    back, v = before(c, 2)
                    for which, bank, made, read in ((0, bank_1, h1_made, si_ready), (1, bank_2, h2_made, ab_ready)):
                        if which == 1 and c == 0:
                            pe.wait_ge(part_low_v.sem, part_low_v.upto(1))
                        if not (first and back):
                            if read.comes(g, v + 1, back=back):
                                pe.wait_ge(read.sem, read.upto(g, v + 1, back=back))
                        split_product(nc, bank[c % 2][:, :], *weight(which, c), of_parity(xh1, g), of_parity(xl1, g), True, True)\
                            .then_inc(made.sem, 1)

                def spread_gate(g, c, first):
                    if c == 0:
                        pe.wait_ge(sel_in.sem, sel_in.upto(0))
                        pe.wait_ge(router.ready.sem, router.ready.upto(g))
                    back, v = before(c, 1)
                    if not (first and back):
                        if ag_ready.comes(g, v + 1, back=back):
                            pe.wait_ge(ag_ready.sem, ag_ready.upto(g, v + 1, back=back))
                    nc.tensor.matmul(bank_g[:, :], sel[:, c * 128:(c + 1) * 128], of_parity(gt1, g),
                                     start=True, stop=True).then_inc(g_made.sem, 1)

                def down(g, c):
                    if c == 0:
                        pe.wait_ge(part_low_v.sem, part_low_v.upto(2))
                        pe.wait_ge(part_low_p.sem, part_low_p.upto(0))
                        if od_ready.comes(g, back=1):
                            pe.wait_ge(od_ready.sem, od_ready.upto(g, back=1))
                    pe.wait_ge(ah_ready.sem, ah_ready.upto(g, c + 1))
                    pe.wait_ge(al_ready.sem, al_ready.upto(g, c + 1))
                    split_product(nc, bank_d[:, :], *weight(2, c), ah[:, c % 4, :], al[:, c % 4, :], c == 0, c == CH - 1)\
                        .then_inc(d_made.sem, 1)

                def turn_output(g, more):
                    pe.wait_ge(od_ready.sem, od_ready.upto(g))
                    if more:
                        pe.wait_ge(router.logits.sem, router.logits.upto(g + 1))
                    for b in range(NB):
                        last = nc.tensor.transpose(bank_p[:, b * D:(b + 1) * D], od[:, b * T:(b + 1) * T], ident)
                    last.then_inc(od_turned.sem, 1)

                def group(g, first, more):
                    for c in range(CH):
                        up(g, c, first)
                        if more:
                            ahead(g + 1, 2 * c, LPLAN)
                        if c >= LAG:
                            down(g, c - LAG)
                        elif not first:
                            down(g - 1, c - LAG + CH)
                        spread_gate(g, c, first)
                        if c == LAG + 1 and not first:
                            turn_output(g - 1, True)
                        if more:
                            ahead(g + 1, 2 * c + 1, LPLAN)

                pe.wait_ge(w1_low.sem, w1_low.upto(0))
                group(0, True, True)
                with pe.Fori(1, G - 1) as g:
                    group(g, False, True)
                group(G - 1, False, False)
                for c in range(CH - LAG, CH):
                    down(G - 1, c)
                turn_output(G - 1, False)


def _constants():
    inv_freq = (1.0 / 10000.0 ** (np.arange(0, HD, 2, dtype=np.float32) / HD)).astype(np.float32)
    freqs = np.arange(T, dtype=np.float32)[:, None] * inv_freq[None, :]
    emb = np.concatenate([freqs, freqs], axis=-1)
    cos, sin = np.cos(emb).astype(np.float32), np.sin(emb).astype(np.float32)
    sin[:, :HD // 2] *= -1.0
    cos, sin = np.tile(cos.T, (HEADS, 1)), np.tile(sin.T, (HEADS, 1))
    c = np.zeros((128, NC_COLS), np.float32)

    def put(name, value):
        a, b = CC[name]
        c[:, a:b] = value

    scale = np.float32(HD ** -0.5)
    put("ident", np.eye(128, dtype=np.float32))
    put("cosq", cos * scale)
    put("sinq", sin * scale)
    put("cosk", cos[:, :S])
    put("sink", sin[:, :S])
    put("mask", ((np.arange(128)[:, None] // HD) % NQ == np.arange(NQ)[None, :]).astype(np.float32))
    put("qmask", (np.arange(128)[:, None] // (NQ * HD) == np.arange(QUADS)[None, :]).astype(np.float32))
    put("tri", (np.arange(8)[None, :] < np.arange(8)[:, None]).astype(np.float32).reshape(1, 64))
    n0 = 2 * E0
    sel0 = np.zeros((n0, E0, 128), np.float32)
    for e in range(E0):
        sel0[e, e] = sel0[E0 + e, e] = 1.0
    n1 = E1 + 1
    sel1 = np.zeros((2 * n1, W1C), np.float32)
    for e in range(n1):
        sel1[e, e * H1:(e + 1) * H1] = sel1[n1 + e, e * H1:(e + 1) * H1] = 1.0
    return c, sel0.reshape(n0, E0 * 128), sel1


def _pack(at, total, parts, rows=128):
    out = np.zeros((rows, total), np.float32)
    for name, value in parts.items():
        a, b = at[name]
        value = np.asarray(value)
        out[:value.shape[0], a:b] = value.reshape(value.shape[0], -1)
    return out


def _layout(i):
    swap = np.arange(D).reshape(HEADS, 2, HD // 2)[:, ::-1].reshape(-1)
    wq, wkv = i["L0_xattn_Wq"], i["L0_xattn_Wkv"]
    wk, wv = wkv[:, :D], wkv[:, D:]
    const, sel0, sel1 = _constants()
    rows = lambda v: np.broadcast_to(v.reshape(1, -1), (128, v.size))
    twice = lambda a, axis: np.concatenate([a, a], axis)
    w1 = np.transpose(i["L0_ffn_W1"], (1, 0, 2)).reshape(M0, E0 * EH0)
    w2 = twice(np.transpose(i["L0_ffn_W2"], (1, 0, 2)), 2)
    ws = _pack(WS, NS_COLS, {
        "enc": i["L0_ffn_W_enc"], "w1": twice(w1, 0), "w2": w2, "c2s": twice(i["L0_ffn_W_c2s"], 0),
        "b2": twice(twice(i["L0_ffn_b2"], 1), 0)})
    wf = _pack(WF, NF_COLS, {
        "s2c": twice(i["L0_ffn_W_s2c"].reshape(2, 128, M0).transpose(1, 0, 2), 2), "wr": i["L0_ffn_Wr"],
        "dec": i["L0_ffn_W_dec"].reshape(2, 128, D).transpose(1, 0, 2), "b_enc": i["L0_ffn_b_enc"].reshape(2, 128).T,
        "b_s2c": twice(i["L0_ffn_b_s2c"], 0).reshape(128, 1), "b1": i["L0_ffn_b1"].T,
        "b_c2s": i["L0_ffn_b_c2s"].reshape(2, 128).T, "br": rows(i["L0_ffn_br"]), "b_dec": rows(i["L0_ffn_b_dec"]),
        "ln_g": rows(i["L0_ffn_ln_g"]), "ln_b": rows(i["L0_ffn_ln_b"])})
    wl = _pack(WL, NL_COLS, {
        "q": i["L1_xattn_Wq"].T, "k": i["L1_xattn_Wk"].T, "v": i["L1_xattn_Wv"].T,
        "bq": i["L1_xattn_bq"].reshape(128, 1), "bk": i["L1_xattn_bk"].reshape(128, 1), "bv": rows(i["L1_xattn_bv"]),
        "wg": i["L1_ffn_Wg"].T, "rb": rows(i["L1_ffn_routing_bias"])})
    n = (E1 + 1) * H1
    w123 = np.zeros((128, 3, W1C), np.float32)
    w123[:, 0, :n] = np.concatenate([i["L1_ffn_W1"].reshape(-1, D), i["L1_ffn_Ws1"]]).T
    w123[:, 1, :n] = np.concatenate([i["L1_ffn_W2"].reshape(-1, D), i["L1_ffn_Ws2"]]).T
    w3 = np.zeros((W1C, D), np.float32)
    w3[:n] = np.concatenate([np.transpose(i["L1_ffn_W3"], (0, 2, 1)).reshape(-1, D), i["L1_ffn_Ws3"].T])
    w123[:, 2, :] = w3.reshape(CH, 128, D).transpose(1, 0, 2).reshape(128, W1C)
    return {
        "x": i["x"], "ctxt": i["ctx_1024"].reshape(B * S, D).T, "gates": np.broadcast_to(
            np.concatenate([i["g_xattn"], i["g_ffn"]]).reshape(1, 4), (128, 4)),
        "wa": np.concatenate([wq, wq[:, swap], wk, wk[:, swap], wv, i["L0_xattn_Wo"]], 1),
        "bo": i["L0_xattn_bo"].reshape(1, D), "const": const, "ws": ws, "wf": wf, "wl": wl,
        "sel0": sel0, "sel1": sel1, "w123": w123.reshape(128, 3 * W1C)}


def kernel(**inputs):
    from concourse import bacc
    from concourse.bass_utils import run_bass_kernel_spmd

    laid_out = _layout({name: np.asarray(a) for name, a in inputs.items()})
    nc = bacc.Bacc("TRN2", target_bir_lowering=False, num_devices=1)
    arrays, args = {}, []
    for name, a in laid_out.items():
        arrays[f"in_{name}"] = np.ascontiguousarray(a)
        args.append(nc.dram_tensor(f"in_{name}", a.shape, F32, kind="ExternalInput").ap())
    args.append(nc.dram_tensor("out_x", (B, T, D), F32, kind="ExternalOutput").ap())
    build(nc, *args)
    return run_bass_kernel_spmd(nc, [arrays], core_ids=[0]).results[0]["out_x"]
```

```python
from contextlib import ExitStack

import numpy as np

import concourse.bass as bass
from concourse import mybir

B, T, S, D = 32, 128, 77, 128
NB = 4
G = B // NB
GT = NB * T
GS = NB * S
HEADS = 16
HD = D // HEADS
QUADS = HEADS // NB
NQ = 4
UNITS = NB * QUADS
VP = 3 * (HD + 1)
E0, M0, EH0, H0 = 8, 64, 128, 256
E1, K1, H1 = 8, 4, D * 2 * 4 // 3
K0 = 2
CH = -(-(E1 + 1) * H1 // 128)
W1C = CH * 128
GATED = -(-E1 * H1 // 128)
EPS = 1e-5
RSQRT_MAGIC = 0x5F3759DF
NEWTON = 3
STEPS = 3 + 3 * NEWTON

ALU = mybir.AluOpType
ACT = mybir.ActivationFunctionType
AX = mybir.AxisListType
F32 = mybir.dt.float32
F32R = mybir.dt.float32r
BF16 = mybir.dt.bfloat16
F16 = mybir.dt.float16
I32 = mybir.dt.int32

WA = {n: i * 128 for i, n in enumerate(("q", "qp", "k", "kp", "v", "o"))}
CC, _at = {}, 0
for _n, _w in (("ident", 128), ("cosq", T), ("sinq", T), ("cosk", S), ("sink", S), ("mask", NQ), ("qmask", QUADS),
               ("tri", E0 * E0)):
    CC[_n] = (_at, _at + _w)
    _at += _w
NC_COLS = _at
WS, _at = {}, 0
for _n, _w in (("enc", H0), ("w1", E0 * EH0), ("w2", E0 * 2 * M0), ("c2s", H0), ("b2", 2 * M0)):
    WS[_n] = (_at, _at + _w)
    _at += _w
NS_COLS = _at
WPARTS = 4
WF, _at = {}, 0
for _n, _w in (("s2c", 2 * 2 * M0), ("wr", E0), ("dec", 2 * D), ("b_enc", 2), ("b_s2c", 1), ("b1", E0),
               ("b_c2s", 2), ("br", E0), ("b_dec", D), ("ln_g", D), ("ln_b", D)):
    WF[_n] = (_at, _at + _w)
    _at += _w
NF_COLS = _at
WL, _at = {}, 0
for _n, _w in (("q", D), ("k", D), ("v", D), ("bq", 1), ("bk", 1), ("bv", D), ("wg", E1), ("rb", E1)):
    WL[_n] = (_at, _at + _w)
    _at += _w
NL_COLS = _at


class Signal:

    def __init__(self, sem, per):
        self.sem, self.per = sem, per

    def upto(self, g, k=None, back=0):
        return g * self.per + ((self.per if k is None else k) - back * self.per)

    def comes(self, g, k=None, back=0):
        return not isinstance(g, int) or self.upto(g, k, back) > 0


def build(nc, x_d, ctxt_d, gates_d, wa_d, bo_d, const_d, ws_d, wf_d, wl_d, sel0_d, sel1_d, w123_d, out_d):
    ctx = ExitStack()
    with ctx:
        def sb(name, shape, dt=F32):
            return ctx.enter_context(nc.sbuf_tensor(name, shape, dt))

        def signal(name, per):
            return Signal(ctx.enter_context(nc.semaphore(name)), per)

        x = sb("x", [T, B, D])
        ctxt = sb("ctxt", [D, GS])
        const = sb("const", [128, NC_COLS])
        tg = sb("tg", [128, 4])
        g_raw = sb("g_raw", [128, 4])
        stats = sb("stats", [128, NB, 6])
        mv = sb("mv", [128, NB, 2])
        work = sb("work", [128, 3, NB])
        xn = sb("xn", [128, NB, D])
        xh = sb("xh", [D, GT], F32R)
        xl = sb("xl", [D, GT], F32R)

        def cc(name):
            a, b = CC[name]
            return const[:, a:b]

        ident = cc("ident")

        w123 = sb("w123", [128, W1C])
        w123_in = ctx.enter_context(nc.semaphore("w123_in"))
        x_in = signal("x_in", 16)
        x_rest_in = signal("x_rest_in", 16)
        f0 = dict(ws=sb("ws", [128, W1C]), wh=sb("f0_wh", [128, W1C], F32R), wl=sb("f0_wl", [128, W1C], F32R),
                  wf=sb("wf", [128, NF_COLS]), sel_raw=sb("sel0_raw", [2 * E0, E0 * 128]),
                  w_in=signal("f0_w_in", 48), w_high=signal("f0_w_high", WPARTS), w_low=signal("f0_w_low", WPARTS))
        fr = Front(nc, ctx, f0, x, cc, ident, stats, mv, work, xn, xh, xl, signal)
        layer0_attention(nc, f0, fr, ws_d, wf_d, sel0_d, x, ctxt, const, cc, ident, tg, g_raw, stats, mv, work, xn, xh, xl,
                         x_d, ctxt_d, gates_d, wa_d, bo_d, const_d, x_in, x_rest_in, signal)
        banks = [ctx.enter_context(nc.psum_tensor(f"bank_{n}", [128, 512], F32)) for n in "pr"]
        a1 = Attention1(nc, ctx, x, ctxt, cc, ident, tg, stats, mv, work, xn, xh, xl, *banks, signal)
        layer0_ffn(nc, f0, fr, a1, tg, xh, xl, w123, w123_d, w123_in, wl_d, ctxt_d, signal)
        layer1(nc, f0, fr, a1, x, ident, tg, ctxt, w123, ctxt_d, sel1_d, out_d, w123_in, signal)


class Norm:

    def __init__(self, signal, name, tile, stats, mv, work, xn, ident, turns=True):
        self.tile, self.stats, self.mv, self.work, self.xn, self.ident = tile, stats, mv, work, xn, ident
        self.bn = signal(f"{name}_bn", NB + 1)
        self.newton = signal(f"{name}_newton", NB + STEPS)
        self.rows = signal(f"{name}_rows", NB)
        self.turned = signal(f"{name}_turned", 1)
        self.high = signal(f"{name}_high", 1)
        self.low = signal(f"{name}_low", 1)
        self.turns = turns

    def over(self, tile, xn):
        other = Norm(lambda name, per: None, "", tile, self.stats, self.mv, self.work, xn, self.ident, self.turns)
        other.bn, other.newton, other.rows, other.turned = self.bn, self.newton, self.rows, self.turned
        other.high, other.low = self.high, self.low
        return other

    def vector_stats(self, nc, g, tiles=range(NB)):
        for t in tiles:
            nc.vector.bn_stats(self.stats[:, t, :], self.tile(g, t)).then_inc(self.bn.sem, 1)

    def vector_moments(self, nc, dve, g):
        dve.wait_ge(self.bn.sem, self.bn.upto(g, NB))
        dve.sem_inc(self.bn.sem, 1)
        for t in range(NB):
            nc.vector.bn_aggr(self.mv[:, t, :], self.stats[:, t, :]).then_inc(self.newton.sem, 1)

    def vector_step(self, nc, dve, g, i):
        v, a, y = self.work[:, 0, :], self.work[:, 1, :], self.work[:, 2, :]
        dve.wait_ge(self.newton.sem, self.newton.upto(g, NB + i))
        if i == 0:
            step = nc.vector.tensor_scalar(v, self.mv[:, :, 1], EPS, None, ALU.add)
        elif i == 1:
            step = nc.vector.tensor_scalar(a.bitcast(I32), v.bitcast(I32), 1, None, ALU.logical_shift_right)
        elif i == 2:
            step = nc.vector.tensor_scalar(y.bitcast(I32), a.bitcast(I32), -1, RSQRT_MAGIC, ALU.mult, ALU.add)
        elif i % 3 == 0:
            step = nc.vector.tensor_tensor(a, y, y, ALU.mult)
        elif i % 3 == 1:
            step = nc.vector.scalar_tensor_tensor(out=a, in0=a, scalar=-0.5, in1=v, op0=ALU.mult, op1=ALU.mult)
        else:
            step = nc.vector.scalar_tensor_tensor(out=y, in0=a, scalar=1.5, in1=y, op0=ALU.add, op1=ALU.mult)
        step.then_inc(self.newton.sem, 1)

    def vector_rows(self, nc, dve, g, tiles=range(NB)):
        dve.wait_ge(self.newton.sem, self.newton.upto(g))
        if self.turns:
            if self.turned.comes(g, back=1):
                dve.wait_ge(self.turned.sem, self.turned.upto(g, back=1))
        for t in tiles:
            nc.vector.tensor_scalar(self.xn[:, t, :], self.tile(g, t), self.mv[:, t, 0:1],
                                    self.work[:, 2, t:t + 1], ALU.subtract, ALU.mult).then_inc(self.rows.sem, 1)

    def tensor_turn(self, nc, pe, g, bank):
        for t in range(NB):
            pe.wait_ge(self.rows.sem, self.rows.upto(g, t + 1))
            last = nc.tensor.transpose(bank[:, t * D:(t + 1) * D], self.xn[:, t, :], self.ident)
        last.then_inc(self.turned.sem, 1)

    def scalar_high(self, nc, act, g, bank, high):
        act.wait_ge(self.turned.sem, self.turned.upto(g))
        nc.scalar.copy(high, bank[:, 0:GT]).then_inc(self.high.sem, 1)

    def vector_low(self, nc, dve, g, bank, high, low):
        dve.wait_ge(self.high.sem, self.high.upto(g))
        nc.vector.tensor_tensor(low, bank[:, 0:GT], high.bitcast(F32), ALU.subtract).then_inc(self.low.sem, 1)


def split_product(nc, out, w_high, w_low, m_high, m_low, start, stop, **kw):
    nc.tensor.matmul(out, w_low, m_high, start=start, stop=False, **kw)
    nc.tensor.matmul(out, w_high, m_low, start=False, stop=False, **kw)
    return nc.tensor.matmul(out, w_high, m_high, start=False, stop=stop, **kw)


PLAN = {"k0": 1, "rk0": 1, "k1": 2, "rk1": 2, "kf": 2, "kb": 5, "turn": 6, "high": 5, "low": 8, "q0": 9, "rq0": 10,
        "q1": 11, "rq1": 12, "qf": 10, "v": 13, "v1": 12, "rest": 15, "v2": 14, "v3": 14, "ahead": 5}

HPLAN = {"steps": 0, "turn": 6, "high": 5, "low": 7, "halves": 6, "enc0": 8, "tanh0": 8, "enc1": 11, "tanh1": 10,
         "spikes0": 11, "spikes1": 11, "steps1": 8, "s2c": 12, "input": 11, "input_low": 13, "wr": 13, "logits": 13,
         "exp": 14, "ranks": 15, "gates": 17}


def layer0_attention(nc, f0, fr, ws_d, wf_d, sel0_d, x, ctxt, const, cc, ident, tg, g_raw, stats, mv, work, xn, xh, xl,
                     x_d, ctxt_d, gates_d, wa_d, bo_d, const_d, x_in, x_rest_in, signal_of):
    with ExitStack() as ctx:
        def sb(name, shape, dt=F32):
            return ctx.enter_context(nc.sbuf_tensor("a0_" + name, shape, dt))

        def pb(name):
            return ctx.enter_context(nc.psum_tensor("a0_" + name, [128, 512], F32))

        def signal(name, per):
            return signal_of("a0_" + name, per)

        wa = sb("wa", [D, 6 * 128])
        bo = sb("bo", [1, D])
        one_row = sb("one_row", [1, T])
        wqh = sb("wqh", [D, 2 * 128], F32R)
        wql = sb("wql", [D, 2 * 128], F32R)
        qc = sb("qc", [D, GT])
        qs = sb("qs", [D, GT])
        qf = sb("qf", [D, 2, GT])
        kc = sb("kc", [D, GS])
        ks = sb("ks", [D, GS])
        kf = sb("kf", [D, GS])
        kb = sb("kb", [D, 2, NQ, NB, S])
        qz = sb("qz", [D, 2, QUADS, T])
        vr1 = sb("vr1", [S, GT])
        vx = sb("vx", [S, 2, NB, HEADS, VP], BF16)
        mx = sb("mx", [T, 2, NQ])
        ss = sb("ss", [T, 2, NQ, S])
        p32 = sb("p32", [S, 2, NQ * T])
        p1 = sb("p1", [S, 4, NQ * T], F16)
        p2 = sb("p2", [S, 4, NQ * T], F16)
        o9 = sb("o9", [T, HEADS, HD + 1])
        rec = sb("rec", [T, HEADS])
        on = sb("on", [T, HEADS, HD])
        ot = sb("ot", [D, 2, T])

        bank_s = [pb("s0"), pb("s1")]
        bank_t = [pb("t0"), pb("t1")]
        bank_o = [pb("o0"), pb("o1")]
        bank_w = pb("w")
        bank_m = pb("m")

        w_in, w_high, w_low = f0["w_in"], f0["w_high"], f0["w_low"]

        def w_part(name, i):
            return f0[name][:, i * NS_COLS // WPARTS:(i + 1) * NS_COLS // WPARTS]

        norm = Norm(signal, "norm", lambda g, t: x[:, g * NB + t, :], stats, mv, work, xn, ident)
        const_in = signal("const_in", 16)
        ctx_in = signal("ctx_in", 16)
        zeroed = signal("zeroed", 1)
        wq_high = signal("wq_high", 2)
        wq_low = signal("wq_low", 1)
        q_made = signal("q_made", 2)
        qcs = signal("qcs", 2)
        k_made = signal("k_made", 2)
        kcs = signal("kcs", 2)
        kf_ready = signal("kf_ready", 1)
        kb_ready = signal("kb_ready", NQ)
        v_made = signal("v_made", 1)
        v_part = signal("v_part", 2)
        v_rest = signal("v_rest", 1)
        v_third = signal("v_third", 1)
        qf_ready = signal("qf_ready", 2)
        qz_ready = signal("qz_ready", UNITS)
        s_full = signal("s_full", UNITS)
        s_max = signal("s_max", UNITS)
        ss_ready = signal("ss_ready", UNITS)
        t_full = signal("t_full", UNITS)
        p1_ready = signal("p1_ready", UNITS)
        p2_ready = signal("p2_ready", UNITS)
        pv_done = signal("pv_done", UNITS)
        o_sum = signal("o_sum", NB)
        o_rec = signal("o_rec", NB)
        on_ready = signal("on_ready", NB)
        on_turned = signal("on_turned", NB)
        ot_ready = signal("ot_ready", NB)
        w_done = signal("w_done", NB)
        x_done = signal("x_done", NB)

        def vx_parts(par):
            return vx[:, bass.ds(par, 1), :, :, :].rearrange("s o b h (n c) -> s (o b) h n c", n=3)

        def lag(u, by):
            return (0, u - by) if u >= by else (1, u - by + UNITS)

        def batch_before(g, u, by):
            b = u // QUADS - by
            return (g, b) if b >= 0 else (g - 1, b + NB)

        with nc.Block() as block:

            @block.sync
            def _(sp):
                sp.dma_start(const[:, :], const_d).then_inc(const_in.sem, 16)
                sp.dma_start(x[:, 0:NB, :], x_d[0:NB].rearrange("b t d -> t b d")).then_inc(x_in.sem, 16)
                sp.dma_start(wa[:, :], wa_d).then_inc(const_in.sem, 16)
                sp.dma_start(bo[:, :], bo_d).then_inc(const_in.sem, 16)
                sp.dma_start(g_raw[:, :], gates_d).then_inc(const_in.sem, 16)
                sp.dma_start(ctxt[:, :], ctxt_d[:, 0:GS]).then_inc(ctx_in.sem, 16)
                sp.dma_start(x[:, NB:B, :], x_d[NB:B].rearrange("b t d -> t b d")).then_inc(x_rest_in.sem, 16)
                with sp.Fori(1, G) as g:
                    if k_made.comes(g, back=1):
                        sp.wait_ge(k_made.sem, k_made.upto(g, back=1))
                    if v_made.comes(g, back=1):
                        sp.wait_ge(v_made.sem, v_made.upto(g, back=1))
                    sp.dma_start(ctxt[:, :], ctxt_d[:, bass.ds(g * GS, GS)]).then_inc(ctx_in.sem, 16)
                for to, of in ((f0["ws"], ws_d), (f0["wf"], wf_d), (f0["sel_raw"], sel0_d)):
                    sp.dma_start(to[:, 0:of.shape[1]], of).then_inc(w_in.sem, 16)

            @block.gpsimd
            def _(pool):
                nc.gpsimd.memset(vx[:, :, :, :, :], 0.0).then_inc(zeroed.sem, 1)
                nc.gpsimd.memset(one_row[:, :], 1.0).then_inc(zeroed.sem, 1)
                pool.wait_ge(zeroed.sem, 2)
                for par in range(2):
                    nc.gpsimd.memset(vx[:, par, :, :, HD:HD + 1], 1.0).then_inc(zeroed.sem, 1)
                pool.wait_ge(zeroed.sem, 4)

                def keys(g):
                    pool.wait_ge(kcs.sem, kcs.upto(g))
                    if kb_ready.comes(g, back=1):
                        pool.wait_ge(kb_ready.sem, kb_ready.upto(g, back=1))
                    nc.gpsimd.tensor_tensor(kf[:, :], kc[:, :], ks[:, :], ALU.add).then_inc(kf_ready.sem, 1)

                def third(g):
                    pool.wait_ge(v_part.sem, v_part.upto(g))
                    v = vx_parts(g % 2)
                    nc.gpsimd.tensor_tensor(v[:, :, :, 2, 0:HD], vr1.rearrange("s (b h c) -> s b h c", b=NB, h=HEADS),
                                            v[:, :, :, 1, 0:HD], ALU.subtract).then_inc(v_third.sem, 1)

                def queries(g):
                    pool.wait_ge(qcs.sem, qcs.upto(g))
                    if qz_ready.comes(g, back=2):
                        pool.wait_ge(qz_ready.sem, qz_ready.upto(g, back=2))
                    nc.gpsimd.tensor_tensor(qf[:, bass.ds(g % 2, 1), :].rearrange("d o n -> d (o n)"), qc[:, :],
                                            qs[:, :], ALU.add).then_inc(qf_ready.sem, 1)

                def front(u):
                    if u == HPLAN["ranks"]:
                        fr.router.gpsimd_ranks(nc, pool, 0)

                def second_part(g, u):
                    back, v = lag(u, 4)
                    pool.wait_ge(p1_ready.sem, p1_ready.upto(g, u + 1))
                    if pv_done.comes(g, v + 1, back=back):
                        pool.wait_ge(pv_done.sem, pv_done.upto(g, v + 1, back=back))
                    nc.gpsimd.tensor_tensor(p2[:, u % 4, :], p32[:, u % 2, :], p1[:, u % 4, :],
                                            ALU.subtract).then_inc(p2_ready.sem, 1)

                def group(g, more):
                    for u in range(UNITS):
                        second_part(g, u)
                        if more:
                            if u == PLAN["kf"]:
                                keys(g + 1)
                            if u == PLAN["qf"]:
                                queries(g + 1)
                            if u == PLAN["v3"]:
                                third(g + 1)
                        else:
                            front(u)

                keys(0)
                queries(0)
                third(0)
                group(0, True)
                with pool.Fori(1, G - 1) as g:
                    group(g, True)
                group(G - 1, False)
                for u in range(UNITS, UNITS + 6):
                    front(u)

            @block.scalar
            def _(act):
                act.wait_ge(const_in.sem, 64)
                nc.scalar.activation(tg[:, :], g_raw[:, :], ACT.Tanh).then_inc(wq_high.sem, 1)
                nc.scalar.copy(wqh[:, :], wa[:, WA["q"]:WA["q"] + 256]).then_inc(wq_high.sem, 1)
                act.wait_ge(zeroed.sem, 4)

                def high(g):
                    if q_made.comes(g, back=1):
                        act.wait_ge(q_made.sem, q_made.upto(g, back=1))
                    norm.scalar_high(nc, act, g, bank_m, xh[:, :])

                def keys(g, j):
                    act.wait_ge(kf_ready.sem, kf_ready.upto(g))
                    if s_full.comes(g, back=2):
                        act.wait_ge(s_full.sem, s_full.upto(g, back=2))
                    nc.scalar.activation(kb[:, bass.ds(g % 2, 1), j, :, :], kf.rearrange("d (o b s) -> d o b s", o=1, b=NB),
                                         ACT.Copy, scale=cc("mask")[:, j:j + 1]).then_inc(kb_ready.sem, 1)

                def queries(g, u):
                    b, c = divmod(u, QUADS)
                    if u == 0:
                        act.wait_ge(qf_ready.sem, qf_ready.upto(g, 1))
                        act.sem_inc(qf_ready.sem, 1)
                    nc.scalar.activation(qz[:, b % 2, c, :].rearrange("d (o t) -> d o t", o=1),
                                         qf[:, bass.ds(g % 2, 1), b * T:(b + 1) * T], ACT.Copy,
                                         scale=cc("qmask")[:, c:c + 1]).then_inc(qz_ready.sem, 1)

                def values(g, bank=bank_m):
                    act.wait_ge(v_made.sem, v_made.upto(g))
                    if pv_done.comes(g, back=2):
                        act.wait_ge(pv_done.sem, pv_done.upto(g, back=2))
                    v = vx_parts(g % 2)
                    nc.scalar.copy(v[:, :, :, 0, 0:HD],
                                   bank[0:S, :].rearrange("s (b h c) -> s b h c", b=NB, h=HEADS)).then_inc(v_part.sem, 1)

                def values2(g):
                    act.wait_ge(v_rest.sem, v_rest.upto(g))
                    v = vx_parts(g % 2)
                    nc.scalar.copy(v[:, :, :, 1, 0:HD],
                                   vr1.rearrange("s (b h c) -> s b h c", b=NB, h=HEADS)).then_inc(v_part.sem, 1)

                def exps(g, u):
                    act.wait_ge(t_full.sem, t_full.upto(g, u + 1))
                    back, v = lag(u, 2)
                    if p2_ready.comes(g, v + 1, back=back):
                        act.wait_ge(p2_ready.sem, p2_ready.upto(g, v + 1, back=back))
                    nc.scalar.activation(p32[:, u % 2, :], bank_t[u % 2][0:S, :], ACT.Exp)
                    back, v = lag(u, 4)
                    if pv_done.comes(g, v + 1, back=back):
                        act.wait_ge(pv_done.sem, pv_done.upto(g, v + 1, back=back))
                    nc.scalar.activation(p1[:, u % 4, :], bank_t[u % 2][0:S, :], ACT.Exp).then_inc(p1_ready.sem, 1)

                def turned(g, b, bank=bank_w):
                    act.wait_ge(on_turned.sem, on_turned.upto(g, b + 1))
                    nc.scalar.copy(ot[:, b % 2, :], bank[:, 0:T]).then_inc(ot_ready.sem, 1)

                def front(u):
                    if u == HPLAN["high"]:
                        act.wait_ge(q_made.sem, q_made.upto(G - 1))
                        fr.norm.scalar_high(nc, act, 0, bank_m, xh[:, :])
                    if u == HPLAN["tanh0"]:
                        act.wait_ge(fr.halves.sem, fr.halves.upto(0))
                        fr.scalar_tanh(nc, act, 0, 0, bank_m)
                    if u == HPLAN["tanh1"]:
                        fr.scalar_tanh(nc, act, 0, 1, bank_m)
                    if u == HPLAN["input"]:
                        fr.scalar_full(nc, act, 0, bank_m)
                        fr.scalar_part(nc, 0, bank_m)
                    if u == HPLAN["exp"]:
                        fr.router.scalar_exp(nc, act, 0)

                def group(g, first, more):
                    for u in range(UNITS):
                        exps(g, u)
                        if u % QUADS == 2 and not (first and u < 2 * QUADS):
                            turned(*batch_before(g, u, 2))
                        if u + PLAN["ahead"] < UNITS:
                            queries(g, u + PLAN["ahead"])
                        if not more:
                            front(u)
                        if more:
                            if PLAN["kb"] <= u < PLAN["kb"] + NQ:
                                keys(g + 1, u - PLAN["kb"])
                            if u == PLAN["high"]:
                                high(g + 1)
                            if u == PLAN["v1"]:
                                values(g + 1)
                            if u == PLAN["v2"]:
                                values2(g + 1)
                        elif u % 3 == 0 and u // 3 < WPARTS:
                            act.wait_ge(w_in.sem, w_in.upto(0))
                            nc.scalar.copy(w_part("wh", u // 3), w_part("ws", u // 3)).then_inc(w_high.sem, 1)
                        if more:
                            if u + PLAN["ahead"] >= UNITS:
                                queries(g + 1, u + PLAN["ahead"] - UNITS)

                values(0, bank_o[0])
                high(0)
                for j in range(NQ):
                    keys(0, j)
                values2(0)
                for u in range(PLAN["ahead"]):
                    queries(0, u)
                group(0, True, True)
                with act.Fori(1, G - 1) as g:
                    group(g, False, True)
                group(G - 1, False, False)
                front(UNITS)
                turned(G - 1, NB - 2)
                front(UNITS + 1)
                turned(G - 1, NB - 1, bank_s[0])
                for u in range(UNITS + 2, UNITS + 6):
                    front(u)

            @block.vector
            def _(dve):
                def low(g):
                    if q_made.comes(g, back=1):
                        dve.wait_ge(q_made.sem, q_made.upto(g, back=1))
                    norm.vector_low(nc, dve, g, bank_m, xh[:, :], xl[:, :])

                def rotate_q(g, i, bank=bank_m):
                    table, out = (("cosq", qc), ("sinq", qs))[i]
                    dve.wait_ge(q_made.sem, q_made.upto(g, i + 1))
                    if qf_ready.comes(g, back=1):
                        dve.wait_ge(qf_ready.sem, qf_ready.upto(g, back=1))
                    nc.vector.tensor_tensor(
                        out.rearrange("d (b t) -> d b t", b=NB), bank[:, :].rearrange("d (b t) -> d b t", b=NB),
                        cc(table).rearrange("d (o t) -> d o t", o=1).to_broadcast([D, NB, T]), ALU.mult)\
                        .then_inc(qcs.sem, 1)

                def rotate_k(g, i, bank=bank_m):
                    table, out = (("cosk", kc), ("sink", ks))[i]
                    dve.wait_ge(k_made.sem, k_made.upto(g, i + 1))
                    if kf_ready.comes(g, back=1):
                        dve.wait_ge(kf_ready.sem, kf_ready.upto(g, back=1))
                    nc.vector.tensor_tensor(
                        out.rearrange("d (b s) -> d b s", b=NB), bank[:, 0:GS].rearrange("d (b s) -> d b s", b=NB),
                        cc(table).rearrange("d (o s) -> d o s", o=1).to_broadcast([D, NB, S]), ALU.mult)\
                        .then_inc(kcs.sem, 1)

                def rest_v(g, bank=bank_m):
                    dve.wait_ge(v_part.sem, v_part.upto(g, 1))
                    if v_third.comes(g, back=1):
                        dve.wait_ge(v_third.sem, v_third.upto(g, back=1))
                    v = vx_parts(g % 2)
                    nc.vector.tensor_tensor(vr1.rearrange("s (b h c) -> s b h c", b=NB, h=HEADS),
                                            bank[0:S, :].rearrange("s (b h c) -> s b h c", b=NB, h=HEADS),
                                            v[:, :, :, 0, 0:HD], ALU.subtract).then_inc(v_rest.sem, 1)

                def scores_of(u):
                    return bank_s[u % 2][:, 0:NQ * S].rearrange("t (j s) -> t j s", j=NQ)

                def maximum(g, u):
                    dve.wait_ge(s_full.sem, s_full.upto(g, u + 1))
                    nc.vector.tensor_reduce(mx[:, u % 2, :], scores_of(u), AX.X, ALU.max).then_inc(s_max.sem, 1)

                def shift(g, u):
                    dve.wait_ge(s_max.sem, s_max.upto(g, u + 1))
                    back, v = lag(u, 2)
                    if t_full.comes(g, v + 1, back=back):
                        dve.wait_ge(t_full.sem, t_full.upto(g, v + 1, back=back))
                    nc.vector.tensor_tensor(ss[:, u % 2, :, :], scores_of(u),
                                            mx[:, u % 2, :].rearrange("t (j o) -> t j o", o=1).to_broadcast([T, NQ, S]),
                                            ALU.subtract).then_inc(ss_ready.sem, 1)

                def output_sum(g, b):
                    dve.wait_ge(pv_done.sem, pv_done.upto(g, QUADS * (b + 1)))
                    if b:
                        dve.wait_ge(on_ready.sem, on_ready.upto(g, b))
                    else:
                        if on_ready.comes(g, NB, back=1):
                            dve.wait_ge(on_ready.sem, on_ready.upto(g, NB, back=1))
                    parts = bank_o[b % 2][:, 0:HEADS * VP].rearrange("t (h n c) -> t h c n", h=HEADS, n=3)
                    nc.vector.tensor_reduce(o9[:, :, :], parts, AX.X, ALU.add).then_inc(o_sum.sem, 1)

                def output_inverse(g, b):
                    dve.wait_ge(o_sum.sem, o_sum.upto(g, b + 1))
                    nc.vector.reciprocal(rec[:, :], o9[:, :, HD]).then_inc(o_rec.sem, 1)

                def output_divide(g, b):
                    dve.wait_ge(o_rec.sem, o_rec.upto(g, b + 1))
                    if b:
                        dve.wait_ge(on_turned.sem, on_turned.upto(g, b))
                    else:
                        if on_turned.comes(g, NB, back=1):
                            dve.wait_ge(on_turned.sem, on_turned.upto(g, NB, back=1))
                    nc.vector.tensor_tensor(on[:, :, :], o9[:, :, 0:HD],
                                            rec.rearrange("t (h o) -> t h o", o=1).to_broadcast([T, HEADS, HD]),
                                            ALU.mult).then_inc(on_ready.sem, 1)

                def residual(g, b, bank=bank_w):
                    dve.wait_ge(w_done.sem, w_done.upto(g, b + 1))
                    nc.vector.scalar_tensor_tensor(out=x[:, g * NB + b, :], in0=bank[:, T:T + D], scalar=tg[:, 0:1],
                                                   in1=x[:, g * NB + b, :], op0=ALU.mult, op1=ALU.add)\
                        .then_inc(x_done.sem, 1)

                def front(u):
                    for h in range(2):
                        k = u - HPLAN["steps1" if h else "steps"]
                        if k == 0:
                            dve.wait_ge(x_done.sem, x_done.upto(h))
                            fr.norm.vector_stats(nc, h)
                            fr.norm.vector_moments(nc, dve, h)
                        if 1 <= k <= STEPS // 3:
                            for i in range(3 * k - 3, 3 * k):
                                fr.norm.vector_step(nc, dve, h, i)
                        if k == STEPS // 3 + 1:
                            if h == 0:
                                dve.wait_ge(norm.turned.sem, norm.turned.upto(G - 1))
                            fr.norm.vector_rows(nc, dve, h)
                    if u == HPLAN["low"]:
                        dve.wait_ge(q_made.sem, q_made.upto(G - 1))
                        fr.norm.vector_low(nc, dve, 0, bank_m, xh[:, :], xl[:, :])
                    if u == HPLAN["halves"]:
                        dve.wait_ge(w_in.sem, w_in.upto(0))
                        fr.vector_halves(nc)
                    if u == HPLAN["spikes0"]:
                        fr.vector_spikes(nc, dve, 0, 0)
                    if u == HPLAN["spikes1"]:
                        fr.vector_spikes(nc, dve, 0, 1)
                    if u == HPLAN["input_low"]:
                        fr.vector_input_low(nc, dve, 0)
                    if u == HPLAN["logits"]:
                        fr.vector_logits(nc, dve, 0, bank_m)
                    if u == HPLAN["gates"]:
                        fr.router.vector_gates(nc, dve, 0)
                        fr.router.vector_gates2(nc, dve, 0)

                def between(g, u, first, more):
                    if u % QUADS == 1 and not (first and u < 2 * QUADS):
                        output_inverse(*batch_before(g, u, 2))
                    if not more:
                        front(u)
                        return
                    if u == 0:
                        dve.wait_ge(x_rest_in.sem, x_rest_in.upto(0))
                        norm.vector_stats(nc, g + 1)
                    if 1 <= u <= 4:
                        norm.vector_step(nc, dve, g + 1, 3 * (u - 1))
                    if u == 5:
                        norm.vector_rows(nc, dve, g + 1, range(NB // 2))
                    if u == PLAN["low"]:
                        low(g + 1)
                    if u == PLAN["rq0"]:
                        rotate_q(g + 1, 0)
                    if u == PLAN["rq1"]:
                        rotate_q(g + 1, 1)
                    if u == PLAN["rest"]:
                        rest_v(g + 1)

                def group(g, first, more):
                    for u in range(UNITS):
                        maximum(g, u)
                        between(g, u, first, more)
                        shift(g, u)
                        if more and u == 0:
                            norm.vector_moments(nc, dve, g + 1)
                        if more and 1 <= u <= 4:
                            norm.vector_step(nc, dve, g + 1, 3 * (u - 1) + 1)
                        if u % QUADS == 0 and not (first and u < 2 * QUADS):
                            output_sum(*batch_before(g, u, 2))
                        if u % QUADS == 1 and not (first and u < 2 * QUADS):
                            output_divide(*batch_before(g, u, 2))
                        if u % QUADS == 1 and not (first and u < 3 * QUADS):
                            residual(*batch_before(g, u, 3))
                        if not more and u % 3 == 1 and u // 3 < WPARTS:
                            dve.wait_ge(w_high.sem, u // 3 + 1)
                            nc.vector.tensor_tensor(w_part("wl", u // 3), w_part("ws", u // 3),
                                                    w_part("wh", u // 3).bitcast(F32), ALU.subtract).then_inc(w_low.sem, 1)
                        if more:
                            if u == PLAN["rk0"]:
                                rotate_k(g + 1, 0)
                            if u == PLAN["rk1"]:
                                rotate_k(g + 1, 1)
                            if 1 <= u <= 4:
                                norm.vector_step(nc, dve, g + 1, 3 * (u - 1) + 2)
                            if u == 5:
                                norm.vector_rows(nc, dve, g + 1, range(NB // 2, NB))

                dve.wait_ge(const_in.sem, 64)
                dve.wait_ge(wq_high.sem, 2)
                nc.vector.tensor_tensor(wql[:, :], wa[:, WA["q"]:WA["q"] + 256], wqh[:, :].bitcast(F32),
                                        ALU.subtract).then_inc(wq_low.sem, 1)
                dve.wait_ge(x_in.sem, x_in.upto(0))
                norm.vector_stats(nc, 0)
                norm.vector_moments(nc, dve, 0)
                for i in range(STEPS):
                    norm.vector_step(nc, dve, 0, i)
                    if i == STEPS // 3:
                        rotate_k(0, 0)
                    if i == 2 * STEPS // 3:
                        rotate_k(0, 1, bank_o[0])
                norm.vector_rows(nc, dve, 0)
                rest_v(0, bank_o[0])
                low(0)
                rotate_q(0, 0)
                rotate_q(0, 1, bank_o[1])
                group(0, True, True)
                with dve.Fori(1, G - 1) as g:
                    group(g, False, True)
                group(G - 1, False, False)
                residual(G - 1, NB - 3)
                for b in (NB - 2, NB - 1):
                    output_sum(G - 1, b)
                    output_inverse(G - 1, b)
                    output_divide(G - 1, b)
                    front(UNITS + b - NB + 2)
                residual(G - 1, NB - 2)
                residual(G - 1, NB - 1, bank_s[0])
                for u in range(UNITS + 2, UNITS + 6):
                    front(u)

            @block.tensor
            def _(pe):
                def project_k(g, i, bank=bank_m):
                    pe.wait_ge(ctx_in.sem, ctx_in.upto(g))
                    if bank is bank_m:
                        if i:
                            pe.wait_ge(kcs.sem, kcs.upto(g, 1))
                        else:
                            if v_rest.comes(g, back=1):
                                pe.wait_ge(v_rest.sem, v_rest.upto(g, back=1))
                    w = WA["kp" if i else "k"]
                    nc.tensor.matmul(bank[:, 0:GS], wa[:, w:w + 128], ctxt[:, :],
                                     start=True, stop=True).then_inc(k_made.sem, 1)

                def project_v(g, bank=bank_m):
                    if bank is bank_m:
                        pe.wait_ge(qcs.sem, qcs.upto(g))
                    else:
                        pe.wait_ge(kcs.sem, kcs.upto(g))
                    for b in range(NB):
                        last = nc.tensor.matmul(bank[0:S, b * D:(b + 1) * D], ctxt[:, b * S:(b + 1) * S],
                                                wa[:, WA["v"]:WA["v"] + 128], start=True, stop=True)
                    last.then_inc(v_made.sem, 1)

                def turn_tokens(g):
                    pe.wait_ge(kcs.sem, kcs.upto(g))
                    norm.tensor_turn(nc, pe, g, bank_m)

                def project_q(g, i, bank=bank_m):
                    if i and bank is bank_m:
                        pe.wait_ge(qcs.sem, qcs.upto(g, 1))
                    else:
                        pe.wait_ge(norm.low.sem, norm.low.upto(g))
                    w = slice(128 * i, 128 * i + 128)
                    split_product(nc, bank[:, :], wqh[:, w], wql[:, w], xh[:, :], xl[:, :], True, True)\
                        .then_inc(q_made.sem, 1)

                def scores(g, u):
                    b, c = divmod(u, QUADS)
                    pe.wait_ge(qz_ready.sem, qz_ready.upto(g, u + 1))
                    if u == 0:
                        pe.wait_ge(kb_ready.sem, kb_ready.upto(g))
                    back, v = lag(u, 2)
                    if ss_ready.comes(g, v + 1, back=back):
                        pe.wait_ge(ss_ready.sem, ss_ready.upto(g, v + 1, back=back))
                    nc.tensor.matmul(bank_s[u % 2][:, 0:NQ * S].rearrange("t (j s) -> t j s", j=NQ), qz[:, b % 2, c, :],
                                     kb[:, bass.ds(g % 2, 1), :, b, :].rearrange("d o j s -> d (o j) s"),
                                     start=True, stop=True).then_inc(s_full.sem, 1)

                def turn(g, u):
                    pe.wait_ge(ss_ready.sem, ss_ready.upto(g, u + 1))
                    back, v = lag(u, 2)
                    if p1_ready.comes(g, v + 1, back=back):
                        pe.wait_ge(p1_ready.sem, p1_ready.upto(g, v + 1, back=back))
                    for j in range(NQ):
                        last = nc.tensor.transpose(bank_t[u % 2][0:S, j * T:(j + 1) * T], ss[:, u % 2, j, :], ident)
                    last.then_inc(t_full.sem, 1)

                def weigh(g, u):
                    b, c = divmod(u, QUADS)
                    if u == 0:
                        pe.wait_ge(v_third.sem, v_third.upto(g))
                    if c == 0:
                        if b >= 2:
                            pe.wait_ge(o_sum.sem, o_sum.upto(g, b - 1))
                        else:
                            if o_sum.comes(g, b + NB - 1, back=1):
                                pe.wait_ge(o_sum.sem, o_sum.upto(g, b + NB - 1, back=1))
                    pe.wait_ge(p1_ready.sem, p1_ready.upto(g, u + 1))
                    pe.wait_ge(p2_ready.sem, p2_ready.upto(g, u + 1))
                    for j in range(NQ):
                        h = NQ * c + j
                        v = vx[:, bass.ds(g % 2, 1), b, h, :].rearrange("s o n -> s (o n)")
                        for i, p in enumerate((p1, p2)):
                            last = nc.tensor.matmul(bank_o[b % 2][:, h * VP:(h + 1) * VP], p[:, u % 4, j * T:(j + 1) * T],
                                                    v, start=(h == 0 and i == 0), stop=(h == HEADS - 1 and i == 1),
                                                    skip_group_check=True)
                    last.then_inc(pv_done.sem, 1)

                def out_turn(g, b, bank=bank_w):
                    pe.wait_ge(on_ready.sem, on_ready.upto(g, b + 1))
                    if bank is bank_w:
                        if b:
                            pe.wait_ge(x_done.sem, x_done.upto(g, b))
                        else:
                            if x_done.comes(g, NB, back=1):
                                pe.wait_ge(x_done.sem, x_done.upto(g, NB, back=1))
                    nc.tensor.transpose(bank[:, 0:T], on[:, :, :].rearrange("t h c -> t (h c)"), ident)\
                        .then_inc(on_turned.sem, 1)

                def out_project(g, b, bank=bank_w):
                    pe.wait_ge(ot_ready.sem, ot_ready.upto(g, b + 1))
                    nc.tensor.matmul(bank[:, T:T + D], one_row[:, :], bo[:, :], start=True, stop=False)
                    nc.tensor.matmul(bank[:, T:T + D], ot[:, b % 2, :], wa[:, WA["o"]:WA["o"] + 128], start=False,
                                     stop=True).then_inc(w_done.sem, 1)

                def front(u):
                    if u == HPLAN["turn"]:
                        pe.wait_ge(v_rest.sem, v_rest.upto(G - 1))
                        fr.norm.tensor_turn(nc, pe, 0, bank_m)
                    if u == HPLAN["enc0"]:
                        pe.wait_ge(fr.norm.low.sem, fr.norm.low.upto(0))
                        pe.wait_ge(w_low.sem, 1)
                        fr.tensor_encode(nc, 0, bank_m)
                    if u == HPLAN["enc1"]:
                        pe.wait_ge(fr.enc_tanh.sem, fr.enc_tanh.upto(0, 1))
                        fr.tensor_encode(nc, 1, bank_m)
                    if u == HPLAN["s2c"]:
                        fr.tensor_input(nc, pe, 0, bank_m)
                    if u == HPLAN["wr"]:
                        pe.wait_ge(fr.c_high.sem, fr.c_high.upto(0))
                        fr.tensor_logits(nc, pe, 0, bank_m)

                def group(g, first, more):
                    for u in range(UNITS):
                        scores(g, u)
                        if not (first and u < 1):
                            back, v = lag(u, 1)
                            turn(g - back, v)
                        if not (first and u < 4):
                            back, v = lag(u, 4)
                            weigh(g - back, v)
                        if u % QUADS == 2 and not (first and u < 2 * QUADS):
                            out_turn(*batch_before(g, u, 2))
                        if u % QUADS == 0 and not (first and u < 3 * QUADS):
                            out_project(*batch_before(g, u, 3))
                        if not more:
                            front(u)
                        if more:
                            if u == PLAN["k0"]:
                                project_k(g + 1, 0)
                            if u == PLAN["k1"]:
                                project_k(g + 1, 1)
                            if u == PLAN["turn"]:
                                turn_tokens(g + 1)
                            if u == PLAN["q0"]:
                                project_q(g + 1, 0)
                            if u == PLAN["q1"]:
                                project_q(g + 1, 1)
                            if u == PLAN["v"]:
                                project_v(g + 1)

                pe.wait_ge(const_in.sem, 64)
                pe.wait_ge(zeroed.sem, 4)
                project_k(0, 0)
                project_k(0, 1, bank_o[0])
                project_v(0, bank_o[0])
                turn_tokens(0)
                pe.wait_ge(wq_low.sem, 1)
                project_q(0, 0)
                project_q(0, 1, bank_o[1])
                group(0, True, True)
                with pe.Fori(1, G - 1) as g:
                    group(g, False, True)
                g = G - 1
                group(g, False, False)
                turn(g, UNITS - 1)
                for u in range(UNITS - 4, UNITS):
                    weigh(g, u)
                out_project(g, NB - 3)
                last_bank = {NB - 2: bank_w, NB - 1: bank_s[0]}
                for b in range(NB - 2, NB):
                    out_turn(g, b, last_bank[b])
                    front(UNITS + b - NB + 2)
                for b in range(NB - 2, NB):
                    out_project(g, b, last_bank[b])
                for u in range(UNITS + 2, UNITS + 6):
                    front(u)


class Router:

    def __init__(self, signal, name, sb, k, tri, ident, extra):
        self.k, self.ident, self.n = k, ident, E0 + extra
        self.tri = tri
        self.lg = sb(f"{name}_lg", [T, NB, E0])
        self.top = sb(f"{name}_top", [T, NB])
        self.d = sb(f"{name}_d", [T, NB, E0])
        self.ex = sb(f"{name}_ex", [T, NB, E0])
        self.gr = sb(f"{name}_gr", [T, NB, E0, E0])
        self.eq = sb(f"{name}_eq", [T, NB, E0, E0])
        self.rank = sb(f"{name}_rank", [T, NB, E0])
        self.em = sb(f"{name}_em", [T, NB, E0])
        self.tot = sb(f"{name}_tot", [T, NB])
        self.parts = sb(f"{name}_parts", [T, NB, 2 * self.n])
        self.logits = signal(f"{name}_logits", 1)
        self.steps = signal(f"{name}_steps", 9)
        self.exp = signal(f"{name}_exp", 1)
        self.compared = signal(f"{name}_compared", 2)
        self.ranks = signal(f"{name}_ranks", 2)
        self.turned = signal(f"{name}_turned", 1)
        self.ready = signal(f"{name}_ready", 1)

    def wide(self, v):
        return v.rearrange("p (t o) -> p t o", o=1).to_broadcast([T, NB, E0])

    def vector_logits(self, nc, dve, g, bank, bias):
        if self.steps.comes(g, back=1):
            dve.wait_ge(self.steps.sem, self.steps.upto(g, back=1))
        if self.ranks.comes(g, back=1):
            dve.wait_ge(self.ranks.sem, self.ranks.upto(g, back=1))
        nc.vector.tensor_tensor(self.lg[:, :, :], bank[:, 0:NB * E0].rearrange("p (t e) -> p t e", e=E0),
                                bias.rearrange("p (o e) -> p o e", o=1).to_broadcast([T, NB, E0]), ALU.add)\
            .then_inc(self.logits.sem, 1)

    def vector_shift(self, nc, dve, g):
        own = self.lg.rearrange("p t (e o) -> p t e o", o=1).to_broadcast([T, NB, E0, E0])
        other = self.lg.rearrange("p t (o e) -> p t o e", o=1).to_broadcast([T, NB, E0, E0])
        dve.wait_ge(self.logits.sem, self.logits.upto(g))
        nc.vector.tensor_reduce(self.top[:, :], self.lg[:, :, :], AX.X, ALU.max).then_inc(self.steps.sem, 1)
        if self.steps.comes(g, 3, back=1):
            dve.wait_ge(self.steps.sem, self.steps.upto(g, 3, back=1))
        nc.vector.tensor_tensor(self.eq[:, :, :, :], other, own, ALU.is_equal).then_inc(self.compared.sem, 1)
        dve.wait_ge(self.steps.sem, self.steps.upto(g, 1))
        nc.vector.tensor_tensor(self.d[:, :, :], self.lg[:, :, :], self.wide(self.top), ALU.subtract)\
            .then_inc(self.steps.sem, 1)
        nc.vector.tensor_tensor(self.gr[:, :, :, :], other, own, ALU.is_gt).then_inc(self.compared.sem, 1)

    def scalar_exp(self, nc, act, g):
        act.wait_ge(self.steps.sem, self.steps.upto(g, 2))
        nc.scalar.activation(self.ex[:, :, :], self.d[:, :, :], ACT.Exp).then_inc(self.exp.sem, 1)

    def gpsimd_ranks(self, nc, pool, g):
        tri = self.tri.rearrange("p (o n) -> p o n", o=1).to_broadcast([T, NB, E0 * E0])
        eq = self.eq.rearrange("p t e f -> p t (e f)")
        pool.wait_ge(self.compared.sem, self.compared.upto(g))
        nc.gpsimd.tensor_tensor(eq, eq, tri, ALU.mult).then_inc(self.ranks.sem, 1)
        pool.wait_ge(self.ranks.sem, self.ranks.upto(g, 1))
        nc.gpsimd.tensor_tensor(self.gr[:, :, :, :], self.gr[:, :, :, :], self.eq[:, :, :, :], ALU.add)\
            .then_inc(self.ranks.sem, 1)

    def vector_gates(self, nc, dve, g):
        dve.wait_ge(self.ranks.sem, self.ranks.upto(g))
        nc.vector.tensor_reduce(self.rank[:, :, :], self.gr[:, :, :, :], AX.X, ALU.add).then_inc(self.steps.sem, 1)
        dve.wait_ge(self.steps.sem, self.steps.upto(g, 3))
        dve.wait_ge(self.exp.sem, self.exp.upto(g))
        nc.vector.scalar_tensor_tensor(out=self.em[:, :, :], in0=self.rank[:, :, :], scalar=self.k - 0.5,
                                       in1=self.ex[:, :, :], op0=ALU.is_lt, op1=ALU.mult).then_inc(self.steps.sem, 1)
        dve.wait_ge(self.steps.sem, self.steps.upto(g, 4))
        nc.vector.tensor_reduce(self.tot[:, :], self.em[:, :, :], AX.X, ALU.add).then_inc(self.steps.sem, 1)

    def vector_gates2(self, nc, dve, g):
        n = self.n
        dve.wait_ge(self.steps.sem, self.steps.upto(g, 5))
        nc.vector.reciprocal(self.tot[:, :], self.tot[:, :]).then_inc(self.steps.sem, 1)
        dve.wait_ge(self.steps.sem, self.steps.upto(g, 6))
        if self.turned.comes(g, back=1):
            dve.wait_ge(self.turned.sem, self.turned.upto(g, back=1))
        nc.vector.tensor_tensor(self.d[:, :, :], self.em[:, :, :], self.wide(self.tot), ALU.mult)\
            .then_inc(self.steps.sem, 1)
        nc.vector.tensor_tensor(self.parts[:, :, 0:E0].bitcast(F32R), self.em[:, :, :], self.wide(self.tot), ALU.mult)\
            .then_inc(self.steps.sem, 1)
        dve.wait_ge(self.steps.sem, self.steps.upto(g, 8))
        nc.vector.tensor_tensor(self.parts[:, :, n:n + E0].bitcast(F32R), self.d[:, :, :], self.parts[:, :, 0:E0],
                                ALU.subtract).then_inc(self.steps.sem, 1)

    def tensor_turn(self, nc, pe, g, bank):
        pe.wait_ge(self.steps.sem, self.steps.upto(g))
        for t in range(NB):
            last = nc.tensor.transpose(bank[0:2 * self.n, t * T:(t + 1) * T], self.parts[:, t, :], self.ident)
        last.then_inc(self.turned.sem, 1)

    def scalar_keep(self, nc, act, g, bank, out):
        act.wait_ge(self.turned.sem, self.turned.upto(g))
        nc.scalar.copy(out, bank[0:2 * self.n, 0:GT]).then_inc(self.ready.sem, 1)


class Front:

    def __init__(self, nc, ctx, f0, x, cc, ident, stats, mv, work, xn, xh, xl, signal_of):
        def sb(name, shape, dt=F32):
            return ctx.enter_context(nc.sbuf_tensor("f0_" + name, shape, dt))

        def signal(name, per):
            return signal_of("f0_" + name, per)

        self.f0, self.x, self.xh, self.xl = f0, x, xh, xl
        self.half_b = sb("half_b", [128, 4])
        self.gl = sb("gl", [128, 2, D])
        self.stats2 = sb("stats2", [128, NB, 6])
        self.mv2 = sb("mv2", [128, NB, 2])
        self.work2 = sb("work2", [128, 3, NB])
        self.te = sb("te", [128, 2, GT])
        self.sp = sb("sp", [128, 2, GT])
        self.c32 = sb("c32", [128, GT])
        self.cs = sb("cs", [128, 2, GT], F32R)
        self.norm = Norm(signal, "norm", lambda g, t: x[:, g * NB + t, :], stats, mv, work, xn, ident)
        self.dec_last = self.te[:, 0, :].rearrange("p (t d) -> p t d", t=NB)
        self.dn_last = self.sp[:, 0, :].rearrange("p (t d) -> p t d", t=NB)
        self.norm2_last = Norm(signal, "norm2", lambda g, t: self.dec_last[:, t, :], self.stats2, self.mv2, self.work2,
                               self.dn_last, ident, turns=False)
        self.scaled = signal("scaled", 2)
        self.x_done = signal("x_done", 1)
        self.router = Router(signal, "router", sb, K0, cc("tri"), ident, 0)
        self.halves = signal("halves", 2)
        self.enc_made = signal("enc_made", 2)
        self.enc_tanh = signal("enc_tanh", 2)
        self.spikes = signal("spikes", 2)
        self.c_made = signal("c_made", 1)
        self.c_full = signal("c_full", 1)
        self.c_high = signal("c_high", 1)
        self.c_ready = signal("c_ready", 1)
        self.l_made = signal("l_made", 1)

    def col(self, name, i=0, n=None, rows=128):
        a, b = WF[name]
        a, b = (a, b) if n is None else (a + i * n, a + (i + 1) * n)
        return self.f0["wf"][0:rows, a:b]

    def split(self, name, i, n=128, rows=128):
        a = WS[name][0] + i * n
        return self.f0["wh"][0:rows, a:a + n], self.f0["wl"][0:rows, a:a + n]

    def cs_of(self, g):
        return self.cs[:, bass.ds(g % 2, 1), :].rearrange("p o n -> p (o n)")

    def gpsimd_scale(self, nc, pool, g, i, dn):
        if i:
            pool.wait_ge(self.scaled.sem, self.scaled.upto(g, 1))
        else:
            pool.wait_ge(self.norm2_last.rows.sem, self.norm2_last.rows.upto(g))
        nc.gpsimd.tensor_tensor(dn[:, :, :], dn[:, :, :], self.gl[:, i:i + 1, :].to_broadcast([128, NB, D]),
                                ALU.add if i else ALU.mult).then_inc(self.scaled.sem, 1)

    def scalar_tanh(self, nc, act, g, i, bank):
        act.wait_ge(self.enc_made.sem, self.enc_made.upto(g, i + 1))
        if self.spikes.comes(g, i + 1, back=1):
            act.wait_ge(self.spikes.sem, self.spikes.upto(g, i + 1, back=1))
        nc.scalar.activation(self.te[:, i, :], bank[:, :], ACT.Tanh, bias=self.half_b[:, i:i + 1],
                             scale=0.5).then_inc(self.enc_tanh.sem, 1)

    def scalar_full(self, nc, act, g, bank):
        act.wait_ge(self.c_made.sem, self.c_made.upto(g))
        if self.l_made.comes(g, back=1):
            act.wait_ge(self.l_made.sem, self.l_made.upto(g, back=1))
        if self.c_ready.comes(g, back=1):
            act.wait_ge(self.c_ready.sem, self.c_ready.upto(g, back=1))
        nc.scalar.activation(self.c32[:, :], bank[:, :], ACT.Identity, bias=self.col("b_s2c"))\
            .then_inc(self.c_full.sem, 1)

    def scalar_part(self, nc, g, bank):
        nc.scalar.activation(self.cs[:, bass.ds(g % 2, 1), :], bank.rearrange("p (o n) -> p o n", o=1),
                             ACT.Identity, bias=self.col("b_s2c")).then_inc(self.c_high.sem, 1)

    def vector_halves(self, nc):
        nc.vector.tensor_scalar(self.half_b[:, 0:2], self.col("b_enc"), 0.5, None, ALU.mult).then_inc(self.halves.sem, 1)
        nc.vector.tensor_scalar(self.half_b[:, 2:4], self.col("b_c2s"), 0.5, None, ALU.mult).then_inc(self.halves.sem, 1)

    def vector_spikes(self, nc, dve, g, i):
        dve.wait_ge(self.enc_tanh.sem, self.enc_tanh.upto(g, i + 1))
        if self.c_made.comes(g, back=1):
            dve.wait_ge(self.c_made.sem, self.c_made.upto(g, back=1))
        nc.vector.tensor_scalar(self.sp[:, i, :], self.te[:, i, :], 0.5, 0.5, ALU.mult, ALU.add)\
            .then_inc(self.spikes.sem, 1)

    def vector_input_low(self, nc, dve, g):
        dve.wait_ge(self.c_full.sem, self.c_full.upto(g))
        dve.wait_ge(self.c_high.sem, self.c_high.upto(g))
        part = self.cs[M0:128, bass.ds(g % 2, 1), :].rearrange("p o n -> p (o n)")
        nc.vector.tensor_tensor(part, self.c32[M0:128, :], part.bitcast(F32), ALU.subtract)\
            .then_inc(self.c_ready.sem, 1)

    def vector_logits(self, nc, dve, g, bank):
        dve.wait_ge(self.l_made.sem, self.l_made.upto(g))
        self.router.vector_logits(nc, dve, g, bank, self.col("br"))
        self.router.vector_shift(nc, dve, g)

    def vector_residual(self, nc, dve, g, dn):
        dve.wait_ge(self.scaled.sem, self.scaled.upto(g))
        xg = self.x[:, bass.ds(g * NB, NB), :]
        nc.vector.tensor_tensor(xg, xg, dn[:, :, :], ALU.add).then_inc(self.x_done.sem, 1)

    def tensor_encode(self, nc, i, bank):
        split_product(nc, bank[:, :], *self.split("enc", i), self.xh[:, :], self.xl[:, :], True, True)\
            .then_inc(self.enc_made.sem, 1)

    def tensor_input(self, nc, pe, g, bank):
        for i in range(2):
            pe.wait_ge(self.spikes.sem, self.spikes.upto(g, i + 1))
            last = nc.tensor.matmul(bank[:, :], self.col("s2c", i, 128), self.sp[:, i, :], start=i == 0, stop=i == 1)
        last.then_inc(self.c_made.sem, 1)

    def tensor_logits(self, nc, pe, g, bank):
        pe.wait_ge(self.c_full.sem, self.c_full.upto(g))
        for t in range(NB):
            last = nc.tensor.matmul(bank[:, t * E0:(t + 1) * E0], self.c32[0:M0, t * T:(t + 1) * T],
                                    self.col("wr", rows=M0), start=True, stop=True)
        last.then_inc(self.l_made.sem, 1)


LPLAN = {"rate": 2, "stats": 1, "steps": 4, "rows": 9, "bias": 11, "turn": 13, "high": 12, "low": 13, "k": 12,
         "kc": 13, "q": 16, "qc": 17, "v": 17, "vc": 19, "s": 19, "shift": 19, "exp": 21, "tot": 24, "pturn": 22,
         "pc": 24, "o": 25, "res": 25, "stats2": 27, "steps2": 29, "rows2": 35, "turn2": 37, "high2": 37, "low2": 37,
         "wg": 38, "lg": 37, "ranks": 37, "rexp": 39, "gates": 43, "gates2": 44, "gturn": 46, "keep": 47}
TPLAN = {"rate": 7, "w1a": 11, "w1b": 13, "stats": 0, "steps": 0, "rows": 1, "bias": 3, "turn": 4, "high": 3,
         "low": 3, "k": 0, "kc": 5, "q": 6, "qc": 6, "v": 6, "vc": 6, "s": 7, "shift": 7, "exp": 8, "tot": 9,
         "pturn": 10, "pc": 10, "o": 11, "res": 11, "stats2": 12, "steps2": 13, "rows2": 15, "turn2": 17,
         "high2": 17, "low2": 18, "wg": 18, "lg": 17, "ranks": 17, "rexp": 19, "gates": 18, "gates2": 18,
         "gturn": 19, "keep": 19}


class Attention1:

    def __init__(self, nc, ctx, x, ctxt, cc, ident, tg, stats, mv, work, xn, xh, xl, bank_p, bank_r, signal_of):
        def sb(name, shape, dt=F32):
            return ctx.enter_context(nc.sbuf_tensor("a1_" + name, shape, dt))

        def signal(name, per):
            return signal_of("a1_" + name, per)

        def x_tile(g, t):
            return x[:, g * NB + t, :]

        self.nc, self.x, self.ctxt, self.ident, self.tg, self.xh, self.xl = nc, x, ctxt, ident, tg, xh, xl
        self.x_tile = x_tile
        self.bank_p = bank_p
        self.bank_r = bank_r
        self.xh1 = sb("xh1", [D, 2, GT], F32R)
        self.xl1 = sb("xl1", [D, 2, GT], F32R)
        self.gt1 = sb("gt1", [128, 2, GT], F32R)
        self.w1h = sb("w1h", [128, W1C], F32R)
        self.w1l = sb("w1l", [128, W1C], F32R)
        self.wl = sb("wl", [128, NL_COLS])
        self.wqh = sb("wqh", [D, D], F32R)
        self.wql = sb("wql", [D, D], F32R)
        self.bqs = sb("bqs", [128, 1])
        self.bvt = sb("bvt", [128, D])
        self.qt = sb("qt", [D, GT])
        self.kt = sb("kt", [D, 2, GS])
        self.v = sb("v", [S, 2, GT])
        self.top = sb("top", [T, NB])
        self.ss = sb("ss", [T, NB, S])
        self.ex = sb("ex", [T, NB, S])
        self.tot = sb("tot", [T, NB])
        self.pt = sb("pt", [S, GT])
        self.x32 = sb("x32", [D, GT])
        self.xn2 = sb("xn2", [128, NB, D])
        self.stats2 = sb("stats2", [128, NB, 6])
        self.mv2 = sb("mv2", [128, NB, 2])
        self.work2 = sb("work2", [128, 3, NB])
        self.norm = Norm(signal, "norm", x_tile, stats, mv, work, xn, ident)
        self.norm2 = Norm(signal, "norm2", x_tile, self.stats2, self.mv2, self.work2, self.xn2, ident)
        self.router = Router(signal, "router", sb, K1, cc("tri"), ident, 1)
        self.w_in = signal("w_in", 16)
        self.w1_in = signal("w1_in", 16)
        self.ctx_in = signal("ctx_in", 16)
        self.w_high = signal("w_high", 1)
        self.w_low = signal("w_low", 5)
        self.q_made = signal("q_made", 1)
        self.q_ready = signal("q_ready", 1)
        self.k_made = signal("k_made", 1)
        self.k_ready = signal("k_ready", 1)
        self.v_made = signal("v_made", 1)
        self.v_ready = signal("v_ready", 1)
        self.s_made = signal("s_made", 1)
        self.s_top = signal("s_top", 1)
        self.ss_ready = signal("ss_ready", 1)
        self.ex_ready = signal("ex_ready", 1)
        self.tot_steps = signal("tot_steps", 3)
        self.p_turned = signal("p_turned", 1)
        self.pt_ready = signal("pt_ready", 1)
        self.o_made = signal("o_made", 1)
        self.x_bias = signal("x_bias", 1)
        self.xa_done = signal("xa_done", NB + 1)
        self.x32_ready = signal("x32_ready", 1)
        self.l_made = signal("l_made", 1)
        self.h2_made = signal("h2_made", CH)
        self.g_made = signal("g_made", GATED)
        self.x_done = signal("x_done", 1)
        self.zeroed = signal("zeroed", 2)
        self.w1_high = signal("w1_high", 2)
        self.w1_low = signal("w1_low", 2)
        self.w3_in = signal("w3_in", 16)

    def col(self, name):
        a, b = WL[name]
        return self.wl[:, a:b]

    def of_parity(self, t, g):
        return t[:, bass.ds(g % 2, 1), :].rearrange("p o n -> p (o n)")

    def gpsimd(self, nc, pool):
        gt1, bvt, norm, router, x_bias = self.gt1, self.bvt, self.norm, self.router, self.x_bias
        zeroed, w_low, x = self.zeroed, self.w_low, self.x

        def bias(g):
            pool.wait_ge(w_low.sem, w_low.upto(0))
            pool.wait_ge(norm.rows.sem, norm.rows.upto(g))
            xg = x[:, bass.ds(g * NB, NB), :]
            nc.gpsimd.tensor_tensor(xg, xg, bvt.rearrange("p (o d) -> p o d", o=1).to_broadcast([T, NB, D]),
                                    ALU.add).then_inc(x_bias.sem, 1)

        def prepare():
            nc.gpsimd.memset(gt1[:, :, :].bitcast(F32), 0.0).then_inc(zeroed.sem, 1)

        def ahead(g, i, plan):
            if i == plan["bias"]:
                bias(g)
            if i == plan["ranks"]:
                router.gpsimd_ranks(nc, pool, g)

        return prepare, ahead

    def scalar(self, nc, act):
        xh1, gt1, wqh, bqs, qt = self.xh1, self.gt1, self.wqh, self.bqs, self.qt
        kt, v, ss, ex, pt = self.kt, self.v, self.ss, self.ex, self.pt
        x32, norm, norm2, router, w_in = self.x32, self.norm, self.norm2, self.router, self.w_in
        w_high, q_made, q_ready, k_made, k_ready = self.w_high, self.q_made, self.q_ready, self.k_made, self.k_ready
        v_made, v_ready, s_made, ss_ready, ex_ready = self.v_made, self.v_ready, self.s_made, self.ss_ready, self.ex_ready
        tot_steps, p_turned, pt_ready = self.tot_steps, self.p_turned, self.pt_ready
        o_made, x32_ready = self.o_made, self.x32_ready
        l_made, h2_made, g_made, bank_p, bank_r = self.l_made, self.h2_made, self.g_made, self.bank_p, self.bank_r
        of_parity, col = self.of_parity, self.col

        def tokens(g):
            if q_made.comes(g, back=1):
                act.wait_ge(q_made.sem, q_made.upto(g, back=1))
            norm.scalar_high(nc, act, g, bank_p, self.xh[:, :])

        def queries(g):
            act.wait_ge(q_made.sem, q_made.upto(g))
            if s_made.comes(g, back=1):
                act.wait_ge(s_made.sem, s_made.upto(g, back=1))
            nc.scalar.activation(qt[:, :], bank_p[:, :], ACT.Identity, bias=bqs[:, :], scale=D ** -0.5)\
                .then_inc(q_ready.sem, 1)

        def keys(g):
            act.wait_ge(k_made.sem, k_made.upto(g))
            if s_made.comes(g, back=2):
                act.wait_ge(s_made.sem, s_made.upto(g, back=2))
            nc.scalar.activation(kt[:, bass.ds(g % 2, 1), :], bank_r[:, 0:GS].rearrange("d (o n) -> d o n", o=1),
                                 ACT.Identity, bias=col("bk")).then_inc(k_ready.sem, 1)

        def values(g):
            act.wait_ge(v_made.sem, v_made.upto(g))
            if o_made.comes(g, back=2):
                act.wait_ge(o_made.sem, o_made.upto(g, back=2))
            nc.scalar.copy(v[:, bass.ds(g % 2, 1), :], bank_r[0:S, :].rearrange("d (o n) -> d o n", o=1))\
                .then_inc(v_ready.sem, 1)

        def exps(g):
            act.wait_ge(ss_ready.sem, ss_ready.upto(g))
            if p_turned.comes(g, back=1):
                act.wait_ge(p_turned.sem, p_turned.upto(g, back=1))
            if tot_steps.comes(g, 1, back=1):
                act.wait_ge(tot_steps.sem, tot_steps.upto(g, 1, back=1))
            nc.scalar.activation(ex[:, :, :], ss[:, :, :], ACT.Exp).then_inc(ex_ready.sem, 1)

        def turned(g):
            act.wait_ge(p_turned.sem, p_turned.upto(g))
            if o_made.comes(g, back=1):
                act.wait_ge(o_made.sem, o_made.upto(g, back=1))
            nc.scalar.copy(pt[:, :], bank_r[0:S, :]).then_inc(pt_ready.sem, 1)

        def tokens2(g):
            if l_made.comes(g, back=1):
                act.wait_ge(l_made.sem, l_made.upto(g, back=1))
            act.wait_ge(norm2.turned.sem, norm2.turned.upto(g))
            nc.scalar.copy(x32[:, :], bank_r[:, :]).then_inc(x32_ready.sem, 1)
            if h2_made.comes(g, back=2):
                act.wait_ge(h2_made.sem, h2_made.upto(g, back=2))
            norm2.scalar_high(nc, act, g, bank_r, of_parity(xh1, g))

        def keep_gates(g):
            if g_made.comes(g, back=2):
                act.wait_ge(g_made.sem, g_made.upto(g, back=2))
            router.scalar_keep(nc, act, g, bank_r, gt1[0:2 * (E1 + 1), bass.ds(g % 2, 1), :].rearrange("p o n -> p (o n)"))

        def prepare():
            act.wait_ge(w_in.sem, w_in.upto(0))
            nc.scalar.copy(wqh[:, :], col("q")).then_inc(w_high.sem, 1)

        def ahead(g, i, plan):
            if i == plan["high"]:
                tokens(g)
            if i == plan["kc"]:
                keys(g)
            if i == plan["qc"]:
                queries(g)
            if i == plan["vc"]:
                values(g)
            if i == plan["exp"]:
                exps(g)
            if i == plan["pc"]:
                turned(g)
            if i == plan["high2"]:
                tokens2(g)
            if i == plan["rexp"]:
                router.scalar_exp(nc, act, g)
            if i == plan["keep"]:
                keep_gates(g)

        return prepare, ahead

    def vector(self, nc, dve):
        xh1, xl1, wqh, wql, bqs = self.xh1, self.xl1, self.wqh, self.wql, self.bqs
        bvt, top, ss, ex, tot = self.bvt, self.top, self.ss, self.ex, self.tot
        norm, norm2, router, w_in, w_high = self.norm, self.norm2, self.router, self.w_in, self.w_high
        w_low, s_made, s_top, ss_ready, ex_ready = self.w_low, self.s_made, self.s_top, self.ss_ready, self.ex_ready
        tot_steps, o_made, x_bias, xa_done, l_made = self.tot_steps, self.o_made, self.x_bias, self.xa_done, self.l_made
        tg, bank_p, bank_r, of_parity, x_tile = self.tg, self.bank_p, self.bank_r, self.of_parity, self.x_tile
        col = self.col

        def shift(g):
            scores = bank_p[:, 0:GS].rearrange("t (b s) -> t b s", b=NB)
            dve.wait_ge(s_made.sem, s_made.upto(g))
            nc.vector.tensor_reduce(top[:, :], scores, AX.X, ALU.max).then_inc(s_top.sem, 1)
            dve.wait_ge(s_top.sem, s_top.upto(g))
            if ex_ready.comes(g, back=1):
                dve.wait_ge(ex_ready.sem, ex_ready.upto(g, back=1))
            nc.vector.tensor_tensor(ss[:, :, :], scores,
                                    top.rearrange("t (b o) -> t b o", o=1).to_broadcast([T, NB, S]),
                                    ALU.subtract).then_inc(ss_ready.sem, 1)

        def totals(g):
            dve.wait_ge(ex_ready.sem, ex_ready.upto(g))
            if xa_done.comes(g, back=1):
                dve.wait_ge(xa_done.sem, xa_done.upto(g, back=1))
            nc.vector.tensor_reduce(tot[:, :], ex[:, :, :], AX.X, ALU.add).then_inc(tot_steps.sem, 1)
            dve.wait_ge(tot_steps.sem, tot_steps.upto(g, 1))
            nc.vector.reciprocal(tot[:, :], tot[:, :]).then_inc(tot_steps.sem, 1)
            dve.wait_ge(tot_steps.sem, tot_steps.upto(g, 2))
            nc.vector.tensor_scalar(tot[:, :], tot[:, :], tg[:, 1:2], None, ALU.mult).then_inc(tot_steps.sem, 1)

        def residual(g):
            dve.wait_ge(o_made.sem, o_made.upto(g))
            dve.wait_ge(tot_steps.sem, tot_steps.upto(g))
            dve.wait_ge(x_bias.sem, x_bias.upto(g))
            for t in range(NB):
                nc.vector.scalar_tensor_tensor(out=x_tile(g, t), in0=bank_p[:, t * D:(t + 1) * D],
                                               scalar=tot[:, t:t + 1], in1=x_tile(g, t), op0=ALU.mult,
                                               op1=ALU.add).then_inc(xa_done.sem, 1)

        def logits(g):
            dve.wait_ge(l_made.sem, l_made.upto(g))
            router.vector_logits(nc, dve, g, bank_p, col("rb"))
            router.vector_shift(nc, dve, g)

        def prepare():
            dve.wait_ge(w_in.sem, w_in.upto(0))
            nc.vector.memset(router.parts[:, :, E1:E1 + 1], 1.0).then_inc(w_low.sem, 1)
            nc.vector.memset(router.parts[:, :, 2 * E1 + 1:2 * E1 + 2], 0.0).then_inc(w_low.sem, 1)
            nc.vector.tensor_scalar(bqs[:, :], col("bq"), D ** -0.5, None, ALU.mult).then_inc(w_low.sem, 1)
            nc.vector.tensor_scalar(bvt[:, :], col("bv"), tg[:, 1:2], None, ALU.mult).then_inc(w_low.sem, 1)
            dve.wait_ge(w_high.sem, w_high.upto(0))
            nc.vector.tensor_tensor(wql[:, :], col("q"), wqh[:, :].bitcast(F32), ALU.subtract)\
                .then_inc(w_low.sem, 1)

        def ahead(g, i, plan):
            for at, n in (("stats", norm), ("stats2", norm2)):
                if i == plan[at]:
                    if n is norm2:
                        dve.wait_ge(xa_done.sem, xa_done.upto(g, NB))
                        dve.sem_inc(xa_done.sem, 1)
                    n.vector_stats(nc, g)
                    n.vector_moments(nc, dve, g)
            for at, n in (("steps", norm), ("steps2", norm2)):
                rate = plan["rate"]
                for j in range(rate * (i - plan[at]), min(rate * (i - plan[at] + 1), STEPS)):
                    if j >= 0:
                        n.vector_step(nc, dve, g, j)
            if i == plan["rows"]:
                norm.vector_rows(nc, dve, g)
            if i == plan["low"]:
                norm.vector_low(nc, dve, g, bank_p, self.xh[:, :], self.xl[:, :])
            if i == plan["shift"]:
                shift(g)
            if i == plan["tot"]:
                totals(g)
            if i == plan["res"]:
                residual(g)
            if i == plan["rows2"]:
                norm2.vector_rows(nc, dve, g)
            if i == plan["low2"]:
                norm2.vector_low(nc, dve, g, bank_r, of_parity(xh1, g), of_parity(xl1, g))
            if i == plan["lg"]:
                logits(g)
            if i == plan["gates"]:
                router.vector_gates(nc, dve, g)
            if i == plan["gates2"]:
                router.vector_gates2(nc, dve, g)

        return prepare, ahead

    def tensor(self, nc, pe):
        wqh, wql, qt, kt, v = self.wqh, self.wql, self.qt, self.kt, self.v
        ex, pt, x32, norm, norm2 = self.ex, self.pt, self.x32, self.norm, self.norm2
        router, ctx_in, q_made, q_ready, k_made = self.router, self.ctx_in, self.q_made, self.q_ready, self.k_made
        k_ready, v_made, v_ready, s_made = self.k_ready, self.v_made, self.v_ready, self.s_made
        ex_ready, p_turned, pt_ready = self.ex_ready, self.p_turned, self.pt_ready
        o_made, xa_done = self.o_made, self.xa_done
        x32_ready, l_made, x_done, ctxt, ident = self.x32_ready, self.l_made, self.x_done, self.ctxt, self.ident
        bank_p, bank_r, col = self.bank_p, self.bank_r, self.col

        def turn_tokens(g):
            if router.logits.comes(g, back=1):
                pe.wait_ge(router.logits.sem, router.logits.upto(g, back=1))
            if x_done.comes(g, back=2):
                pe.wait_ge(x_done.sem, x_done.upto(g, back=2))
            norm.tensor_turn(nc, pe, g, bank_p)

        def queries(g):
            pe.wait_ge(norm.low.sem, norm.low.upto(g))
            split_product(nc, bank_p[:, :], wqh[:, :], wql[:, :], self.xh[:, :], self.xl[:, :], True, True)\
                .then_inc(q_made.sem, 1)

        def keys(g):
            pe.wait_ge(ctx_in.sem, ctx_in.upto(g))
            if router.ready.comes(g, back=1):
                pe.wait_ge(router.ready.sem, router.ready.upto(g, back=1))
            nc.tensor.matmul(bank_r[:, 0:GS], col("k"), ctxt[:, :], start=True, stop=True)\
                .then_inc(k_made.sem, 1)

        def values(g):
            pe.wait_ge(k_ready.sem, k_ready.upto(g))
            for b in range(NB):
                last = nc.tensor.matmul(bank_r[0:S, b * D:(b + 1) * D], ctxt[:, b * S:(b + 1) * S], col("v"),
                                        start=True, stop=True)
            last.then_inc(v_made.sem, 1)

        def scores(g):
            pe.wait_ge(q_ready.sem, q_ready.upto(g))
            pe.wait_ge(k_ready.sem, k_ready.upto(g))
            for b in range(NB):
                last = nc.tensor.matmul(bank_p[:, b * S:(b + 1) * S], qt[:, b * T:(b + 1) * T],
                                        kt[:, bass.ds(g % 2, 1), b * S:(b + 1) * S].rearrange("d o n -> d (o n)"),
                                        start=True, stop=True)
            last.then_inc(s_made.sem, 1)

        def turn_weights(g):
            pe.wait_ge(ex_ready.sem, ex_ready.upto(g))
            pe.wait_ge(v_ready.sem, v_ready.upto(g))
            for b in range(NB):
                last = nc.tensor.transpose(bank_r[0:S, b * T:(b + 1) * T], ex[:, b, :], ident)
            last.then_inc(p_turned.sem, 1)

        def attend(g):
            pe.wait_ge(pt_ready.sem, pt_ready.upto(g))
            pe.wait_ge(v_ready.sem, v_ready.upto(g))
            for b in range(NB):
                last = nc.tensor.matmul(bank_p[:, b * D:(b + 1) * D], pt[:, b * T:(b + 1) * T],
                                        v[:, bass.ds(g % 2, 1), b * D:(b + 1) * D].rearrange("s o n -> s (o n)"),
                                        start=True, stop=True)
            last.then_inc(o_made.sem, 1)

        def turn_tokens2(g):
            pe.wait_ge(pt_ready.sem, pt_ready.upto(g))
            norm2.tensor_turn(nc, pe, g, bank_r)

        def logits(g):
            pe.wait_ge(x32_ready.sem, x32_ready.upto(g))
            pe.wait_ge(xa_done.sem, xa_done.upto(g, NB))
            for t in range(NB):
                last = nc.tensor.matmul(bank_p[:, t * E1:(t + 1) * E1], x32[:, t * T:(t + 1) * T], col("wg"),
                                        start=True, stop=True)
            last.then_inc(l_made.sem, 1)

        def turn_gates(g):
            pe.wait_ge(norm2.low.sem, norm2.low.upto(g))
            router.tensor_turn(nc, pe, g, bank_r)

        def ahead(g, i, plan):
            if i == plan["turn"]:
                turn_tokens(g)
            if i == plan["k"]:
                keys(g)
            if i == plan["q"]:
                queries(g)
            if i == plan["v"]:
                values(g)
            if i == plan["s"]:
                scores(g)
            if i == plan["pturn"]:
                turn_weights(g)
            if i == plan["o"]:
                attend(g)
            if i == plan["turn2"]:
                turn_tokens2(g)
            if i == plan["wg"]:
                logits(g)
            if i == plan["gturn"]:
                turn_gates(g)

        return ahead


FPLAN = {"turn": 0, "high": 0, "low": 0, "enc0": 2, "enc1": 3, "tanh0": 3, "tanh1": 3, "spikes0": 2, "spikes1": 2,
         "s2c": 6, "input": 7, "input_low": 7, "wr": 8, "logits": 8, "exp": 10, "ranks": 7, "gates": 12,
         "turn_gates": 15, "keep": 15, "out_high": 5, "out_low": 5, "m0": 8, "m_tanh0": 9, "m_spikes0": 10, "m1": 11,
         "m_tanh1": 11, "m_spikes1": 11, "decode": 15, "decoded": 14, "stats": 1, "scale": 9, "scale2": 10,
         "residual": 14}


def layer0_ffn(nc, f0, fr, a1, tg, xh, xl, w123, w123_d, w123_in, wl_d, ctxt_d, signal_of):
    with ExitStack() as ctx:
        def sb(name, shape, dt=F32):
            return ctx.enter_context(nc.sbuf_tensor("f0_" + name, shape, dt))

        def pb(name):
            return ctx.enter_context(nc.psum_tensor("f0_" + name, [128, 512], F32))

        def signal(name, per):
            return signal_of("f0_" + name, per)

        sel_raw = f0["sel_raw"]
        sel = sb("sel", [128, E0 * 128], F32R)
        gt = sb("gt", [128, 2, GT], F32R)
        r = sb("r", [EH0, 2, GT])
        hp = sb("hp", [EH0, 2, GT])
        hh = sb("hh", [EH0, 4, GT], F32R)
        hl = sb("hl", [EH0, 4, GT], F32R)
        ys = sb("ys", [128, GT], F32R)
        tm = sb("tm", [128, 2, GT])
        sm = sb("sm", [128, 2, GT])
        dec = sb("dec", [T, NB, D])
        dn = sb("dn", [T, NB, D])
        split, col, half_b, gl = fr.split, fr.col, fr.half_b, fr.gl
        bank_a = [a1.bank_p, a1.bank_r]
        bank_z = [pb("z0"), pb("z1")]
        bank_g = [pb("g0"), pb("g1")]
        bank_y = pb("y")
        bank_c = pb("c")

        norm, router, spikes, enc_made, enc_tanh = fr.norm, fr.router, fr.spikes, fr.enc_made, fr.enc_tanh
        c_high, c_ready = fr.c_high, fr.c_ready
        norm2 = fr.norm2_last.over(lambda g, t: dec[:, t, :], dn)
        zeroed = signal("zeroed", 2)
        sel_ready = signal("sel_ready", 1)
        gl_ready = signal("gl_ready", 1)
        z_made = signal("z_made", E0)
        g_made = signal("g_made", E0)
        r_ready = signal("r_ready", E0)
        hp_ready = signal("hp_ready", E0)
        hh_ready = signal("hh_ready", E0)
        hl_ready = signal("hl_ready", E0)
        y_made = signal("y_made", E0)
        ys_high = signal("ys_high", 1)
        ys_ready = signal("ys_ready", 1)
        m_made = signal("m_made", 2)
        m_tanh = signal("m_tanh", 2)
        m_spikes = signal("m_spikes", 2)
        d_made = signal("d_made", 1)
        d_ready = signal("d_ready", 1)

        def before(e, by):
            return (0, e - by) if e >= by else (1, e - by + E0)

        with nc.Block() as block:

            @block.sync
            def _(sp_):
                sp_.dma_start(a1.wl[:, :], wl_d).then_inc(a1.w_in.sem, 16)
                sp_.dma_start(a1.ctxt[:, :], ctxt_d[:, 0:GS]).then_inc(a1.ctx_in.sem, 16)
                sp_.dma_start(w123[:, :], w123_d[:, 0:W1C]).then_inc(a1.w1_in.sem, 16)
                sp_.dma_start(f0["ws"][:, :], w123_d[:, W1C:2 * W1C]).then_inc(w123_in, 16)
                sp_.wait_ge(a1.w1_low.sem, a1.w1_low.upto(0))
                sp_.dma_start(w123[:, :], w123_d[:, 2 * W1C:3 * W1C]).then_inc(a1.w3_in.sem, 16)

            @block.gpsimd
            def _(pool):
                def low(g, e):
                    pool.wait_ge(hh_ready.sem, hh_ready.upto(g, e + 1))
                    back, v = before(e, 4)
                    if y_made.comes(g, v + 1, back=back):
                        pool.wait_ge(y_made.sem, y_made.upto(g, v + 1, back=back))
                    nc.gpsimd.tensor_tensor(hl[:, e % 4, :], hp[:, e % 2, :], hh[:, e % 4, :].bitcast(F32),
                                            ALU.subtract).then_inc(hl_ready.sem, 1)

                def scale(g, i):
                    fr.gpsimd_scale(nc, pool, g, i, dn)

                prepare, ahead1 = a1.gpsimd(nc, pool)

                def others(g, i, behind, more):
                    if not more:
                        ahead1(0, i, TPLAN)
                    if more and i == FPLAN["ranks"]:
                        router.gpsimd_ranks(nc, pool, g + 1)
                    if behind >= 2 and i == FPLAN["scale"]:
                        scale(g - 2, 0)
                    if behind >= 2 and i == FPLAN["scale2"]:
                        scale(g - 2, 1)

                def group(g, behind, more):
                    for e in range(E0):
                        low(g, e)
                        others(g, 2 * e, behind, more)
                        others(g, 2 * e + 1, behind, more)

                nc.gpsimd.memset(sel[:, :].bitcast(F32), 0.0).then_inc(zeroed.sem, 1)
                group(0, 0, True)
                group(1, 1, True)
                pool.wait_ge(gl_ready.sem, gl_ready.upto(0))
                with pool.Fori(2, G - 1) as g:
                    group(g, 2, True)
                prepare()
                group(G - 1, 2, False)
                for i in range(2):
                    n = slice(i * W1C // 2, (i + 1) * W1C // 2)
                    pool.wait_ge(a1.w1_high.sem, a1.w1_high.upto(0, i + 1))
                    nc.gpsimd.tensor_tensor(a1.w1l[:, n], w123[:, n], a1.w1h[:, n].bitcast(F32), ALU.subtract)\
                        .then_inc(a1.w1_low.sem, 1)
                for i in range(2):
                    ahead1(0, 2 * E0 + 2 * i, TPLAN)
                    ahead1(0, 2 * E0 + 2 * i + 1, TPLAN)
                    scale(G - 2, i)
                for n in range(4, 16):
                    ahead1(0, 2 * E0 + n, TPLAN)

            @block.scalar
            def _(act):
                act.wait_ge(zeroed.sem, zeroed.upto(0))
                nc.scalar.copy(sel[0:2 * E0, :], sel_raw[:, :]).then_inc(sel_ready.sem, 1)

                def keep_gates(g):
                    if y_made.comes(g, back=2):
                        act.wait_ge(y_made.sem, y_made.upto(g, back=2))
                    router.scalar_keep(nc, act, g, bank_a[1],
                                       gt[0:2 * E0, bass.ds(g % 2, 1), :].rearrange("p o n -> p (o n)"))

                def relu(g, e):
                    act.wait_ge(z_made.sem, z_made.upto(g, e + 1))
                    back, v = before(e, 2)
                    if hp_ready.comes(g, v + 1, back=back):
                        act.wait_ge(hp_ready.sem, hp_ready.upto(g, v + 1, back=back))
                    nc.scalar.activation(r[:, e % 2, :], bank_z[e % 2][:, :], ACT.Relu, bias=col("b1", e, 1))\
                        .then_inc(r_ready.sem, 1)

                def high(g, e):
                    act.wait_ge(hp_ready.sem, hp_ready.upto(g, e + 1))
                    back, v = before(e, 4)
                    if y_made.comes(g, v + 1, back=back):
                        act.wait_ge(y_made.sem, y_made.upto(g, v + 1, back=back))
                    nc.scalar.copy(hh[:, e % 4, :], hp[:, e % 2, :]).then_inc(hh_ready.sem, 1)

                def out_high(g):
                    act.wait_ge(y_made.sem, y_made.upto(g))
                    if m_made.comes(g, back=1):
                        act.wait_ge(m_made.sem, m_made.upto(g, back=1))
                    nc.scalar.copy(ys[:, :], bank_y[:, :]).then_inc(ys_high.sem, 1)

                def m_tanh_(g, i):
                    act.wait_ge(m_made.sem, m_made.upto(g, i + 1))
                    if m_spikes.comes(g, i + 1, back=1):
                        act.wait_ge(m_spikes.sem, m_spikes.upto(g, i + 1, back=1))
                    nc.scalar.activation(tm[:, i, :], bank_c[:, :], ACT.Tanh, bias=half_b[:, 2 + i:3 + i],
                                         scale=0.5).then_inc(m_tanh.sem, 1)

                prepare, ahead1 = a1.scalar(nc, act)

                def others(g, i, behind, more):
                    if not more:
                        if i == TPLAN["high"]:
                            act.wait_ge(enc_made.sem, enc_made.upto(G - 1))
                        ahead1(0, i, TPLAN)
                        if i in (TPLAN["w1a"], TPLAN["w1b"]):
                            n = slice(0, W1C // 2) if i == TPLAN["w1a"] else slice(W1C // 2, W1C)
                            act.wait_ge(a1.w1_in.sem, a1.w1_in.upto(0))
                            nc.scalar.copy(a1.w1h[:, n], w123[:, n]).then_inc(a1.w1_high.sem, 1)
                    if behind >= 1 and i == FPLAN["out_high"]:
                        out_high(g - 1)
                    if behind >= 1 and i == FPLAN["m_tanh0"]:
                        m_tanh_(g - 1, 0)
                    if behind >= 1 and i == FPLAN["m_tanh1"]:
                        m_tanh_(g - 1, 1)
                    if not more:
                        return
                    if i == FPLAN["high"]:
                        norm.scalar_high(nc, act, g + 1, bank_a[0], xh[:, :])
                    if i == FPLAN["tanh0"]:
                        fr.scalar_tanh(nc, act, g + 1, 0, bank_a[1])
                    if i == FPLAN["tanh1"]:
                        fr.scalar_tanh(nc, act, g + 1, 1, bank_a[0])
                    if i == FPLAN["input"]:
                        fr.scalar_full(nc, act, g + 1, bank_a[1])
                        if z_made.comes(g + 1, back=2):
                            act.wait_ge(z_made.sem, z_made.upto(g + 1, back=2))
                        fr.scalar_part(nc, g + 1, bank_a[1])
                    if i == FPLAN["exp"]:
                        router.scalar_exp(nc, act, g + 1)
                    if i == FPLAN["keep"]:
                        keep_gates(g + 1)

                def group(g, behind, more):
                    for e in range(E0):
                        relu(g, e)
                        others(g, 2 * e, behind, more)
                        if e >= 1:
                            high(g, e - 1)
                        elif behind:
                            high(g - 1, E0 - 1)
                        others(g, 2 * e + 1, behind, more)

                keep_gates(0)
                group(0, 0, True)
                group(1, 1, True)
                with act.Fori(2, G - 1) as g:
                    group(g, 2, True)
                prepare()
                group(G - 1, 2, False)
                high(G - 1, E0 - 1)
                out_high(G - 1)
                ahead1(0, 16, TPLAN)
                m_tanh_(G - 1, 0)
                ahead1(0, 17, TPLAN)
                m_tanh_(G - 1, 1)
                for i in range(18, 32):
                    ahead1(0, i, TPLAN)

            @block.vector
            def _(dve):
                def gated(g, e):
                    dve.wait_ge(r_ready.sem, r_ready.upto(g, e + 1))
                    dve.wait_ge(g_made.sem, g_made.upto(g, e + 1))
                    back, v = before(e, 2)
                    if hl_ready.comes(g, v + 1, back=back):
                        dve.wait_ge(hl_ready.sem, hl_ready.upto(g, v + 1, back=back))
                    nc.vector.tensor_tensor(hp[:, e % 2, :], bank_g[e % 2][:, :], r[:, e % 2, :], ALU.mult)\
                        .then_inc(hp_ready.sem, 1)

                def out_low(g):
                    dve.wait_ge(ys_high.sem, ys_high.upto(g))
                    nc.vector.tensor_tensor(ys[M0:128, :], bank_y[M0:128, :], ys[M0:128, :].bitcast(F32), ALU.subtract)\
                        .then_inc(ys_ready.sem, 1)

                def moe_spikes(g, i):
                    dve.wait_ge(m_tanh.sem, m_tanh.upto(g, i + 1))
                    if d_made.comes(g, back=1):
                        dve.wait_ge(d_made.sem, d_made.upto(g, back=1))
                    nc.vector.tensor_scalar(sm[:, i, :], tm[:, i, :], 0.5, 0.5, ALU.mult, ALU.add)\
                        .then_inc(m_spikes.sem, 1)

                def decoded(g, out=dec):
                    dve.wait_ge(d_made.sem, d_made.upto(g))
                    if norm2.rows.comes(g, back=1):
                        dve.wait_ge(norm2.rows.sem, norm2.rows.upto(g, back=1))
                    nc.vector.tensor_tensor(out[:, :, :], bank_c.rearrange("p (t d) -> p t d", t=NB),
                                            col("b_dec").rearrange("p (o d) -> p o d", o=1).to_broadcast([128, NB, D]),
                                            ALU.add).then_inc(d_ready.sem, 1)

                def residual(g):
                    fr.vector_residual(nc, dve, g, dn)

                prepare, ahead1 = a1.vector(nc, dve)

                def others(g, i, behind, more, more2):
                    if not more:
                        if i == TPLAN["rows"]:
                            dve.wait_ge(norm.turned.sem, norm.turned.upto(G - 1))
                        if i == TPLAN["low"]:
                            dve.wait_ge(enc_made.sem, enc_made.upto(G - 1))
                        ahead1(0, i, TPLAN)
                    if behind >= 1 and i == FPLAN["out_low"]:
                        out_low(g - 1)
                    if more and i == FPLAN["low"]:
                        norm.vector_low(nc, dve, g + 1, bank_a[0], xh[:, :], xl[:, :])
                    if more and i == FPLAN["spikes0"]:
                        fr.vector_spikes(nc, dve, g + 1, 0)
                    if more and i == FPLAN["spikes1"]:
                        fr.vector_spikes(nc, dve, g + 1, 1)
                    if more and i == FPLAN["input_low"]:
                        fr.vector_input_low(nc, dve, g + 1)
                    if more and i == FPLAN["logits"]:
                        fr.vector_logits(nc, dve, g + 1, bank_a[0])
                    if behind >= 1 and i == FPLAN["m_spikes0"]:
                        moe_spikes(g - 1, 0)
                    if more and i == FPLAN["gates"]:
                        router.vector_gates(nc, dve, g + 1)
                        router.vector_gates2(nc, dve, g + 1)
                    if behind >= 1 and i == FPLAN["m_spikes1"]:
                        moe_spikes(g - 1, 1)
                    if behind >= 1 and i == FPLAN["decoded"]:
                        decoded(g - 1)
                    if behind >= 2 and i == FPLAN["residual"]:
                        residual(g - 2)
                    k = i - FPLAN["stats"]
                    if k == 0:
                        if behind >= 2:
                            dve.wait_ge(d_ready.sem, d_ready.upto(g - 2))
                            norm2.vector_stats(nc, g - 2)
                        if more2:
                            norm.vector_stats(nc, g + 2)
                        if behind >= 2:
                            norm2.vector_moments(nc, dve, g - 2)
                        if more2:
                            norm.vector_moments(nc, dve, g + 2)
                    if 1 <= k <= STEPS // 2:
                        for j in (2 * k - 2, 2 * k - 1):
                            if behind >= 2:
                                norm2.vector_step(nc, dve, g - 2, j)
                            if more2:
                                norm.vector_step(nc, dve, g + 2, j)
                    if behind >= 2 and k == STEPS // 2 + 1:
                        norm2.vector_rows(nc, dve, g - 2)
                    if more2 and k == STEPS // 2 + 2:
                        norm.vector_rows(nc, dve, g + 2)

                def group(g, behind, more, more2):
                    for e in range(E0):
                        gated(g, e)
                        others(g, 2 * e, behind, more, more2)
                        others(g, 2 * e + 1, behind, more, more2)

                nc.vector.memset(gt[:, :, :].bitcast(F32), 0.0).then_inc(zeroed.sem, 1)
                a, b = WF["ln_g"][0], WF["ln_b"][1]
                nc.vector.tensor_scalar(gl.rearrange("p a d -> p (a d)"), f0["wf"][:, a:b], tg[:, 2:3], None, ALU.mult)\
                    .then_inc(gl_ready.sem, 1)
                group(0, 0, True, True)
                group(1, 1, True, True)
                with dve.Fori(2, G - 2) as g:
                    group(g, 2, True, True)
                group(G - 2, 2, True, False)
                prepare()
                group(G - 1, 2, False, False)

                out_low(G - 1)
                dve.wait_ge(d_ready.sem, d_ready.upto(G - 2))
                norm2.vector_stats(nc, G - 2)
                norm2.vector_moments(nc, dve, G - 2)
                for i in range(STEPS):
                    norm2.vector_step(nc, dve, G - 2, i)
                    if i == STEPS // 3:
                        moe_spikes(G - 1, 0)
                        ahead1(0, 16, TPLAN)
                norm2.vector_rows(nc, dve, G - 2)
                ahead1(0, 17, TPLAN)
                moe_spikes(G - 1, 1)
                ahead1(0, 18, TPLAN)
                for i in range(19, 32):
                    ahead1(0, i, TPLAN)
                    if i == 22:
                        residual(G - 2)
                dve.wait_ge(spikes.sem, spikes.upto(G - 1))
                decoded(G - 1, fr.dec_last)

            @block.tensor
            def _(pe):
                def turn_tokens(g):
                    if router.logits.comes(g, back=1):
                        pe.wait_ge(router.logits.sem, router.logits.upto(g, back=1))
                    norm.tensor_turn(nc, pe, g, bank_a[0])

                def encode(g, i):
                    pe.wait_ge(norm.low.sem, norm.low.upto(g))
                    if i == 0:
                        if router.ready.comes(g, back=1):
                            pe.wait_ge(router.ready.sem, router.ready.upto(g, back=1))
                    fr.tensor_encode(nc, i, bank_a[1 - i])

                def turn_gates(g):
                    pe.wait_ge(c_high.sem, c_high.upto(g))
                    router.tensor_turn(nc, pe, g, bank_a[1])

                def hidden(g, e):
                    pe.wait_ge(c_ready.sem, c_ready.upto(g))
                    back, v = before(e, 2)
                    if r_ready.comes(g, v + 1, back=back):
                        pe.wait_ge(r_ready.sem, r_ready.upto(g, v + 1, back=back))
                    high_, low_ = split("w1", e)
                    both = fr.cs_of(g)
                    nc.tensor.matmul(bank_z[e % 2][:, :], low_, both, start=True, stop=False)
                    nc.tensor.matmul(bank_z[e % 2][:, :], high_, both, start=False, stop=True).then_inc(z_made.sem, 1)

                def gates_of(g):
                    return gt[:, bass.ds(g % 2, 1), :].rearrange("p o n -> p (o n)")

                def spread_gate(g, e):
                    if e == 0:
                        pe.wait_ge(sel_ready.sem, sel_ready.upto(0))
                    pe.wait_ge(router.ready.sem, router.ready.upto(g))
                    back, v = before(e, 2)
                    if hp_ready.comes(g, v + 1, back=back):
                        pe.wait_ge(hp_ready.sem, hp_ready.upto(g, v + 1, back=back))
                    nc.tensor.matmul(bank_g[e % 2][:, :], sel[:, e * 128:(e + 1) * 128], gates_of(g), start=True,
                                     stop=True).then_inc(g_made.sem, 1)

                def second_bias(g):
                    if ys_ready.comes(g, back=1):
                        pe.wait_ge(ys_ready.sem, ys_ready.upto(g, back=1))
                    high_, low_ = split("b2", 0)
                    nc.tensor.matmul(bank_y[:, :], low_, gates_of(g), start=True, stop=False)
                    nc.tensor.matmul(bank_y[:, :], high_, gates_of(g), start=False, stop=False)

                def output(g, e):
                    if e == 0:
                        second_bias(g)
                    pe.wait_ge(hh_ready.sem, hh_ready.upto(g, e + 1))
                    pe.wait_ge(hl_ready.sem, hl_ready.upto(g, e + 1))
                    split_product(nc, bank_y[:, :], *split("w2", e), hh[:, e % 4, :], hl[:, e % 4, :], False, e == E0 - 1)\
                        .then_inc(y_made.sem, 1)

                def to_spikes(g, i):
                    pe.wait_ge(ys_ready.sem, ys_ready.upto(g))
                    if i:
                        pe.wait_ge(m_tanh.sem, m_tanh.upto(g, 1))
                    else:
                        if d_ready.comes(g, back=1):
                            pe.wait_ge(d_ready.sem, d_ready.upto(g, back=1))
                    high_, low_ = split("c2s", i)
                    nc.tensor.matmul(bank_c[:, :], low_, ys[:, :], start=True, stop=False)
                    nc.tensor.matmul(bank_c[:, :], high_, ys[:, :], start=False, stop=True).then_inc(m_made.sem, 1)

                def decode(g):
                    pe.wait_ge(m_spikes.sem, m_spikes.upto(g))
                    for t in range(NB):
                        for i in range(2):
                            last = nc.tensor.matmul(bank_c[:, t * D:(t + 1) * D], sm[:, i, t * T:(t + 1) * T],
                                                    col("dec", i, D), start=i == 0, stop=i == 1)
                    last.then_inc(d_made.sem, 1)

                ahead1 = a1.tensor(nc, pe)

                def others(g, i, behind, more):
                    if not more:
                        if i == TPLAN["turn"]:
                            pe.wait_ge(router.logits.sem, router.logits.upto(G - 1))
                        if i == TPLAN["k"]:
                            pe.wait_ge(router.ready.sem, router.ready.upto(G - 1))
                        ahead1(0, i, TPLAN)
                    if behind >= 1 and i == FPLAN["m0"]:
                        to_spikes(g - 1, 0)
                    if behind >= 1 and i == FPLAN["m1"]:
                        to_spikes(g - 1, 1)
                    if behind >= 1 and i == FPLAN["decode"]:
                        decode(g - 1)
                    if not more:
                        return
                    if i == FPLAN["turn"]:
                        turn_tokens(g + 1)
                    if i == FPLAN["enc0"]:
                        encode(g + 1, 0)
                    if i == FPLAN["enc1"]:
                        encode(g + 1, 1)
                    if i == FPLAN["s2c"]:
                        fr.tensor_input(nc, pe, g + 1, bank_a[1])
                    if i == FPLAN["wr"]:
                        pe.wait_ge(enc_tanh.sem, enc_tanh.upto(g + 1))
                        fr.tensor_logits(nc, pe, g + 1, bank_a[0])
                    if i == FPLAN["turn_gates"]:
                        turn_gates(g + 1)

                def group(g, behind, more):
                    for e in range(E0):
                        hidden(g, e)
                        spread_gate(g, e)
                        others(g, 2 * e, behind, more)
                        if e >= 3:
                            output(g, e - 3)
                        elif behind:
                            output(g - 1, e - 3 + E0)
                        others(g, 2 * e + 1, behind, more)

                turn_gates(0)
                group(0, 0, True)
                group(1, 1, True)
                with pe.Fori(2, G - 1) as g:
                    group(g, 2, True)
                pe.wait_ge(a1.w_low.sem, a1.w_low.upto(0))
                group(G - 1, 2, False)
                for e in range(E0 - 3, E0):
                    output(G - 1, e)
                ahead1(0, 16, TPLAN)
                to_spikes(G - 1, 0)
                ahead1(0, 17, TPLAN)
                to_spikes(G - 1, 1)
                ahead1(0, 18, TPLAN)
                decode(G - 1)
                for i in range(19, 32):
                    ahead1(0, i, TPLAN)


def layer1(nc, f0, fr, a1, x, ident, tg, ctxt, w123, ctxt_d, sel1_d, out_d, w123_in, signal_of):
    LAG = 3
    REST = 6
    with ExitStack() as ctx:
        def sb(name, shape, dt=F32):
            return ctx.enter_context(nc.sbuf_tensor("l1_" + name, shape, dt))

        def pb(name):
            return ctx.enter_context(nc.psum_tensor("l1_" + name, [128, 512], F32))

        def signal(name, per):
            return signal_of("l1_" + name, per)

        wh = [a1.w1h, sb("w2h", [128, W1C], F32R), f0["wh"]]
        wlo = [a1.w1l, sb("w2l", [128, W1C], F32R), f0["wl"]]
        came_to = [w123, f0["ws"], w123]
        xh1, xl1, gt1, of_parity = a1.xh1, a1.xl1, a1.gt1, a1.of_parity
        bank_p, norm2, router = a1.bank_p, a1.norm2, a1.router
        w3_in, w1_low, zeroed = a1.w3_in, a1.w1_low, a1.zeroed
        ctx_in, k_made, v_made, x_done = a1.ctx_in, a1.k_made, a1.v_made, a1.x_done
        h2_made, g_made = a1.h2_made, a1.g_made
        n1 = 2 * (E1 + 1)
        sel = sb("sel", [128, W1C], F32R)
        si, ab, ag = (f0["ws"][:, 2 * i * GT:2 * (i + 1) * GT].rearrange("p (a n) -> p a n", a=2) for i in range(3))
        ah2 = sb("ah", [128, 2, GT], F32R)
        ah = [fr.cs[:, 0, :], fr.cs[:, 1, :], ah2[:, 0, :], ah2[:, 1, :]]
        al = sb("al", [128, 4, GT], F32R)
        od = w123[:, 0:GT]

        bank_1 = [pb("h10"), pb("h11")]
        bank_2 = [pb("h20"), pb("h21")]
        bank_g = pb("g")
        bank_d = pb("d")

        part_high = signal("part_high", 1)
        part_low_v = signal("part_low_v", 1)
        part_low_p = signal("part_low_p", 1)
        sel_in = signal("sel_in", 16)
        h1_made = signal("h1_made", CH)
        si_ready = signal("si_ready", CH)
        ab_ready = signal("ab_ready", CH)
        ag_ready = signal("ag_ready", CH)
        ah_ready = signal("ah_ready", CH)
        al_ready = signal("al_ready", CH)
        d_made = signal("d_made", CH)
        od_ready = signal("od_ready", 1)
        od_turned = signal("od_turned", 1)
        stored = signal("stored", 16)

        def before(c, by):
            return (0, c - by) if c >= by else (1, c - by + CH)

        def weight(which, c):
            return wh[which][:, c * 128:(c + 1) * 128], wlo[which][:, c * 128:(c + 1) * 128]

        def part(tiles, i):
            return tiles[1 + i // 2][:, i % 2 * W1C // 2:(i % 2 + 1) * W1C // 2]

        with nc.Block() as block:

            @block.sync
            def _(sp):
                def load(g):
                    if k_made.comes(g, back=1):
                        sp.wait_ge(k_made.sem, k_made.upto(g, back=1))
                    if v_made.comes(g, back=1):
                        sp.wait_ge(v_made.sem, v_made.upto(g, back=1))
                    sp.dma_start(ctxt[:, :], ctxt_d[:, bass.ds(g * GS, GS)]).then_inc(ctx_in.sem, 16)

                def store(g):
                    sp.wait_ge(x_done.sem, x_done.upto(g))
                    sp.dma_start(out_d[bass.ds(g * NB, NB)].rearrange("b t d -> t b d"),
                                 x[:, bass.ds(g * NB, NB), :]).then_inc(stored.sem, 16)

                load(1)
                with sp.Fori(1, G - 1) as g:
                    load(g + 1)
                    store(g - 1)
                store(G - 2)
                store(G - 1)
                sp.wait_ge(stored.sem, 16 * G)

            @block.gpsimd
            def _(pool):
                _, ahead = a1.gpsimd(nc, pool)

                def low(g, c):
                    pool.wait_ge(ah_ready.sem, ah_ready.upto(g, c + 1))
                    nc.gpsimd.tensor_tensor(al[:, c % 4, :], ag[:, c % 2, :], ah[c % 4].bitcast(F32),
                                            ALU.subtract).then_inc(al_ready.sem, 1)

                def group(g, first, more):
                    for c in range(CH):
                        low(g, c)
                        if first and c in (REST + 6, REST + 7):
                            fr.gpsimd_scale(nc, pool, G - 1, c - REST - 6, fr.dn_last)
                        if more:
                            ahead(g + 1, 2 * c, LPLAN)
                            ahead(g + 1, 2 * c + 1, LPLAN)

                nc.gpsimd.memset(sel[:, :].bitcast(F32), 0.0).then_inc(zeroed.sem, 1)
                pool.wait_ge(zeroed.sem, zeroed.upto(0))
                pool.dma_start(sel[0:n1, :], sel1_d.bitcast(F32R)).then_inc(sel_in.sem, 16)
                pool.wait_ge(part_high.sem, part_high.upto(3))
                nc.gpsimd.tensor_tensor(part(wlo, 3), part(came_to, 3), part(wh, 3).bitcast(F32), ALU.subtract)\
                    .then_inc(part_low_p.sem, 1)
                group(0, True, True)
                pool.wait_ge(fr.x_done.sem, fr.x_done.upto(G - 1))
                with pool.Fori(1, G - 1) as g:
                    group(g, False, True)
                group(G - 1, False, False)

            @block.scalar
            def _(act):
                _, ahead = a1.scalar(nc, act)

                def weights_high(i):
                    if i == 0:
                        act.wait_ge(w123_in, 16)
                    if i == 2:
                        act.wait_ge(w3_in.sem, w3_in.upto(0))
                    nc.scalar.copy(part(wh, i), part(came_to, i)).then_inc(part_high.sem, 1)

                def silu(g, c, first):
                    if first and c == 0:
                        act.wait_ge(part_low_v.sem, part_low_v.upto(1))
                    act.wait_ge(h1_made.sem, h1_made.upto(g, c + 1))
                    back, v = before(c, 2)
                    if not (first and back):
                        if ab_ready.comes(g, v + 1, back=back):
                            act.wait_ge(ab_ready.sem, ab_ready.upto(g, v + 1, back=back))
                    nc.scalar.activation(si[:, c % 2, :], bank_1[c % 2][:, :], ACT.Silu).then_inc(si_ready.sem, 1)

                def high(g, c, first):
                    act.wait_ge(ag_ready.sem, ag_ready.upto(g, c + 1))
                    back, v = before(c, 4)
                    if not (first and back):
                        if d_made.comes(g, v + 1, back=back):
                            act.wait_ge(d_made.sem, d_made.upto(g, v + 1, back=back))
                    nc.scalar.copy(ah[c % 4], ag[:, c % 2, :]).then_inc(ah_ready.sem, 1)

                def output(g):
                    act.wait_ge(d_made.sem, d_made.upto(g))
                    nc.scalar.copy(od[:, :], bank_d[:, :]).then_inc(od_ready.sem, 1)

                def group(g, first, more):
                    for c in range(CH):
                        silu(g, c, first)
                        if more:
                            ahead(g + 1, 2 * c, LPLAN)
                        if c >= 1:
                            high(g, c - 1, first)
                        elif not first:
                            high(g - 1, CH - 1, False)
                        if c == LAG and not first:
                            output(g - 1)
                        if more:
                            ahead(g + 1, 2 * c + 1, LPLAN)

                for i in range(4):
                    weights_high(i)
                group(0, True, True)
                with act.Fori(1, G - 1) as g:
                    group(g, False, True)
                group(G - 1, False, False)
                high(G - 1, CH - 1, False)
                output(G - 1)

            @block.vector
            def _(dve):
                def product(g, c, first):
                    dve.wait_ge(si_ready.sem, si_ready.upto(g, c + 1))
                    dve.wait_ge(h2_made.sem, h2_made.upto(g, c + 1))
                    back, v = before(c, 2)
                    if not (first and back):
                        if ag_ready.comes(g, v + 1, back=back):
                            dve.wait_ge(ag_ready.sem, ag_ready.upto(g, v + 1, back=back))
                    nc.vector.tensor_tensor(ab[:, c % 2, :], bank_2[c % 2][:, :], si[:, c % 2, :], ALU.mult)\
                        .then_inc(ab_ready.sem, 1)

                def gated(g, c, first):
                    if c < GATED:
                        dve.wait_ge(g_made.sem, g_made.upto(g, c + 1))
                    dve.wait_ge(ab_ready.sem, ab_ready.upto(g, c + 1))
                    back, v = before(c, 2)
                    if not (first and back):
                        if al_ready.comes(g, v + 1, back=back):
                            dve.wait_ge(al_ready.sem, al_ready.upto(g, v + 1, back=back))
                    if c < GATED:
                        nc.vector.tensor_tensor(ag[:, c % 2, :], bank_g[:, :], ab[:, c % 2, :], ALU.mult)\
                            .then_inc(ag_ready.sem, 1)
                    else:
                        nc.vector.tensor_copy(ag[:, c % 2, :], ab[:, c % 2, :]).then_inc(ag_ready.sem, 1)

                def add_output(g):
                    dve.wait_ge(od_turned.sem, od_turned.upto(g))
                    xg = x[:, bass.ds(g * NB, NB), :]
                    nc.vector.scalar_tensor_tensor(out=xg, in0=bank_p.rearrange("t (b d) -> t b d", b=NB),
                                                   scalar=tg[:, 3:4], in1=xg, op0=ALU.mult, op1=ALU.add)\
                        .then_inc(x_done.sem, 1)

                _, ahead = a1.vector(nc, dve)

                def weights_low(i):
                    dve.wait_ge(part_high.sem, part_high.upto(i))
                    nc.vector.tensor_tensor(part(wlo, i), part(came_to, i), part(wh, i).bitcast(F32), ALU.subtract)\
                        .then_inc(part_low_v.sem, 1)

                def rest(c):
                    last, k = fr.norm2_last, c - REST
                    if k == 0:
                        last.vector_stats(nc, G - 1)
                        last.vector_moments(nc, dve, G - 1)
                    if 1 <= k <= STEPS // 3:
                        for i in range(3 * k - 3, 3 * k):
                            last.vector_step(nc, dve, G - 1, i)
                    if k == STEPS // 3 + 1:
                        last.vector_rows(nc, dve, G - 1)
                    if k == STEPS // 3 + 6:
                        fr.vector_residual(nc, dve, G - 1, fr.dn_last)

                def group(g, first, more):
                    for c in range(CH):
                        product(g, c, first)
                        if first:
                            rest(c)
                        if more:
                            ahead(g + 1, 2 * c, LPLAN)
                        gated(g, c, first)
                        if c == LAG + 2 and not first:
                            add_output(g - 1)
                        if more:
                            ahead(g + 1, 2 * c + 1, LPLAN)

                for i in range(3):
                    weights_low(i)
                group(0, True, True)
                dve.wait_ge(fr.x_done.sem, fr.x_done.upto(G - 1))
                with dve.Fori(1, G - 1) as g:
                    group(g, False, True)
                group(G - 1, False, False)
                add_output(G - 1)

            @block.tensor
            def _(pe):
                ahead = a1.tensor(nc, pe)

                def up(g, c, first):
                    if c == 0:
                        pe.wait_ge(norm2.low.sem, norm2.low.upto(g))
                    back, v = before(c, 2)
                    for which, bank, made, read in ((0, bank_1, h1_made, si_ready), (1, bank_2, h2_made, ab_ready)):
                        if which == 1 and c == 0:
                            pe.wait_ge(part_low_v.sem, part_low_v.upto(1))
                        if not (first and back):
                            if read.comes(g, v + 1, back=back):
                                pe.wait_ge(read.sem, read.upto(g, v + 1, back=back))
                        split_product(nc, bank[c % 2][:, :], *weight(which, c), of_parity(xh1, g), of_parity(xl1, g),
                                      True, True).then_inc(made.sem, 1)

                def spread_gate(g, c, first):
                    if c == 0:
                        pe.wait_ge(sel_in.sem, sel_in.upto(0))
                        pe.wait_ge(router.ready.sem, router.ready.upto(g))
                    back, v = before(c, 1)
                    if not (first and back):
                        if ag_ready.comes(g, v + 1, back=back):
                            pe.wait_ge(ag_ready.sem, ag_ready.upto(g, v + 1, back=back))
                    nc.tensor.matmul(bank_g[:, :], sel[:, c * 128:(c + 1) * 128], of_parity(gt1, g),
                                     start=True, stop=True).then_inc(g_made.sem, 1)

                def down(g, c):
                    if c == 0:
                        pe.wait_ge(part_low_v.sem, part_low_v.upto(2))
                        pe.wait_ge(part_low_p.sem, part_low_p.upto(0))
                        if od_ready.comes(g, back=1):
                            pe.wait_ge(od_ready.sem, od_ready.upto(g, back=1))
                    pe.wait_ge(ah_ready.sem, ah_ready.upto(g, c + 1))
                    pe.wait_ge(al_ready.sem, al_ready.upto(g, c + 1))
                    split_product(nc, bank_d[:, :], *weight(2, c), ah[c % 4], al[:, c % 4, :], c == 0, c == CH - 1)\
                        .then_inc(d_made.sem, 1)

                def turn_output(g, more):
                    pe.wait_ge(od_ready.sem, od_ready.upto(g))
                    if more:
                        pe.wait_ge(router.logits.sem, router.logits.upto(g + 1))
                    for b in range(NB):
                        last = nc.tensor.transpose(bank_p[:, b * D:(b + 1) * D], od[:, b * T:(b + 1) * T], ident)
                    last.then_inc(od_turned.sem, 1)

                def group(g, first, more):
                    for c in range(CH):
                        up(g, c, first)
                        if more:
                            ahead(g + 1, 2 * c, LPLAN)
                        if c >= LAG:
                            down(g, c - LAG)
                        elif not first:
                            down(g - 1, c - LAG + CH)
                        if c < GATED:
                            spread_gate(g, c, first)
                        if c == LAG + 1 and not first:
                            turn_output(g - 1, True)
                        if more:
                            ahead(g + 1, 2 * c + 1, LPLAN)

                pe.wait_ge(w1_low.sem, w1_low.upto(0))
                group(0, True, True)
                with pe.Fori(1, G - 1) as g:
                    group(g, False, True)
                group(G - 1, False, False)
                for c in range(CH - LAG, CH):
                    down(G - 1, c)
                turn_output(G - 1, False)


def _constants():
    inv_freq = (1.0 / 10000.0 ** (np.arange(0, HD, 2, dtype=np.float32) / HD)).astype(np.float32)
    freqs = np.arange(T, dtype=np.float32)[:, None] * inv_freq[None, :]
    emb = np.concatenate([freqs, freqs], axis=-1)
    cos, sin = np.cos(emb).astype(np.float32), np.sin(emb).astype(np.float32)
    sin[:, :HD // 2] *= -1.0
    cos, sin = np.tile(cos.T, (HEADS, 1)), np.tile(sin.T, (HEADS, 1))
    c = np.zeros((128, NC_COLS), np.float32)

    def put(name, value):
        a, b = CC[name]
        c[:, a:b] = value

    scale = np.float32(HD ** -0.5)
    put("ident", np.eye(128, dtype=np.float32))
    put("cosq", cos * scale)
    put("sinq", sin * scale)
    put("cosk", cos[:, :S])
    put("sink", sin[:, :S])
    put("mask", ((np.arange(128)[:, None] // HD) % NQ == np.arange(NQ)[None, :]).astype(np.float32))
    put("qmask", (np.arange(128)[:, None] // (NQ * HD) == np.arange(QUADS)[None, :]).astype(np.float32))
    put("tri", (np.arange(8)[None, :] < np.arange(8)[:, None]).astype(np.float32).reshape(1, 64))
    n0 = 2 * E0
    sel0 = np.zeros((n0, E0, 128), np.float32)
    for e in range(E0):
        sel0[e, e] = sel0[E0 + e, e] = 1.0
    n1 = E1 + 1
    sel1 = np.zeros((2 * n1, W1C), np.float32)
    for e in range(n1):
        sel1[e, e * H1:(e + 1) * H1] = sel1[n1 + e, e * H1:(e + 1) * H1] = 1.0
    return c, sel0.reshape(n0, E0 * 128), sel1


def _pack(at, total, parts, rows=128):
    out = np.zeros((rows, total), np.float32)
    for name, value in parts.items():
        a, b = at[name]
        value = np.asarray(value)
        out[:value.shape[0], a:b] = value.reshape(value.shape[0], -1)
    return out


def _layout(i):
    swap = np.arange(D).reshape(HEADS, 2, HD // 2)[:, ::-1].reshape(-1)
    wq, wkv = i["L0_xattn_Wq"], i["L0_xattn_Wkv"]
    wk, wv = wkv[:, :D], wkv[:, D:]
    const, sel0, sel1 = _constants()
    rows = lambda v: np.broadcast_to(v.reshape(1, -1), (128, v.size))
    twice = lambda a, axis: np.concatenate([a, a], axis)
    w1 = np.transpose(i["L0_ffn_W1"], (1, 0, 2)).reshape(M0, E0 * EH0)
    w2 = twice(np.transpose(i["L0_ffn_W2"], (1, 0, 2)), 2)
    ws = _pack(WS, NS_COLS, {
        "enc": i["L0_ffn_W_enc"], "w1": twice(w1, 0), "w2": w2, "c2s": twice(i["L0_ffn_W_c2s"], 0),
        "b2": twice(twice(i["L0_ffn_b2"], 1), 0)})
    wf = _pack(WF, NF_COLS, {
        "s2c": twice(i["L0_ffn_W_s2c"].reshape(2, 128, M0).transpose(1, 0, 2), 2), "wr": i["L0_ffn_Wr"],
        "dec": i["L0_ffn_W_dec"].reshape(2, 128, D).transpose(1, 0, 2), "b_enc": i["L0_ffn_b_enc"].reshape(2, 128).T,
        "b_s2c": twice(i["L0_ffn_b_s2c"], 0).reshape(128, 1), "b1": i["L0_ffn_b1"].T,
        "b_c2s": i["L0_ffn_b_c2s"].reshape(2, 128).T, "br": rows(i["L0_ffn_br"]), "b_dec": rows(i["L0_ffn_b_dec"]),
        "ln_g": rows(i["L0_ffn_ln_g"]), "ln_b": rows(i["L0_ffn_ln_b"])})
    wl = _pack(WL, NL_COLS, {
        "q": i["L1_xattn_Wq"].T, "k": i["L1_xattn_Wk"].T, "v": i["L1_xattn_Wv"].T,
        "bq": i["L1_xattn_bq"].reshape(128, 1), "bk": i["L1_xattn_bk"].reshape(128, 1), "bv": rows(i["L1_xattn_bv"]),
        "wg": i["L1_ffn_Wg"].T, "rb": rows(i["L1_ffn_routing_bias"])})
    n = (E1 + 1) * H1
    w123 = np.zeros((128, 3, W1C), np.float32)
    w123[:, 0, :n] = np.concatenate([i["L1_ffn_W1"].reshape(-1, D), i["L1_ffn_Ws1"]]).T
    w123[:, 1, :n] = np.concatenate([i["L1_ffn_W2"].reshape(-1, D), i["L1_ffn_Ws2"]]).T
    w3 = np.zeros((W1C, D), np.float32)
    w3[:n] = np.concatenate([np.transpose(i["L1_ffn_W3"], (0, 2, 1)).reshape(-1, D), i["L1_ffn_Ws3"].T])
    w123[:, 2, :] = w3.reshape(CH, 128, D).transpose(1, 0, 2).reshape(128, W1C)
    return {
        "x": i["x"], "ctxt": i["ctx_1024"].reshape(B * S, D).T, "gates": np.broadcast_to(
            np.concatenate([i["g_xattn"], i["g_ffn"]]).reshape(1, 4), (128, 4)),
        "wa": np.concatenate([wq, wq[:, swap], wk, wk[:, swap], wv, i["L0_xattn_Wo"]], 1),
        "bo": i["L0_xattn_bo"].reshape(1, D), "const": const, "ws": ws, "wf": wf, "wl": wl,
        "sel0": sel0, "sel1": sel1, "w123": w123.reshape(128, 3 * W1C)}


def kernel(**inputs):
    from concourse import bacc
    from concourse.bass_utils import run_bass_kernel_spmd

    laid_out = _layout({name: np.asarray(a) for name, a in inputs.items()})
    nc = bacc.Bacc("TRN2", target_bir_lowering=False, num_devices=1)
    arrays, args = {}, []
    for name, a in laid_out.items():
        arrays[f"in_{name}"] = np.ascontiguousarray(a)
        args.append(nc.dram_tensor(f"in_{name}", a.shape, F32, kind="ExternalInput").ap())
    args.append(nc.dram_tensor("out_x", (B, T, D), F32, kind="ExternalOutput").ap())
    build(nc, *args)
    return run_bass_kernel_spmd(nc, [arrays], core_ids=[0]).results[0]["out_x"]
```
